# Optimizing a Trainium2 kernel written in Bass

```python
import numpy as np
import jax
import jax.numpy as jnp

def _softmax(x, axis=-1):
    return jax.nn.softmax(x, axis=axis)

def _gelu(x):
    return jax.nn.gelu(x, approximate=True)

def _silu(x):
    return jax.nn.silu(x)

def _sigmoid(x):
    return jax.nn.sigmoid(x)

def _layernorm(x, axis=-1, eps=1e-05):
    m = jnp.mean(x, axis=axis, keepdims=True)
    v = jnp.var(x, axis=axis, keepdims=True)
    return (x - m) / jnp.sqrt(v + eps)

def _scatter_add(tgt, idx, src, axis=0):
    return tgt.at[idx].add(src)

def _segment_sum(src, seg, n):
    return jax.ops.segment_sum(src, seg, n)
kernel_name = 'mk_adj_ffn_d2_adj_r2_dc3b48'

def setup_inputs(seed: int=0):
    np.random.seed(seed)
    _w = jnp.asarray

    def _rec_inputs():
        import jax
        import jax.numpy as jnp
        _gk = jax.random.key(seed)
        x = 7.22e-05 + 1 * jax.random.normal(jax.random.fold_in(_gk, 1), (32, 256, 128), jnp.float32)
        _a = jax.random.bernoulli(jax.random.fold_in(_gk, 2), 0.015625, (32, 256, 256))
        _a = jnp.logical_or(_a, jnp.swapaxes(_a, -1, -2))
        _a = jnp.logical_or(_a, jnp.eye(256, dtype=bool))
        _af = _a.astype(jnp.float32)
        _af = _af * jax.random.uniform(jax.random.fold_in(_gk, 3), (32, 256, 256), jnp.float32, 0.05, 1)
        adj = _af
        return (x, adj)
    x, adj = _rec_inputs()

    def _L0_gnn_setup():
        import jax, jax.numpy as jnp
        import numpy as np
        B, K, H = (32, 512, 128)
        LN_EPS = 1e-05

        def layer_norm(x, gamma, beta):
            mu = jnp.mean(x, axis=-1, keepdims=True)
            var = jnp.mean(jnp.square(x - mu), axis=-1, keepdims=True)
            return (x - mu) * jax.lax.rsqrt(var + LN_EPS) * gamma + beta
        key = jax.random.key(seed)
        k1, k2, k3, k4 = jax.random.split(key, 4)
        x = jax.random.normal(k1, (B, K, H), dtype=jnp.float32)
        adj = jax.random.uniform(k2, (B, K, K), dtype=jnp.float32)
        s = 1.0 / np.sqrt(H)
        W_rel = jax.random.normal(k3, (H, H), dtype=jnp.float32) * s
        b_rel = jnp.zeros((H,), dtype=jnp.float32)
        W_root = jax.random.normal(k4, (H, H), dtype=jnp.float32) * s
        ln_gamma = jnp.ones((H,), dtype=jnp.float32)
        ln_beta = jnp.zeros((H,), dtype=jnp.float32)
        return {'x': x, 'adj': adj, 'W_rel': W_rel, 'b_rel': b_rel, 'W_root': W_root, 'ln_gamma': ln_gamma, 'ln_beta': ln_beta}
    _L0_gnn_all = _L0_gnn_setup()
    _L0_gnn_in = {k: v for k, v in _L0_gnn_all.items() if k in ('W_rel', 'b_rel', 'W_root', 'ln_gamma', 'ln_beta')}
    del _L0_gnn_all

    def _L0_ffn_setup():
        import math
        import jax, jax.numpy as jnp
        import numpy as np
        CAPACITY_FACTOR = 1.25
        TOP_K = 2
        LN_EPS = 1e-05

        def _layer_norm(x, gamma, beta):
            mu = jnp.mean(x, axis=-1, keepdims=True)
            var = jnp.var(x, axis=-1, keepdims=True)
            return (x - mu) * jax.lax.rsqrt(var + LN_EPS) * gamma + beta
        key = jax.random.key(seed)
        ks = jax.random.split(key, 4)
        B, S, D, F, E = (8, 2048, 128, 256, 8)
        x = jax.random.normal(ks[0], (B, S, D), dtype=jnp.float32)
        Wr = jax.random.normal(ks[1], (D, E), dtype=jnp.float32) / np.sqrt(D)
        br = jnp.zeros((E,), jnp.float32)
        W1 = jax.random.normal(ks[2], (E, D, F), dtype=jnp.float32) / np.sqrt(D)
        b1 = jnp.zeros((E, F), jnp.float32)
        W2 = jax.random.normal(ks[3], (E, F, D), dtype=jnp.float32) / np.sqrt(F)
        b2 = jnp.zeros((E, D), jnp.float32)
        gamma = jnp.ones((D,), jnp.float32)
        beta = jnp.zeros((D,), jnp.float32)
        return {'x': x, 'Wr': Wr, 'br': br, 'W1': W1, 'b1': b1, 'W2': W2, 'b2': b2, 'gamma': gamma, 'beta': beta}
    _L0_ffn_all = _L0_ffn_setup()
    _L0_ffn_in = {k: v for k, v in _L0_ffn_all.items() if k in ('Wr', 'br', 'W1', 'b1', 'W2', 'b2', 'gamma', 'beta')}
    del _L0_ffn_all

    def _L1_gnn_setup():
        import jax, jax.numpy as jnp
        import numpy as np
        B, N, D = (4, 2048, 128)
        DENSITY = 0.02
        key = jax.random.key(seed)
        kx, ka1, ka2, kwt, kbt, kwh, kth = jax.random.split(key, 7)
        x = jax.random.normal(kx, (B, N, D), dtype=jnp.float32)
        mask = jax.random.uniform(ka1, (B, N, N)) < DENSITY
        vals = jax.random.uniform(ka2, (B, N, N), dtype=jnp.float32)
        adj = jnp.where(mask, vals, 0.0).astype(jnp.float32)
        s = 0.02
        W_t = s * jax.random.normal(kwt, (D, D), dtype=jnp.float32)
        b_t = s * jax.random.normal(kbt, (D,), dtype=jnp.float32)
        W_h = s * jax.random.normal(kwh, (D, D), dtype=jnp.float32)
        theta = s * jax.random.normal(kth, (D, D), dtype=jnp.float32)
        return {'x': x, 'adj': adj, 'W_t': W_t, 'b_t': b_t, 'W_h': W_h, 'theta': theta}
    _L1_gnn_all = _L1_gnn_setup()
    _L1_gnn_in = {k: v for k, v in _L1_gnn_all.items() if k in ('W_t', 'b_t', 'W_h', 'theta')}
    del _L1_gnn_all

    def _L1_ffn_setup():
        import jax, jax.numpy as jnp
        import numpy as np
        N_EXPERTS = 8
        TOP_K = 2
        key = jax.random.key(seed)
        ks = jax.random.split(key, 5)
        B, T, C, E, H = (8, 1024, 128, 8, 341)
        scale = 1.0 / np.sqrt(C)
        return {'x': jax.random.normal(ks[0], (B, T, C), dtype=jnp.float32), 'router_w': jax.random.normal(ks[1], (E, C), dtype=jnp.float32) * scale, 'w1': jax.random.normal(ks[2], (E, H, C), dtype=jnp.float32) * scale, 'w2': jax.random.normal(ks[3], (E, C, H), dtype=jnp.float32) * (1.0 / np.sqrt(H)), 'w3': jax.random.normal(ks[4], (E, H, C), dtype=jnp.float32) * scale}
    _L1_ffn_all = _L1_ffn_setup()
    _L1_ffn_in = {k: v for k, v in _L1_ffn_all.items() if k in ('router_w', 'w1', 'w2', 'w3')}
    del _L1_ffn_all
    return {'x': x, 'adj': adj, 'L0_gnn_W_rel': _L0_gnn_in['W_rel'], 'L0_gnn_b_rel': _L0_gnn_in['b_rel'], 'L0_gnn_W_root': _L0_gnn_in['W_root'], 'L0_gnn_ln_gamma': _L0_gnn_in['ln_gamma'], 'L0_gnn_ln_beta': _L0_gnn_in['ln_beta'], 'L0_ffn_Wr': _L0_ffn_in['Wr'], 'L0_ffn_br': _L0_ffn_in['br'], 'L0_ffn_W1': _L0_ffn_in['W1'], 'L0_ffn_b1': _L0_ffn_in['b1'], 'L0_ffn_W2': _L0_ffn_in['W2'], 'L0_ffn_b2': _L0_ffn_in['b2'], 'L0_ffn_gamma': _L0_ffn_in['gamma'], 'L0_ffn_beta': _L0_ffn_in['beta'], 'L1_gnn_W_t': _L1_gnn_in['W_t'], 'L1_gnn_b_t': _L1_gnn_in['b_t'], 'L1_gnn_W_h': _L1_gnn_in['W_h'], 'L1_gnn_theta': _L1_gnn_in['theta'], 'L1_ffn_router_w': _L1_ffn_in['router_w'], 'L1_ffn_w1': _L1_ffn_in['w1'], 'L1_ffn_w2': _L1_ffn_in['w2'], 'L1_ffn_w3': _L1_ffn_in['w3']}

def reference(x, adj, L0_gnn_W_rel, L0_gnn_b_rel, L0_gnn_W_root, L0_gnn_ln_gamma, L0_gnn_ln_beta, L0_ffn_Wr, L0_ffn_br, L0_ffn_W1, L0_ffn_b1, L0_ffn_W2, L0_ffn_b2, L0_ffn_gamma, L0_ffn_beta, L1_gnn_W_t, L1_gnn_b_t, L1_gnn_W_h, L1_gnn_theta, L1_ffn_router_w, L1_ffn_w1, L1_ffn_w2, L1_ffn_w3):
    import jax
    import jax.numpy as jnp

    def _L0_gnn_ref(x, adj, W_rel, b_rel, W_root, ln_gamma, ln_beta):
        import jax, jax.numpy as jnp
        import numpy as np
        B, K, H = (32, 512, 128)
        LN_EPS = 1e-05

        def layer_norm(x, gamma, beta):
            mu = jnp.mean(x, axis=-1, keepdims=True)
            var = jnp.mean(jnp.square(x - mu), axis=-1, keepdims=True)
            return (x - mu) * jax.lax.rsqrt(var + LN_EPS) * gamma + beta
        h = layer_norm(x, ln_gamma, ln_beta)
        agg = jnp.einsum('bij,bjh->bih', adj, h)
        conv = jnp.einsum('bkh,ho->bko', agg, W_rel) + b_rel + jnp.einsum('bkh,ho->bko', h, W_root)
        return x + jax.nn.relu(conv)

    def _L0_ffn_ref(x, Wr, br, W1, b1, W2, b2, gamma, beta):
        import math
        import jax, jax.numpy as jnp
        import numpy as np
        CAPACITY_FACTOR = 1.25
        TOP_K = 2
        LN_EPS = 1e-05

        def _layer_norm(x, gamma, beta):
            mu = jnp.mean(x, axis=-1, keepdims=True)
            var = jnp.var(x, axis=-1, keepdims=True)
            return (x - mu) * jax.lax.rsqrt(var + LN_EPS) * gamma + beta
        B, S, D = x.shape
        E = Wr.shape[1]
        N = B * S
        K = TOP_K
        logits = jnp.mean(x, axis=1) @ Wr + br
        routing_weights = jax.nn.softmax(logits, axis=-1)
        capacity = float(math.ceil(N * CAPACITY_FACTOR / E))
        expected_loads = routing_weights.sum(axis=0) * (N / B)
        scale = jnp.where(expected_loads > capacity, capacity / expected_loads, 1.0)
        routing_weights = jax.nn.softmax(routing_weights * scale, axis=-1)
        rw_tok = jnp.broadcast_to(routing_weights[:, None, :], (B, S, E)).reshape(N, E)
        top_w, top_i = jax.lax.top_k(rw_tok, K)
        top_w = jax.nn.softmax(top_w, axis=-1)
        xf = x.reshape(N, D)
        h = jax.nn.gelu(jnp.einsum('nd,edf->enf', xf, W1) + b1[:, None, :], approximate=False)
        y = jnp.einsum('enf,efd->end', h, W2) + b2[:, None, :]
        w_dense = jnp.zeros((N, E), x.dtype).at[jnp.arange(N)[:, None], top_i].add(top_w)
        out = jnp.einsum('ne,end->nd', w_dense, y).reshape(B, S, D)
        out = _layer_norm(out + x, gamma, beta)
        return out

    def _L1_gnn_ref(x, adj, W_t, b_t, W_h, theta):
        import jax, jax.numpy as jnp
        import numpy as np
        B, N, D = (4, 2048, 128)
        DENSITY = 0.02
        in_degrees = jnp.sum(adj, axis=-1)
        norm = jnp.power(in_degrees + 1e-06, -0.5)[..., None]
        f_hom = jnp.einsum('bnd,de->bne', x, theta) * norm
        f_hom = jnp.einsum('bnm,bmd->bnd', adj, f_hom) * norm
        f_het = jnp.einsum('bnd,de->bne', x, W_h)
        gate = jax.nn.sigmoid(jnp.einsum('bnd,de->bne', x, W_t) + b_t)
        out = gate * f_hom + (1.0 - gate) * f_het
        return jax.nn.elu(out)

    def _L1_ffn_ref(x, router_w, w1, w2, w3):
        import jax, jax.numpy as jnp
        import numpy as np
        N_EXPERTS = 8
        TOP_K = 2
        B, T, C = x.shape
        flat = x.reshape(-1, C)
        logits = flat @ router_w.T
        probs = jax.nn.softmax(logits, axis=-1)
        topk_probs, topk_idx = jax.lax.top_k(probs, TOP_K)
        topk_probs = topk_probs / (jnp.sum(topk_probs, axis=-1, keepdims=True) + 1e-09)
        onehot = jax.nn.one_hot(topk_idx, N_EXPERTS, dtype=flat.dtype)
        gates = jnp.einsum('nk,nke->ne', topk_probs, onehot)
        h1 = jnp.einsum('nc,ehc->neh', flat, w1)
        h3 = jnp.einsum('nc,ehc->neh', flat, w3)
        h = jax.nn.silu(h1) * h3
        y = jnp.einsum('neh,ech->nec', h, w2)
        out = jnp.einsum('ne,nec->nc', gates, y)
        return out.reshape(B, T, C)
    x = x + _L0_gnn_ref(_layernorm(x, axis=-1), adj, L0_gnn_W_rel, L0_gnn_b_rel, L0_gnn_W_root, L0_gnn_ln_gamma, L0_gnn_ln_beta)
    x = x + _L0_ffn_ref(_layernorm(x, axis=-1), L0_ffn_Wr, L0_ffn_br, L0_ffn_W1, L0_ffn_b1, L0_ffn_W2, L0_ffn_b2, L0_ffn_gamma, L0_ffn_beta)
    x = x + _L1_gnn_ref(_layernorm(x, axis=-1), adj, L1_gnn_W_t, L1_gnn_b_t, L1_gnn_W_h, L1_gnn_theta)
    x = x + _L1_ffn_ref(_layernorm(x, axis=-1), L1_ffn_router_w, L1_ffn_w1, L1_ffn_w2, L1_ffn_w3)
    return x

_drawn_inputs = setup_inputs


def setup_inputs(seed=0):
    import zlib

    import numpy as np

    out = dict(_drawn_inputs(seed))
    spreads = {'L0_gnn_b_rel': (0.0, 0.1),
     'L0_gnn_ln_gamma': (1.0, 0.2),
     'L0_gnn_ln_beta': (0.0, 0.1),
     'L0_ffn_br': (0.0, 0.1),
     'L0_ffn_b1': (0.0, 0.468),
     'L0_ffn_b2': (0.0, 0.365),
     'L0_ffn_gamma': (1.0, 0.2),
     'L0_ffn_beta': (0.0, 0.1)}
    factors = {'L1_gnn_W_t': 8.0, 'L1_gnn_b_t': 64.0, 'L1_gnn_theta': 3.286}
    for name, (base, spread) in spreads.items():
        noise = np.random.default_rng([zlib.crc32(name.encode()), seed]).standard_normal(out[name].shape)
        drawn = base * np.exp(spread * noise) if base else spread * noise
        out[name] = jnp.asarray(drawn.astype(out[name].dtype))
    for name, factor in factors.items():
        out[name] = (out[name] * factor).astype(out[name].dtype)
    return out
```

```python
import concourse.bass as bass
from concourse import mybir
from contextlib import ExitStack

P = 128
UNROLL = 4
PEEL = 12
LN_EPS = 1e-5
DEG_EPS = 1e-6


def pipeline(eng, count, lag, step, peel=PEEL):
    whole = count // UNROLL
    for n in range(peel):
        step(n, n % UNROLL)
    with eng.Fori(peel // UNROLL, whole) as g:
        for u in range(UNROLL):
            step(g * UNROLL + u, u)
    for n in range(whole * UNROLL, count + lag):
        step(n, n % UNROLL)


def live(n, lag, count):
    return not isinstance(n, int) or 0 <= n - lag < count


def reused(eng, done, m, depth, per=1):
    if not isinstance(m, int) or m >= depth:
        eng.wait_ge(done, (m - depth + 1) * per)


def build(nc, x, adj, W_rel, b_rel, W_root, g_gamma, g_beta, Wr, br, W1, b1, W2, b2, f_gamma, f_beta,
          W_t, b_t, W_h, theta, router_w, w1, w2, w3, out):
    F32 = mybir.dt.float32
    ACT = mybir.ActivationFunctionType
    ALU = mybir.AluOpType
    AX = mybir.AxisListType

    B, S, D = x.shape
    T = S // P
    NT = B * T
    E, _, F = W1.shape
    FC = F // P
    K = 2
    H = w1.shape[1]
    HC = -(-H // P)
    HL = H - (HC - 1) * P
    NG = NT * K + E
    ROW = D + 4
    NOWHERE = 1.0e6
    CAPACITY = float(-(-B * S * 5 // (4 * E)))

    ctx = ExitStack()
    with ctx:
        def sb(name, shape, dt=F32):
            return ctx.enter_context(nc.sbuf_tensor(name, shape, dt))

        def pb(name, shape):
            return ctx.enter_context(nc.psum_tensor(name, shape, F32))

        def sem(name):
            return ctx.enter_context(nc.semaphore(name))

        def dram(name, shape, dt=F32):
            return nc.dram_tensor(name, shape, dt, kind="Internal").ap()

        adjT_dram = dram("adjT_dram", (B, P, T * S))

        X = sb("X", [P, NT, D])
        X0T = sb("X0T", [D, B * S])
        tok_sum = sb("tok_sum", [D, B])
        deg = sb("deg", [P, NT])
        mean1 = sb("mean1", [P, NT])
        rstd1 = sb("rstd1", [P, NT])
        ident = sb("ident", [P, P])
        hold = sb("hold", [1, 1])
        half = sb("half", [P, NT])
        NROW = 2 + 16 + 8
        rows = sb("rows", [NROW, D])
        cols = sb("cols", [D, NROW])
        Wg = sb("Wg", [D, 2, D])
        brel = sb("brel", [P, D])

        ones = sb("ones", [P, P])
        one_S = sb("one_S", [P, P])
        Wr_sb = sb("Wr_sb", [D, E])
        br_b = sb("br_b", [P, E])
        b2_sb = sb("b2_sb", [E, D])
        fgam = sb("fgam", [P, D])
        fbet = sb("fbet", [P, D])
        rank_e = sb("rank_e", [P, E])
        wk = sb("wk", [P, B, K])
        eidx = sb("eidx", [P, B, K], mybir.dt.int32)
        b1s = sb("b1s", [P, B, K, FC])
        b2b = sb("b2b", [P, B, D])
        rv = [sb(f"rv{i}", [P, B]) for i in range(8)]
        r8 = [sb(f"r8_{i}", [P, E]) for i in range(3)]
        oh = sb("oh", [P, B, K, E])
        wd8 = sb("wd8", [E, B])
        b2w = sb("b2w", [B, D])
        b2w_dram = dram("b2w_dram", (B, D))
        Wc = sb("Wc", [D, 3, D])
        bt_row = sb("bt_row", [1, D])
        norm = sb("norm", [P, NT])
        w1T = sb("w1T", [D, E, H])
        w3T = sb("w3T", [D, E, H])
        w2T = sb("w2T", [P, E, HC, D])
        mean3 = sb("mean3", [P, NT])
        rstd3 = sb("rstd3", [P, NT])
        tri = sb("tri", [P, P])
        etab = sb("etab", [P, NG])
        etab_i = sb("etab_i", [1, NG], mybir.dt.int32)
        gidx = sb("gidx", [P, NG])
        tok_id = sb("tok_id", [P, NT])
        pad_row = sb("pad_row", [P, ROW])
        slots_dram = dram("slots_dram", (NG * P, ROW))
        y_dram = dram("y_dram", (K * NT * P, D))
        dispatch_i = sb("dispatch_i", [P, 4, K], mybir.dt.int32)
        scatter_i = sb("scatter_i", [P, 4], mybir.dt.int32)
        isk1 = sb("isk1", [P, 4, 1])
        gate = sb("gate", [P, NG])
        dest = sb("dest", [P, NG])
        padd = sb("padd", [P, 2])
        W1b = sb("W1b", [P, 4, K, F])
        W2b = sb("W2b", [P, 4, K, FC, D])
        gT = sb("gT", [P, 2, K, FC, S])
        xb = sb("xb", [P, 4, T, D])
        yb = sb("yb", [P, 4, T, D])
        xbeta = sb("xbeta", [P, 4, T, D])

        AJ = sb("AJ", [P, 4, T, S])
        AT = sb("AT", [P, 4, T, S])
        mv = sb("mv", [P, 4, T, 2])
        st = sb("st", [P, 2, T, 6])
        q = sb("q", [P, 4, 2, T])
        x0 = sb("x0", [P, 2, T, D])
        z = sb("z", [P, 2, T, D])
        xx = sb("xx", [P, 4, T, D])
        hT = sb("hT", [D, 4, S])
        hrel = sb("hrel", [P, 2, T, D + 1])
        cv = sb("cv", [P, 2, T, D])
        mv1 = sb("mv1", [P, 2, T, 2])
        st1 = sb("st1", [P, 2, T, 6])
        q1 = sb("q1", [P, 2, T])
        xp = sb("xp", [P, 2, T, D])

        PS = pb("PS", [P, 8, 512])
        ps = [PS[:, i] for i in range(8)]
        ps_at, ps_cv, ps_z, ps_hr, ps_xp = ps[0:2], ps[2:4], ps[4:6], ps[6], ps[7]

        w_stage = gT[:].rearrange("p a k c s -> p a (k c s)")
        w2_stage = xb[:].rearrange("p (a b) t c -> p a (b t c)", a=2)
        gflat = gT[:].rearrange("p a k c s -> p (a k c s)")
        wflat = W1b[:].rearrange("p a k f -> p (a k f)")
        het = gflat[:, 0:1024].rearrange("p (a t c) -> p a t c", a=4, t=T)
        th = gflat[:, 1024:2048].rearrange("p (a t c) -> p a t c", a=4, t=T)
        dd = wflat[:, 0:512].rearrange("p (a t c) -> p a t c", a=2, t=T)
        oo = wflat[:, 512:1024].rearrange("p (a t c) -> p a t c", a=2, t=T)
        mn = wflat[:, 1024:1536].rearrange("p (a t c) -> p a t c", a=2, t=T)
        ee = wflat[:, 1536:2048].rearrange("p (a t c) -> p a t c", a=2, t=T)
        ajflat = AJ[:].rearrange("p a t s -> p (a t s)")
        rt = [ajflat[:, i * B * E:(i + 1) * B * E].rearrange("p (b e) -> p b e", e=E) for i in range(7)]
        b2flat = b2b[:].rearrange("p b c -> p (b c)")
        lgt = b2flat[:, 0:NT * E].rearrange("p (t e) -> p t e", e=E)
        SR = NT * E
        R = [b2flat[:, SR * (i + 1):SR * (i + 2)].rearrange("p (t e) -> p t e", e=E) for i in range(7)]
        x0flat = X0T[:]
        at = [0]

        def carve(*shape):
            n = 1
            for d in shape:
                n *= d
            v = x0flat[:, at[0]:at[0] + n]
            at[0] += n
            if len(shape) == 1:
                return v
            names = "abcd"[:len(shape)]
            return v.rearrange(f"p ({' '.join(names)}) -> p {' '.join(names)}", **dict(zip(names, shape)))

        XR = carve(4, ROW)
        XS = carve(4, ROW)
        xsT = carve(2, P)
        sg = carve(2, H)
        hh = carve(2, HC * P)
        hhT = carve(2, HC, P)
        YS = carve(4, D)
        pay = carve(NT, 4)
        slot_f = carve(NT, K)
        slot_i = carve(NT, K).bitcast(mybir.dt.int32)
        v_ = [carve(NT) for _ in range(8)]
        etmp = carve(NG, E)
        cnt = [carve(E) for _ in range(6)]
        cnt_i = carve(E).bitcast(mybir.dt.int32)
        ya = AJ[:].rearrange("p a t s -> p a (t s)")
        ybb = AT[:].rearrange("p a t s -> p a (t s)")

        def tokens(t, m):
            return t[:, bass.ds(m * T, T), :]

        s_id = sem("s_id"); s_ones = sem("s_ones"); s_row = sem("s_row"); s_wg = sem("s_wg"); s_colp = sem("s_colp"); s_col = sem("s_col")
        x_in = [sem(f"x_in{i}") for i in range(4)]
        adj_in = [sem(f"adj_in{i}") for i in range(4)]
        at_ps = sem("at_ps"); at_sb = sem("at_sb"); at_out = [sem(f"at_out{i}") for i in range(4)]
        stat = sem("stat"); pow0 = sem("pow0"); q_rdy = sem("q_rdy")
        x0_rdy = sem("x0_rdy"); z_rdy = sem("z_rdy"); xx_rdy = sem("xx_rdy")
        z_ps = sem("z_ps"); hT_rdy = sem("hT_rdy"); hr_ps = sem("hr_ps"); hr_rdy = sem("hr_rdy")
        cv_ps = sem("cv_ps"); cv_bias = sem("cv_bias"); cv_read = sem("cv_read"); x1_rdy = sem("x1_rdy"); stat1 = sem("stat1"); q1_rdy = sem("q1_rdy"); pow1 = sem("pow1")
        xp_rdy = sem("xp_rdy"); xp_ps = sem("xp_ps"); xp_sb = sem("xp_sb")
        s_cst = sem("s_cst"); rlink = sem("rlink"); r_g = sem("r_g"); r_lg = sem("r_lg"); r_sub = sem("r_sub"); r_exp = sem("r_exp")
        r_wd8 = sem("r_wd8"); r_b2 = sem("r_b2"); r_b2w = sem("r_b2w"); r_b2d = sem("r_b2d"); r_b2b = sem("r_b2b"); r_done = sem("r_done"); r_eidx = sem("r_eidx")
        w_in = [sem(f"w_in{i}") for i in range(4)]
        f_h = sem("f_h"); f_g = sem("f_g"); f_y = sem("f_y"); f_xn = sem("f_xn"); f_xb = sem("f_xb"); f_xbeta = sem("f_xbeta")
        f_acc = sem("f_acc"); f_sum = sem("f_sum"); f_st = sem("f_st"); f_q = sem("f_q"); f_pow = sem("f_pow"); f_n = sem("f_n"); f_gm = sem("f_gm"); x2_rdy = sem("x2_rdy")
        s_wc = sem("s_wc"); c_deg = sem("c_deg"); c_norm = sem("c_norm")
        ws_in = [sem(f"ws_in{i}") for i in range(4)]
        wp_ps = sem("wp_ps"); wp_sb = sem("wp_sb")
        at_in = [sem(f"at_in{i}") for i in range(4)]
        c_st = sem("c_st"); c_q = sem("c_q"); c_pow = sem("c_pow"); c_z = sem("c_z"); c_zt = sem("c_zt"); c_xT = sem("c_xT"); c_p = sem("c_p")
        c_f1 = sem("c_f1"); c_pr = sem("c_pr"); c_hom = sem("c_hom"); c_d = sem("c_d"); c_gd = sem("c_gd"); c_o = sem("c_o"); c_mn = sem("c_mn"); c_exp = sem("c_exp")
        c_t2 = sem("c_t2"); x3_rdy = sem("x3_rdy"); c_st3 = sem("c_st3"); c_q3 = sem("c_q3"); c_pow3 = sem("c_pow3"); c_z3 = sem("c_z3"); c_z3t = sem("c_z3t"); c_x3T = sem("c_x3T")
        c_lgp = sem("c_lgp"); c_lg = sem("c_lg")
        qlink = sem("qlink"); q_sub = sem("q_sub"); q_exp = sem("q_exp"); q_M = sem("q_M"); q_rank = sem("q_rank"); q_read = sem("q_read"); q_done = sem("q_done")
        pad_out = sem("pad_out"); p_held = sem("p_held"); d_pad = sem("d_pad")
        d_row = sem("d_row"); d_sc = [sem(f"d_sc{i}") for i in range(4)]
        e_in = [sem(f"e_in{i}") for i in range(4)]
        e_xt = sem("e_xt"); e_xT = sem("e_xT"); e_is = sem("e_is"); e_gate = sem("e_gate"); e_dest = sem("e_dest"); e_h = sem("e_h"); e_silu = sem("e_silu"); e_hh = sem("e_hh")
        e_ht = sem("e_ht"); e_hT = sem("e_hT"); e_y = sem("e_y"); e_ys = sem("e_ys"); e_sc = [sem(f"e_sc{i}") for i in range(4)]
        o_in = [sem(f"o_in{i}") for i in range(4)]; o_a = sem("o_a"); o_b = sem("o_b"); o_out = [sem(f"o_out{i}") for i in range(4)]
        s_out = sem("s_out")

        block = ctx.enter_context(nc.Block())

        L_Z, L_ZT, L_AT, L_HREL, L_CONV, L_X1, L_XP, L_XPT = 1, 2, 3, 3, 4, 5, 6, 7
        LAG1 = L_XPT
        L_Y, L_SUM, L_X2 = 1, 2, 3
        LAG3 = L_X2
        M_Z, M_ZT, M_P, M_HOM, M_O, M_X3, M_Z3, M_Z3T, M_LG = 1, 2, 3, 4, 5, 6, 7, 8, 9
        N_XT, N_H, N_MUL, N_HT, N_Y, N_SC = 1, 2, 3, 4, 5, 6

        @block.sync
        def _(sp):
            sp.dma_start(rows[0:1, :], g_gamma.rearrange("(a c) -> a c", a=1)).then_inc(s_row, 16)
            sp.dma_start(rows[1:2, :], g_beta.rearrange("(a c) -> a c", a=1)).then_inc(s_row, 16)
            sp.dma_start(rows[2:18, :], b1.rearrange("e (f c) -> (e f) c", c=D)).then_inc(s_row, 16)
            sp.dma_start(rows[18:26, :], router_w).then_inc(s_row, 16)

            def load(n, u):
                if live(n, 0, B):
                    reused(sp, q_rdy, n, 4, per=2)
                    sp.dma_start(tokens(X, n), x[bass.ds(n, 1)].rearrange("o (t p) c -> p (o t) c", p=P)).then_inc(x_in[u], 16)
                    reused(sp, at_ps, n, 4)
                    sp.dma_start(AJ[:, u], adj[bass.ds(n, 1)].rearrange("o (t p) j -> p (o t) j", p=P)).then_inc(adj_in[u], 16)
                    if isinstance(n, int) and n == 1:
                        sp.dma_start(Wr_sb[:], Wr).then_inc(s_cst, 16)
                        for i, w in enumerate((theta, W_h, W_t)):
                            sp.dma_start(Wc[:, i], w).then_inc(s_wc, 16)
                        sp.dma_start(bt_row[:], b_t.rearrange("(a c) -> a c", a=1)).then_inc(s_wc, 16)
                        sp.dma_start(br_b[:], br.rearrange("(a c) -> a c", a=1).to_broadcast([P, E])).then_inc(s_cst, 16)
                        sp.dma_start(b2_sb[:], b2).then_inc(s_cst, 16)
                        sp.dma_start(fgam[:], f_gamma.rearrange("(a c) -> a c", a=1).to_broadcast([P, D])).then_inc(s_cst, 16)
                        sp.dma_start(fbet[:], f_beta.rearrange("(a c) -> a c", a=1).to_broadcast([P, D])).then_inc(s_cst, 16)
                    if isinstance(n, int) and n == 0:
                        sp.dma_start(Wg[:, 0], W_rel).then_inc(s_wg, 16)
                        sp.dma_start(Wg[:, 1], W_root).then_inc(s_wg, 16)
                        sp.dma_start(brel[:], b_rel.rearrange("(a c) -> a c", a=1).to_broadcast([P, D])).then_inc(s_wg, 16)
            pipeline(sp, B, 0, load)
            sp.wait_ge(r_b2w, 1)
            sp.dma_start(b2w_dram, b2w[:]).then_inc(r_b2d, 16)
            sp.wait_ge(r_b2d, 16)
            sp.dma_start(b2b[:].rearrange("p b c -> p (b c)"), b2w_dram.rearrange("b c -> (b c)").unsqueeze(0).to_broadcast([P, B * D])).then_inc(r_b2b, 16)
            sp.wait_ge(r_eidx, 1)

            def load_experts(n, u):
                if live(n, 0, B):
                    reused(sp, f_y, n, 4)
                    for k in range(K):
                        e = sp.value_load(eidx[0:1, bass.ds(n, 1), k:k + 1].rearrange("p b k -> p (b k)"), min_val=0, max_val=E - 1)
                        sp.dma_start(W1b[:, u, k], W1[bass.ds(e, 1)].rearrange("o d f -> d (o f)")).then_inc(w_in[u], 16)
                        sp.dma_start(W2b[:, u, k], W2[bass.ds(e, 1)].rearrange("o (c p) d -> p (o c) d", p=P)).then_inc(w_in[u], 16)
            pipeline(sp, B, 0, load_experts)
            for u in range(4):
                sp.wait_ge(at_out[u], 16 * (B // 4))

            def load_adjT(n, u):
                reused(sp, c_hom, n, 4)
                sp.dma_start(AT[:, u].rearrange("p t i -> p (t i)"), adjT_dram[bass.ds(n, 1)].rearrange("o p f -> p (o f)")).then_inc(at_in[u], 16)
            pipeline(sp, B, 0, load_adjT, peel=4)

            def load_raw(n, u):
                reused(sp, wp_ps, n, 2)
                if isinstance(n, int) and n < 2:
                    sp.wait_ge(x3_rdy, B)
                one = bass.ds(n, 1)
                for i, w in enumerate((w1, w3)):
                    dst = w_stage[:, u % 2, i * HC * P:(i + 1) * HC * P].rearrange("p (c d) -> p c d", c=HC)
                    sp.dma_start(dst[:, 0:HC - 1], w[one, 0:(HC - 1) * P].rearrange("o (c p) d -> p (o c) d", p=P)).then_inc(ws_in[u], 16)
                    sp.dma_start(dst[0:HL, HC - 1], w[one, (HC - 1) * P:H].rearrange("o p d -> (o p) d")).then_inc(ws_in[u], 16)
                sp.dma_start(w2_stage[:, u % 2, 0:H], w2[one].rearrange("o d h -> (o d) h")).then_inc(ws_in[u], 16)
            pipeline(sp, E, 0, load_raw, peel=4)
            for u in range(4):
                sp.wait_ge(d_sc[u], 16 * K * (NT // 4))

            def load_slots(n, u):
                reused(sp, e_gate, n, 4, per=2)
                reused(sp, e_xt, n, 4)
                sp.dma_start(XS[:, u], slots_dram[bass.ds(n * P, P)]).then_inc(e_in[u], 16)
            pipeline(sp, NG, 0, load_slots, peel=4)

            for u in range(4):
                sp.wait_ge(e_sc[u], 16 * (NG // 4))

            def load_y(n, u):
                if live(n, 0, NT // 4):
                    if not isinstance(n, int) or n >= 4:
                        sp.wait_ge(o_out[u], (n - u) * 4)
                    sp.dma_start(ya[:, u].rearrange("p (t c) -> p t c", c=D), y_dram[bass.ds(n * 4 * P, 4 * P)].rearrange("(t p) c -> p t c", p=P)).then_inc(o_in[u], 16)
                    sp.dma_start(ybb[:, u].rearrange("p (t c) -> p t c", c=D), y_dram[bass.ds(n * 4 * P + NT * P, 4 * P)].rearrange("(t p) c -> p t c", p=P)).then_inc(o_in[u], 16)
            pipeline(sp, NT // 4, 0, load_y, peel=4)

        @block.gpsimd
        def _(gp):
            gp.memset(ident[:], 0.0).then_inc(s_ones, 1)
            gp.memset(half[:], -0.5).then_inc(s_ones, 1)
            gp.memset(hrel[:, :, :, D:D + 1], 1.0).then_inc(s_ones, 1)
            gp.memset(ones[:], 1.0).then_inc(s_ones, 1)
            gp.memset(one_S[:], 1.0 / S).then_inc(s_ones, 1)
            gp.iota(rank_e[:], pattern=[[-1, E]], base=E, channel_multiplier=0, allow_small_or_imprecise_dtypes=True).then_inc(s_ones, 1)
            gp.wait_ge(s_ones, 6)
            gp.memset(pad_row[:], 0.0).then_inc(pad_out, 1)
            gp.wait_ge(pad_out, 1)
            gp.memset(pad_row[:, D + 2:D + 3], -1.0).then_inc(pad_out, 1)
            gp.memset(pad_row[:, D + 3:D + 4], NOWHERE).then_inc(pad_out, 1)
            gp.memset(padd[:], 0.0).then_inc(pad_out, 1)
            gp.iota(gidx[:], pattern=[[1, NG]], base=0, channel_multiplier=0, allow_small_or_imprecise_dtypes=True).then_inc(pad_out, 1)
            gp.iota(tok_id[:], pattern=[[P, NT]], base=0, channel_multiplier=1, allow_small_or_imprecise_dtypes=True).then_inc(pad_out, 1)
            gp.affine_select(out=tri[:], in_=ones[:], compare_op=ALU.is_gt, fill=0.0, base=0,
                             pattern=[[1, P]], channel_multiplier=-1).then_inc(pad_out, 1)
            gp.affine_select(out=ident[:], in_=ident[:], compare_op=ALU.not_equal, fill=1.0, base=0,
                             pattern=[[-1, P]], channel_multiplier=1).then_inc(s_id, 1)

            def step(n, u):
                if live(n, 0, B):
                    gp.wait_ge(q_rdy, (n + 1) * 2)
                    gp.tensor_tensor(q[:, u], q[:, u], half[:, 0:4].rearrange("p (a t) -> p a t", a=2), ALU.pow).then_inc(pow0, 1)
                m = n - L_Z
                if live(n, L_Z, B):
                    gp.wait_ge(x0_rdy, m + 1)
                    reused(gp, x1_rdy, m, 4)
                    gp.tensor_tensor(xx[:, (u - 1) % 4], tokens(X, m), x0[:, (u - 1) % 2], ALU.add).then_inc(xx_rdy, 1)
                m = n - L_X1
                if live(n, L_X1, B):
                    gp.wait_ge(q1_rdy, m + 1)
                    gp.tensor_tensor(rstd1[:, bass.ds(m * T, T)], q1[:, (u - L_X1) % 2], half[:, 0:T], ALU.pow).then_inc(pow1, 1)
            pipeline(gp, B, LAG1, step)
            gp.wait_ge(c_deg, 1)
            gp.tensor_tensor(norm[:], norm[:], half[:], ALU.pow).then_inc(c_norm, 1)
            gp.wait_ge(s_cst, 80)
            gp.wait_ge(r_b2b, 16)

            def ffn0(n, u):
                if live(n, 0, B):
                    gp.wait_ge(f_xn, n + 1)
                    gp.tensor_tensor(xb[:, u], xb[:, u], b2b[:, bass.ds(n, 1), :].to_broadcast([P, T, D]), ALU.add).then_inc(f_xb, 1)
                    reused(gp, x2_rdy, n, 4)
                    gp.tensor_tensor(xbeta[:, u], tokens(X, n), fbet[:].unsqueeze(1).to_broadcast([P, T, D]), ALU.add).then_inc(f_xbeta, 1)
                m = n - L_SUM
                if live(n, L_SUM, B):
                    gp.wait_ge(f_q, m + 1)
                    gp.tensor_tensor(q[:, (u - L_SUM) % 4, 0], q[:, (u - L_SUM) % 4, 0], half[:, 0:T], ALU.pow).then_inc(f_pow, 1)
            pipeline(gp, B, LAG3, ffn0)

            def gnn1(n, u):
                if live(n, 0, B):
                    gp.wait_ge(c_q, n + 1)
                    gp.tensor_tensor(q[:, u, 0], q[:, u, 0], half[:, 0:T], ALU.pow).then_inc(c_pow, 1)
                m = n - M_X3
                if live(n, M_X3, B):
                    gp.wait_ge(c_q3, m + 1)
                    gp.tensor_tensor(rstd3[:, bass.ds(m * T, T)], q1[:, (u - M_X3) % 2], half[:, 0:T], ALU.pow).then_inc(c_pow3, 1)
            pipeline(gp, B, M_LG, gnn1, peel=16)

            def held(done, value, before):
                if not isinstance(before, int) or before > 0:
                    gp.wait_ge(p_held, before)
                gp.wait_ge(done, value)
                gp.tensor_tensor(padd[:, 0:1], padd[:, 1:2], padd[:, 1:2], ALU.add).then_inc(p_held, 1)

            gp.wait_ge(d_pad, 16)

            def dispatch(n, u):
                held(d_row, n + 1, n)
                for k in range(K):
                    gp.indirect_dma_start(slots_dram, bass.IndirectOffsetOnAxis(ap=dispatch_i[:, u, k:k + 1].bitcast(mybir.dt.uint32), axis=0),
                                          XR[:, u], None).then_inc(d_sc[u], 16)
            pipeline(gp, NT, 0, dispatch, peel=4)

            def give(n, u):
                m = n - N_SC
                if live(n, N_SC, NG):
                    v = (u - N_SC) % 4
                    gp.wait_ge(e_dest, m + 1)
                    held(e_ys, m + 1, NT + m)
                    gp.indirect_dma_start(y_dram, bass.IndirectOffsetOnAxis(ap=scatter_i[:, v:v + 1].bitcast(mybir.dt.uint32), axis=0),
                                          YS[:, v], None, bounds_check=K * NT * P - 1, oob_is_err=False).then_inc(e_sc[v], 16)
            pipeline(gp, NG, N_SC, give)

        @block.scalar
        def _(act):
            act.wait_ge(s_colp, 1)
            act.activation(cols[:], ps_z[0][:, 0:NROW], ACT.Copy).then_inc(s_col, 1)
            act.wait_ge(s_col, 1)

            def step(n, u):
                m = n - L_XPT
                if live(n, L_XPT, B):
                    act.wait_ge(xp_ps, m + 1)
                    act.activation(X0T[:, bass.ds(m * S, S)], ps_xp[:, 0:S], ACT.Identity, accum_out=tok_sum[:, bass.ds(m, 1)]).then_inc(xp_sb, 1)
                m = n - L_ZT
                if live(n, L_ZT, B):
                    v = (u - L_ZT) % 4
                    act.wait_ge(z_ps, m + 1)
                    reused(act, cv_ps, m, 4)
                    act.activation(hT[:, v], ps_z[v % 2][:, 0:S], ACT.Identity, scale=cols[:, 0:1], bias=cols[:, 1:2]).then_inc(hT_rdy, 1)
                m = n - L_AT
                if live(n, L_AT, B):
                    v = (u - L_AT) % 4
                    act.wait_ge(at_ps, m + 1)
                    reused(act, cv_ps, m, 4)
                    if not isinstance(m, int) or m >= 4:
                        act.wait_ge(at_out[v], (m - v) * 4)
                    act.activation(AT[:, v], ps_at[v % 2][:].rearrange("p (t i) -> p t i", t=T), ACT.Copy).then_inc(at_sb, 1)
                m = n - L_HREL
                if live(n, L_HREL, B):
                    v = (u - L_HREL) % 4
                    act.wait_ge(hr_ps, m + 1)
                    reused(act, cv_ps, m, 2)
                    act.activation(hrel[:, v % 2, :, 0:D], ps_hr[:, 0:S].rearrange("p (t c) -> p t c", t=T), ACT.Copy).then_inc(hr_rdy, 1)
                m = n - L_AT
                if live(n, L_AT, B):
                    v = (u - L_AT) % 4
                    act.wait_ge(at_sb, m + 1)
                    act.dma_start(adjT_dram[bass.ds(m, 1)].rearrange("o p f -> p (o f)"), AT[:, v].rearrange("p t i -> p (t i)")).then_inc(at_out[v], 16)
            pipeline(act, B, LAG1, step)
            act.wait_ge(pad_out, 4)
            act.dma_start(slots_dram.rearrange("(g p) c -> p g c", p=P), pad_row[:].unsqueeze(1).to_broadcast([P, NG, ROW])).then_inc(d_pad, 16)

            act.wait_ge(r_sub, 1)
            act.activation(rt[2], rt[1], ACT.Exp).then_inc(r_exp, 1)
            act.wait_ge(r_sub, 2)
            act.activation(rt[2], rt[1], ACT.Exp).then_inc(r_exp, 1)
            act.wait_ge(r_sub, 3)
            act.activation(rv[5][:], rv[4][:], ACT.Exp).then_inc(r_exp, 1)
            act.wait_ge(r_b2, 1)
            act.activation(b2w[:], ps[1][0:B, 0:D], ACT.Copy).then_inc(r_b2w, 1)
            act.wait_ge(r_done, 1)

            def ffn0(n, u):
                if live(n, 0, B):
                    reused(act, f_y, n, 2)
                    for k in range(K):
                        act.wait_ge(f_h, n * K + k + 1)
                        for c in range(FC):
                            act.activation(gT[:, u % 2, k, c], ps[(u % 2) * K + k][:, c * S:(c + 1) * S], ACT.Gelu,
                                           bias=b1s[:, bass.ds(n, 1), k, c:c + 1].rearrange("p b c -> p (b c)")).then_inc(f_g, 1)
            pipeline(act, B, LAG3, ffn0)

            act.wait_ge(f_y, B)
            act.wait_ge(c_norm, 1)

            def gnn1(n, u):
                m = n - M_Z3T
                if live(n, M_Z3T, B):
                    act.wait_ge(c_z3t, m + 1)
                    reused(act, c_lgp, m, 2)
                    act.activation(xp[:, (u - M_Z3T) % 2].rearrange("p t c -> p (t c)"), ps[1][:, 0:S], ACT.Copy).then_inc(c_x3T, 1)
                m = n - M_ZT
                if live(n, M_ZT, B):
                    act.wait_ge(c_zt, m + 1)
                    reused(act, c_p, m, 2)
                    act.activation(hT[:, (u - M_ZT) % 2], ps[0][:, 0:S], ACT.Copy).then_inc(c_xT, 1)
                m = n - M_P
                if live(n, M_P, B):
                    v = (u - M_P) % 4
                    pp = PS[:, 2 + 2 * (v % 2):4 + 2 * (v % 2)]
                    act.wait_ge(c_p, m + 1)
                    reused(act, c_hom, m, 2)
                    reused(act, c_o, m, 4)
                    for t in range(T):
                        last = act.activation(hrel[:, v % 2, t, 0:D], pp[:, t, 0:D], ACT.Copy, scale=norm[:, bass.ds(m * T + t, 1)])
                    last.then_inc(c_f1, 1)
                    act.activation(het[:, v], pp[:, :, D:2 * D], ACT.Copy)
                    act.activation(th[:, v], pp[:, :, 2 * D:3 * D], ACT.Tanh, scale=0.5).then_inc(c_pr, 1)
                m = n - M_O
                if live(n, M_O, B):
                    act.wait_ge(c_mn, m + 1)
                    reused(act, x3_rdy, m, 2)
                    act.activation(ee[:, (u - M_O) % 2], mn[:, (u - M_O) % 2], ACT.Exp).then_inc(c_exp, 1)
            pipeline(act, B, M_LG, gnn1, peel=16)

            act.wait_ge(q_sub, 1)
            act.activation(R[1], R[0], ACT.Exp).then_inc(q_exp, 1)

            def turned(n, u):
                act.wait_ge(wp_ps, n + 1)
                e = bass.ds(n, 1)
                act.activation(w1T[:, e], ps[3][:, 0:H].unsqueeze(1), ACT.Copy)
                act.activation(w3T[:, e], ps[4][:, 0:H].unsqueeze(1), ACT.Copy)
                act.activation(w2T[:, e, 0:HC - 1].rearrange("p o c d -> p (o c) d"), ps[5][:, 0:(HC - 1) * D].rearrange("p (c d) -> p c d", d=D), ACT.Copy)
                act.activation(w2T[0:HL, e, HC - 1], ps[5][0:HL, (HC - 1) * D:HC * D].unsqueeze(1), ACT.Copy).then_inc(wp_sb, 1)
            pipeline(act, E, 0, turned, peel=4)

            def ffn1(n, u):
                m = n - N_Y
                if live(n, N_Y, NG):
                    v = (u - N_Y) % 4
                    act.wait_ge(e_y, m + 1)
                    act.wait_ge(e_gate, (m + 1) * 2)
                    if not isinstance(m, int) or m >= 4:
                        act.wait_ge(e_sc[v], (m - v) * 4)
                    act.activation(YS[:, v], ps[6 + v % 2][:, 0:D], ACT.Copy, scale=gate[:, bass.ds(m, 1)]).then_inc(e_ys, 1)
                m = n - N_HT
                if live(n, N_HT, NG):
                    v = (u - N_HT) % 4
                    act.wait_ge(e_ht, m + 1)
                    reused(act, e_y, m, 2)
                    act.activation(hhT[:, v % 2].rearrange("p c s -> p (c s)"), ps[5][:, 0:HC * P], ACT.Copy).then_inc(e_hT, 1)
                m = n - N_H
                if live(n, N_H, NG):
                    v = (u - N_H) % 4
                    act.wait_ge(e_h, m + 1)
                    reused(act, e_hh, m, 2)
                    act.activation(sg[:, v % 2], ps[1 + v % 2][:, 0:H], ACT.Silu).then_inc(e_silu, 1)
            pipeline(act, NG, N_SC, ffn1)

            def store(n, u):
                act.wait_ge(o_b, n + 1)
                act.dma_start(out[bass.ds(n * 2, 2)].rearrange("b (t p) c -> p (b t) c", p=P), ya[:, u].rearrange("p (t c) -> p t c", c=D)).then_inc(o_out[u], 16)
            pipeline(act, NT // 4, 0, store, peel=4)
            for u in range(4):
                act.wait_ge(o_out[u], 16 * (NT // 16))

        @block.vector
        def _(dve):
            def held(done, value):
                dve.wait_ge(done, value)
                dve.memset(hold[:], 0.0)

            dve.wait_ge(s_ones, 6)
            dve.wait_ge(s_wg, 48)

            def step(n, u):
                if live(n, 0, B):
                    held(x_in[u], (n - u) * 4 + 16)
                    for t in range(T):
                        dve.bn_stats(st[:, u % 2, t], X[:, bass.ds(n * T + t, 1), :].rearrange("p o c -> p (o c)")).then_inc(stat, 1)
                    held(stat, n * 2 * T + T)
                    for t in range(T):
                        dve.bn_aggr(mv[:, u, t], st[:, u % 2, t]).then_inc(stat, 1)
                    dve.wait_ge(stat, (n + 1) * 2 * T)
                    var = mv[:, u, :, 1:2].rearrange("p t o -> p (t o)")
                    dve.tensor_scalar(q[:, u, 0], var, LN_EPS, None, ALU.add).then_inc(q_rdy, 1)
                    dve.tensor_scalar(q[:, u, 1], var, 1.0 + LN_EPS, LN_EPS * LN_EPS, ALU.mult, ALU.add).then_inc(q_rdy, 1)
                m = n - L_Z
                if live(n, L_Z, B):
                    v = (u - 1) % 4
                    dve.wait_ge(pow0, m + 1)
                    reused(dve, xx_rdy, m, 2)
                    reused(dve, z_ps, m, 2)
                    for t in range(T):
                        xt = X[:, bass.ds(m * T + t, 1), :].rearrange("p o c -> p (o c)")
                        last0 = dve.tensor_scalar(x0[:, v % 2, t], xt, mv[:, v, t, 0:1], q[:, v, 0, t:t + 1], ALU.subtract, ALU.mult)
                        lastz = dve.tensor_scalar(z[:, v % 2, t], xt, mv[:, v, t, 0:1], q[:, v, 1, t:t + 1], ALU.subtract, ALU.mult)
                    last0.then_inc(x0_rdy, 1)
                    lastz.then_inc(z_rdy, 1)
                m = n - L_X1
                if live(n, L_X1, B):
                    v = (u - L_X1) % 4
                    dve.wait_ge(cv_ps, m + 1)
                    pc = ps_cv[v % 2][:].rearrange("p (t c) -> p t c", t=T)
                    dve.tensor_tensor(cv[:, v % 2], pc[:, :, 0:D], brel[:].unsqueeze(1).to_broadcast([P, T, D]), ALU.add).then_inc(cv_bias, 1)
                    dve.wait_ge(cv_bias, m + 1)
                    dve.wait_ge(xx_rdy, m + 1)
                    dve.scalar_tensor_tensor(tokens(X, m), cv[:, v % 2], 0.0, xx[:, v], ALU.max, ALU.add).then_inc(x1_rdy, 1)
                    dve.wait_ge(x1_rdy, m + 1)
                    dve.tensor_scalar(deg[:, bass.ds(m * T, T)], pc[:, :, D:D + 1].rearrange("p t o -> p (t o)"), 1.0, None, ALU.mult).then_inc(cv_read, 1)
                    for t in range(T):
                        dve.bn_stats(st1[:, v % 2, t], X[:, bass.ds(m * T + t, 1), :].rearrange("p o c -> p (o c)")).then_inc(stat1, 1)
                    held(stat1, m * 2 * T + T)
                    for t in range(T):
                        dve.bn_aggr(mv1[:, v % 2, t], st1[:, v % 2, t]).then_inc(stat1, 1)
                    dve.wait_ge(stat1, (m + 1) * 2 * T)
                    dve.tensor_copy(mean1[:, bass.ds(m * T, T)], mv1[:, v % 2, :, 0:1].rearrange("p t o -> p (t o)"))
                    dve.tensor_scalar(q1[:, v % 2], mv1[:, v % 2, :, 1:2].rearrange("p t o -> p (t o)"), LN_EPS, None, ALU.add).then_inc(q1_rdy, 1)
                m = n - L_XP
                if live(n, L_XP, B):
                    v = (u - L_XP) % 4
                    dve.wait_ge(pow1, m + 1)
                    reused(dve, xp_ps, m, 2)
                    for t in range(T):
                        last = dve.tensor_scalar(xp[:, v % 2, t], X[:, bass.ds(m * T + t, 1), :].rearrange("p o c -> p (o c)"),
                                                 mv1[:, v % 2, t, 0:1], rstd1[:, bass.ds(m * T + t, 1)], ALU.subtract, ALU.mult)
                    last.then_inc(xp_rdy, 1)
            pipeline(dve, B, LAG1, step)

            dve.wait_ge(cv_read, B)
            dve.tensor_scalar(norm[:], deg[:], DEG_EPS, None, ALU.add).then_inc(c_deg, 1)

            links = [0]

            def link(ins):
                links[0] += 1
                ins.then_inc(rlink, 1)
                dve.wait_ge(rlink, links[0])

            def over_e(v):
                return v.unsqueeze(2).to_broadcast([P, B, E])

            def over_b(v):
                return v.unsqueeze(1).to_broadcast([P, B, E])

            dve.wait_ge(s_cst, 80)
            dve.wait_ge(xp_sb, B)
            dve.tensor_tensor(rt[0], over_e(tok_sum[:]), over_b(Wr_sb[:]), ALU.mult).then_inc(r_g, 1)
            dve.wait_ge(r_lg, 1)
            lg = ps[0][:, 0:B * E].rearrange("p (b e) -> p b e", e=E)
            link(dve.tensor_tensor(rt[0], lg, over_b(br_b[:]), ALU.add))

            def softmax(src, dst, nth):
                link(dve.tensor_reduce(rv[0][:], src, AX.X, ALU.max))
                dve.tensor_tensor(rt[1], src, over_e(rv[0][:]), ALU.subtract).then_inc(r_sub, 1)
                dve.wait_ge(r_exp, nth)
                link(dve.tensor_reduce(rv[0][:], rt[2], AX.X, ALU.add))
                link(dve.reciprocal(rv[1][:], rv[0][:]))
                link(dve.tensor_tensor(dst, rt[2], over_e(rv[1][:]), ALU.mult))

            softmax(rt[0], rt[3], 1)
            link(dve.tensor_reduce(r8[0][:], rt[3].rearrange("p b e -> p e b"), AX.X, ALU.add))
            link(dve.tensor_scalar(r8[1][:], r8[0][:], float(S), None, ALU.mult))
            link(dve.reciprocal(r8[0][:], r8[1][:]))
            link(dve.tensor_scalar(r8[2][:], r8[0][:], CAPACITY, 1.0, ALU.mult, ALU.min))
            link(dve.tensor_tensor(rt[0], rt[3], over_b(r8[2][:]), ALU.mult))
            softmax(rt[0], rt[3], 2)

            def first_max(w, top, key, hot):
                link(dve.tensor_reduce(top, w, AX.X, ALU.max))
                link(dve.tensor_tensor(key, w, over_e(top), ALU.is_equal))
                link(dve.tensor_tensor(key, key, over_b(rank_e[:]), ALU.mult))
                link(dve.tensor_reduce(rv[7][:], key, AX.X, ALU.max))
                link(dve.tensor_tensor(hot, key, over_e(rv[7][:]), ALU.is_equal))

            for k in range(K):
                first_max(rt[3], rv[2 + k][:], rt[4], oh[:, :, k])
                link(dve.tensor_scalar(rv[6][:], rv[7][:], -1.0, float(E), ALU.mult, ALU.add))
                link(dve.tensor_copy(eidx[:, :, k:k + 1].rearrange("p b k -> p (b k)"), rv[6][:]))
                if k == 0:
                    link(dve.scalar_tensor_tensor(rt[3], oh[:, :, k], -2.0, rt[3], ALU.mult, ALU.add))
            dve.tensor_tensor(rv[4][:], rv[3][:], rv[2][:], ALU.subtract).then_inc(r_sub, 1)
            dve.sem_inc(r_eidx, 1)
            dve.wait_ge(r_exp, 3)
            link(dve.tensor_scalar(rv[6][:], rv[5][:], 1.0, None, ALU.add))
            link(dve.reciprocal(rv[7][:], rv[6][:]))
            w_of = [wk[:, :, k:k + 1].rearrange("p b k -> p (b k)") for k in range(K)]
            link(dve.tensor_copy(w_of[0], rv[7][:]))
            link(dve.tensor_tensor(w_of[1], rv[5][:], rv[7][:], ALU.mult))
            link(dve.tensor_tensor(rt[4], oh[:, :, 0], over_e(w_of[0]), ALU.mult))
            link(dve.tensor_tensor(rt[5], oh[:, :, 1], over_e(w_of[1]), ALU.mult))
            link(dve.tensor_tensor(rt[4], rt[4], rt[5], ALU.add))
            link(dve.tensor_tensor(rt[5][0:E], rt[4][0:E], ident[0:E, 0:E].unsqueeze(1).to_broadcast([E, B, E]), ALU.mult))
            dve.tensor_reduce(wd8[:], rt[5][0:E], AX.X, ALU.add).then_inc(r_wd8, 1)
            b1c = cols[:, 2:18].rearrange("p (e c) -> p c e", c=FC)
            for k in range(K):
                for c in range(FC):
                    link(dve.tensor_tensor(rt[6], oh[:, :, k], over_b(b1c[:, c]), ALU.mult))
                    link(dve.tensor_reduce(b1s[:, :, k, c:c + 1].rearrange("p b c -> p (b c)"), rt[6], AX.X, ALU.add))
            dve.memset(hold[:], 0.0).then_inc(r_done, 1)

            def ffn0(n, u):
                if live(n, 0, B):
                    reused(dve, f_sum, n, 4)
                    for t in range(T):
                        last = dve.tensor_scalar(xb[:, u, t], X[:, bass.ds(n * T + t, 1), :].rearrange("p o c -> p (o c)"),
                                                 mean1[:, bass.ds(n * T + t, 1)], rstd1[:, bass.ds(n * T + t, 1)], ALU.subtract, ALU.mult)
                    last.then_inc(f_xn, 1)
                m = n - L_SUM
                if live(n, L_SUM, B):
                    v = (u - L_SUM) % 4
                    dve.wait_ge(f_xb, m + 1)
                    dve.wait_ge(f_y, m + 1)
                    py = ps[4 + v % 2][:].rearrange("p (k t c) -> p k t c", k=K, t=T)
                    dve.scalar_tensor_tensor(yb[:, v], py[:, 0], wk[:, bass.ds(m, 1), 0:1].rearrange("p b k -> p (b k)"), xb[:, v], ALU.mult, ALU.add).then_inc(f_acc, 1)
                    dve.wait_ge(f_acc, m + 1)
                    dve.scalar_tensor_tensor(yb[:, v], py[:, 1], wk[:, bass.ds(m, 1), 1:2].rearrange("p b k -> p (b k)"), yb[:, v], ALU.mult, ALU.add).then_inc(f_sum, 1)
                    held(f_sum, m + 1)
                    for t in range(T):
                        dve.bn_stats(st[:, v % 2, t], yb[:, v, t]).then_inc(f_st, 1)
                    held(f_st, m * 2 * T + T)
                    for t in range(T):
                        dve.bn_aggr(mv[:, v, t], st[:, v % 2, t]).then_inc(f_st, 1)
                    dve.wait_ge(f_st, (m + 1) * 2 * T)
                    dve.tensor_scalar(q[:, v, 0], mv[:, v, :, 1:2].rearrange("p t o -> p (t o)"), LN_EPS, None, ALU.add).then_inc(f_q, 1)
                m = n - L_X2
                if live(n, L_X2, B):
                    v = (u - L_X2) % 4
                    dve.wait_ge(f_pow, m + 1)
                    for t in range(T):
                        last = dve.tensor_scalar(yb[:, v, t], yb[:, v, t], mv[:, v, t, 0:1], q[:, v, 0, t:t + 1], ALU.subtract, ALU.mult)
                    last.then_inc(f_n, 1)
                    dve.wait_ge(f_n, m + 1)
                    dve.tensor_tensor(yb[:, v], yb[:, v], fgam[:].unsqueeze(1).to_broadcast([P, T, D]), ALU.mult).then_inc(f_gm, 1)
                    dve.wait_ge(f_gm, m + 1)
                    dve.wait_ge(f_xbeta, m + 1)
                    dve.tensor_tensor(tokens(X, m), yb[:, v], xbeta[:, v], ALU.add).then_inc(x2_rdy, 1)
            pipeline(dve, B, LAG3, ffn0)

            dve.wait_ge(f_y, B)
            dve.wait_ge(f_xb, B)

            def gnn1(n, u):
                if live(n, 0, B):
                    for t in range(T):
                        dve.bn_stats(st[:, u % 2, t], X[:, bass.ds(n * T + t, 1), :].rearrange("p o c -> p (o c)")).then_inc(c_st, 1)
                    held(c_st, n * 2 * T + T)
                    for t in range(T):
                        dve.bn_aggr(mv[:, u, t], st[:, u % 2, t]).then_inc(c_st, 1)
                    dve.wait_ge(c_st, (n + 1) * 2 * T)
                    dve.tensor_scalar(q[:, u, 0], mv[:, u, :, 1:2].rearrange("p t o -> p (t o)"), LN_EPS, None, ALU.add).then_inc(c_q, 1)
                m = n - M_Z
                if live(n, M_Z, B):
                    v = (u - M_Z) % 4
                    dve.wait_ge(c_pow, m + 1)
                    reused(dve, c_zt, m, 2)
                    for t in range(T):
                        last = dve.tensor_scalar(z[:, v % 2, t], X[:, bass.ds(m * T + t, 1), :].rearrange("p o c -> p (o c)"), mv[:, v, t, 0:1], q[:, v, 0, t:t + 1], ALU.subtract, ALU.mult)
                    last.then_inc(c_z, 1)
                m = n - M_O
                if live(n, M_O, B):
                    v = (u - M_O) % 4
                    dve.wait_ge(c_hom, m + 1)
                    dve.wait_ge(c_pr, m + 1)
                    for t in range(T):
                        last = dve.scalar_tensor_tensor(dd[:, v % 2, t], ps[6][:, t * D:(t + 1) * D], norm[:, bass.ds(m * T + t, 1)], het[:, v, t], ALU.mult, ALU.subtract)
                    last.then_inc(c_d, 1)
                    dve.wait_ge(c_d, m + 1)
                    dve.scalar_tensor_tensor(dd[:, v % 2], th[:, v], 1.0, dd[:, v % 2], ALU.add, ALU.mult).then_inc(c_gd, 1)
                    dve.wait_ge(c_gd, m + 1)
                    dve.scalar_tensor_tensor(oo[:, v % 2], dd[:, v % 2], 0.5, het[:, v], ALU.mult, ALU.add).then_inc(c_o, 1)
                    dve.wait_ge(c_o, m + 1)
                    reused(dve, c_exp, m, 2)
                    dve.tensor_scalar(mn[:, v % 2], oo[:, v % 2], 0.0, None, ALU.min).then_inc(c_mn, 1)
                    dve.scalar_tensor_tensor(tokens(X, m), oo[:, v % 2], 0.0, tokens(X, m), ALU.max, ALU.add).then_inc(c_t2, 1)
                m = n - M_X3
                if live(n, M_X3, B):
                    v = (u - M_X3) % 4
                    dve.wait_ge(c_exp, m + 1)
                    dve.wait_ge(c_t2, m + 1)
                    dve.scalar_tensor_tensor(tokens(X, m), ee[:, v % 2], -1.0, tokens(X, m), ALU.add, ALU.add).then_inc(x3_rdy, 1)
                    held(x3_rdy, m + 1)
                    for t in range(T):
                        dve.bn_stats(st1[:, v % 2, t], X[:, bass.ds(m * T + t, 1), :].rearrange("p o c -> p (o c)")).then_inc(c_st3, 1)
                    held(c_st3, m * 2 * T + T)
                    for t in range(T):
                        dve.bn_aggr(mv1[:, v % 2, t], st1[:, v % 2, t]).then_inc(c_st3, 1)
                    dve.wait_ge(c_st3, (m + 1) * 2 * T)
                    dve.tensor_scalar(q1[:, v % 2], mv1[:, v % 2, :, 1:2].rearrange("p t o -> p (t o)"), LN_EPS, None, ALU.add).then_inc(c_q3, 1)
                    dve.tensor_copy(mean3[:, bass.ds(m * T, T)], mv1[:, v % 2, :, 0:1].rearrange("p t o -> p (t o)"))
                m = n - M_Z3
                if live(n, M_Z3, B):
                    v = (u - M_Z3) % 4
                    dve.wait_ge(c_pow3, m + 1)
                    reused(dve, c_z3t, m, 2)
                    for t in range(T):
                        last = dve.tensor_scalar(x0[:, v % 2, t], X[:, bass.ds(m * T + t, 1), :].rearrange("p o c -> p (o c)"), mv1[:, v % 2, t, 0:1], rstd3[:, bass.ds(m * T + t, 1)], ALU.subtract, ALU.mult)
                    last.then_inc(c_z3, 1)
                m = n - M_LG
                if live(n, M_LG, B):
                    dve.wait_ge(c_lgp, m + 1)
                    dve.tensor_scalar(lgt[:, bass.ds(m * T, T)], ps[7][:, 0:T * E].rearrange("p (t e) -> p t e", e=E), 1.0, None, ALU.mult).then_inc(c_lg, 1)
            pipeline(dve, B, M_LG, gnn1, peel=16)

            qlinks = [0]

            def qlink_(ins):
                qlinks[0] += 1
                ins.then_inc(qlink, 1)
                dve.wait_ge(qlink, qlinks[0])

            def oe(v, n=NT):
                return v.unsqueeze(2).to_broadcast([P, n, E])

            def ot(v, n=NT):
                return v.unsqueeze(1).to_broadcast([P, n, E])

            dve.wait_ge(pad_out, 7)
            dve.wait_ge(c_lg, B)
            qlink_(dve.tensor_reduce(v_[0], lgt, AX.X, ALU.max))
            dve.tensor_tensor(R[0], lgt, oe(v_[0]), ALU.subtract).then_inc(q_sub, 1)
            dve.wait_ge(q_exp, 1)
            qlink_(dve.tensor_reduce(v_[0], R[1], AX.X, ALU.add))
            qlink_(dve.reciprocal(v_[1], v_[0]))
            qlink_(dve.tensor_tensor(R[0], R[1], oe(v_[1]), ALU.mult))
            hot, top = [R[2], R[3]], [v_[2], v_[3]]
            for k in range(K):
                qlink_(dve.tensor_reduce(top[k], R[0], AX.X, ALU.max))
                qlink_(dve.tensor_tensor(R[1], R[0], oe(top[k]), ALU.is_equal))
                qlink_(dve.tensor_tensor(R[1], R[1], ot(rank_e[:]), ALU.mult))
                qlink_(dve.tensor_reduce(v_[4 + k], R[1], AX.X, ALU.max))
                qlink_(dve.tensor_tensor(hot[k], R[1], oe(v_[4 + k]), ALU.is_equal))
                if k == 0:
                    qlink_(dve.scalar_tensor_tensor(R[0], hot[k], -2.0, R[0], ALU.mult, ALU.add))
            dve.tensor_tensor(R[4], hot[0], hot[1], ALU.add).then_inc(q_M, 1)
            qlink_(dve.tensor_tensor(v_[0], top[0], top[1], ALU.add))
            qlink_(dve.tensor_scalar(v_[1], v_[0], 1e-9, None, ALU.add))
            qlink_(dve.reciprocal(v_[0], v_[1]))
            qlink_(dve.tensor_tensor(v_[6], top[0], v_[0], ALU.mult))
            qlink_(dve.tensor_tensor(v_[7], top[1], v_[0], ALU.mult))

            def col(t, c):
                return t[:, :, c:c + 1].rearrange("p t c -> p (t c)")

            dve.tensor_copy(col(pay, 0), v_[7])
            dve.tensor_tensor(col(pay, 1), v_[6], v_[7], ALU.subtract)
            dve.tensor_scalar(col(pay, 2), v_[4], -1.0, float(E), ALU.mult, ALU.add)
            dve.tensor_scalar(col(pay, 3), tok_id[:], float(NT * P), None, ALU.add)
            dve.wait_ge(q_rank, 1)
            tot = ps[2][:, 0:NT * E].rearrange("p (t e) -> p t e", e=E)
            qlink_(dve.tensor_copy(R[5], tot))
            for e in range(E):
                dve.tensor_tensor_scan(col(R[6], e), ones[:, 0:NT], col(R[5], e), 0.0, ALU.mult, ALU.add).then_inc(q_read, 1)
            dve.wait_ge(q_read, E)
            qlink_(dve.tensor_tensor(R[5], R[6], R[5], ALU.subtract))
            last_t = R[6][:, NT - 1:NT].rearrange("p o e -> p (o e)")
            qlink_(dve.tensor_scalar(cnt[0], last_t, float(P - 1), None, ALU.add))
            qlink_(dve.tensor_copy(cnt_i, cnt[0]))
            qlink_(dve.tensor_scalar(cnt_i, cnt_i, P.bit_length() - 1, None, ALU.logical_shift_right))
            qlink_(dve.tensor_copy(cnt[1], cnt_i))
            qlink_(dve.tensor_tensor_scan(cnt[2], ones[:, 0:E], cnt[1], 0.0, ALU.mult, ALU.add))
            qlink_(dve.tensor_tensor(cnt[3], cnt[2], cnt[1], ALU.subtract))
            qlink_(dve.tensor_scalar(cnt[4], cnt[3], float(P), None, ALU.mult))
            qlink_(dve.tensor_tensor(etmp, oe(gidx[:], NG), ot(cnt[2], NG), ALU.is_ge))
            qlink_(dve.tensor_reduce(etab[:], etmp, AX.X, ALU.add))
            qlink_(dve.tensor_scalar(etab[:], etab[:], float(E - 1), None, ALU.min))
            qlink_(dve.tensor_copy(etab_i[:], etab[0:1, :]))
            qlink_(dve.tensor_tensor(R[5], R[5], ot(cnt[4]), ALU.add))
            qlink_(dve.tensor_tensor(R[5], ps[0][:, 0:NT * E].rearrange("p (t e) -> p t e", e=E), R[5], ALU.add))
            for k in range(K):
                qlink_(dve.tensor_tensor(R[6], R[5], hot[k], ALU.mult))
                qlink_(dve.tensor_reduce(v_[k], R[6], AX.X, ALU.add))
                qlink_(dve.tensor_copy(col(slot_i, k), v_[k]))
            dve.memset(hold[:], 0.0).then_inc(q_done, 1)

            def rows_out(n, u):
                if not isinstance(n, int) or n >= 4:
                    dve.wait_ge(d_sc[u], (n - u) * 4 * K)
                one = bass.ds(n, 1)
                dve.tensor_scalar(XR[:, u, 0:D], X[:, one, :].rearrange("p o c -> p (o c)"), mean3[:, one], rstd3[:, one], ALU.subtract, ALU.mult)
                dve.tensor_scalar(XR[:, u, D:ROW], pay[:, one].rearrange("p o c -> p (o c)"), 1.0, None, ALU.mult)
                dve.tensor_copy(dispatch_i[:, u], slot_i[:, one].rearrange("p o k -> p (o k)")).then_inc(d_row, 1)
            dve.memset(hh[:, :, H:HC * P], 0.0).then_inc(qlink, 1)
            qlinks[0] += 1
            pipeline(dve, NT, 0, rows_out, peel=4)

            def ffn1(n, u):
                m = n - N_XT
                if live(n, N_XT, NG):
                    v = (u - N_XT) % 4
                    dve.wait_ge(e_xt, m + 1)
                    reused(dve, e_h, m, 2)
                    dve.tensor_copy(xsT[:, v % 2], ps[0][:, 0:P]).then_inc(e_xT, 1)
                    dve.tensor_scalar(isk1[:, v], XS[:, v, D + 2:D + 3], etab[:, bass.ds(m, 1)], None, ALU.is_equal).then_inc(e_is, 1)
                m = n - N_MUL
                if live(n, N_MUL, NG):
                    v = (u - N_MUL) % 4
                    dve.wait_ge(e_silu, m + 1)
                    reused(dve, e_ht, m, 2)
                    dve.tensor_tensor(hh[:, v % 2, 0:H], ps[3 + v % 2][:, 0:H], sg[:, v % 2], ALU.mult).then_inc(e_hh, 1)
                m = n - N_XT
                if live(n, N_XT, NG):
                    v = (u - N_XT) % 4
                    dve.wait_ge(e_is, m + 1)
                    dve.scalar_tensor_tensor(gate[:, bass.ds(m, 1)], isk1[:, v], XS[:, v, D + 1:D + 2], XS[:, v, D:D + 1], ALU.mult, ALU.add).then_inc(e_gate, 1)
                    dve.scalar_tensor_tensor(dest[:, bass.ds(m, 1)], isk1[:, v], -float(NT * P), XS[:, v, D + 3:D + 4], ALU.mult, ALU.add).then_inc(e_gate, 1)
                m = n - N_Y
                if live(n, N_Y, NG):
                    v = (u - N_Y) % 4
                    if not isinstance(m, int) or m >= 4:
                        dve.wait_ge(e_sc[v], (m - v) * 4)
                    dve.tensor_scalar(scatter_i[:, v:v + 1], dest[:, bass.ds(m, 1)], 1.0, None, ALU.mult).then_inc(e_dest, 1)
            pipeline(dve, NG, N_SC, ffn1)

            def last_sum(n, u):
                dve.wait_ge(o_in[u], (n - u) * 8 + 32)
                dve.tensor_tensor(ybb[:, u], ybb[:, u], ya[:, u], ALU.add).then_inc(o_a, 1)
                dve.wait_ge(o_a, n + 1)
                dve.tensor_tensor(ya[:, u], ybb[:, u], X[:, bass.ds(n * 4, 4), :].rearrange("p t c -> p (t c)"), ALU.add).then_inc(o_b, 1)
            pipeline(dve, NT // 4, 0, last_sum, peel=4)

        @block.tensor
        def _(pe):
            pe.wait_ge(s_id, 1)
            pe.wait_ge(s_row, 64)
            pe.transpose(ps_z[0][:, 0:NROW], rows[:], ident[0:NROW, 0:NROW]).then_inc(s_colp, 1)
            pe.wait_ge(s_col, 1)
            pe.wait_ge(s_wg, 48)

            def step(n, u):
                m = n - L_XPT
                if live(n, L_XPT, B):
                    v = (u - L_XPT) % 4
                    pe.wait_ge(xp_rdy, m + 1)
                    reused(pe, xp_sb, m, 1)
                    for t in range(T):
                        last = pe.transpose(ps_xp[:, t * P:(t + 1) * P], xp[:, v % 2, t], ident[:])
                    last.then_inc(xp_ps, 1)
                m = n - L_CONV
                if live(n, L_CONV, B):
                    v = (u - L_CONV) % 4
                    pe.wait_ge(at_sb, m + 1)
                    pe.wait_ge(hr_rdy, m + 1)
                    reused(pe, cv_read, m, 2)
                    for t in range(T):
                        acc = ps_cv[v % 2][:, t * S:t * S + D + 1]
                        for j in range(T):
                            pe.matmul(acc, AT[:, v, j, t * P:(t + 1) * P], hrel[:, v % 2, j], start=(j == 0), stop=False)
                        last = pe.matmul(ps_cv[v % 2][:, t * S:t * S + D], hT[:, v, t * P:(t + 1) * P], Wg[:, 1], start=False, stop=True)
                    last.then_inc(cv_ps, 1)
                m = n - L_ZT
                if live(n, L_ZT, B):
                    v = (u - L_ZT) % 4
                    pe.wait_ge(z_rdy, m + 1)
                    reused(pe, hT_rdy, m, 2)
                    for t in range(T):
                        last = pe.transpose(ps_z[v % 2][:, t * P:(t + 1) * P], z[:, v % 2, t], ident[:])
                    last.then_inc(z_ps, 1)
                m = n - L_AT
                if live(n, L_AT, B):
                    v = (u - L_AT) % 4
                    pe.wait_ge(adj_in[v], (m - v) * 4 + 16)
                    reused(pe, at_sb, m, 2)
                    for i in range(T):
                        for j in range(T):
                            last = pe.transpose(ps_at[v % 2][:, j * S + i * P:j * S + (i + 1) * P], AJ[:, v, i, j * P:(j + 1) * P], ident[:])
                    last.then_inc(at_ps, 1)
                m = n - L_HREL
                if live(n, L_HREL, B):
                    v = (u - L_HREL) % 4
                    pe.wait_ge(hT_rdy, m + 1)
                    reused(pe, hr_rdy, m, 1)
                    for t in range(T):
                        last = pe.matmul(ps_hr[:, t * D:(t + 1) * D], hT[:, v, t * P:(t + 1) * P], Wg[:, 0], start=True, stop=True)
                    last.then_inc(hr_ps, 1)
            pipeline(pe, B, LAG1, step)

            pe.wait_ge(r_g, 1)
            pe.matmul(ps[0][:, 0:B * E], one_S[:], rt[0].rearrange("p b e -> p (b e)"), start=True, stop=True).then_inc(r_lg, 1)
            pe.wait_ge(r_wd8, 1)
            pe.matmul(ps[1][0:B, 0:D], wd8[:], b2_sb[:], start=True, stop=True).then_inc(r_b2, 1)
            pe.wait_ge(r_b2w, 1)
            pe.wait_ge(cv_read, B)

            def ffn0(n, u):
                if live(n, 0, B):
                    pe.wait_ge(w_in[u], (n - u) * 16 + 64)
                    reused(pe, f_g, n, 2, per=K * FC)
                    for k in range(K):
                        for c in range(FC):
                            last = pe.matmul(ps[(u % 2) * K + k][:, c * S:(c + 1) * S], W1b[:, u, k, c * P:(c + 1) * P], X0T[:, bass.ds(n * S, S)], start=True, stop=True)
                        last.then_inc(f_h, 1)
                m = n - L_Y
                if live(n, L_Y, B):
                    v = (u - L_Y) % 4
                    pe.wait_ge(f_g, (m + 1) * K * FC)
                    reused(pe, f_sum, m, 2)
                    for k in range(K):
                        for t in range(T):
                            at = (k * T + t) * D
                            for c in range(FC):
                                last = pe.matmul(ps[4 + v % 2][:, at:at + D], gT[:, v % 2, k, c, t * P:(t + 1) * P], W2b[:, v, k, c], start=(c == 0), stop=(c == FC - 1))
                    last.then_inc(f_y, 1)
            pipeline(pe, B, LAG3, ffn0)

            pe.wait_ge(s_wc, 64)
            pe.wait_ge(f_sum, B)

            def gnn1(n, u):
                m = n - M_LG
                if live(n, M_LG, B):
                    v = (u - M_LG) % 4
                    pe.wait_ge(c_x3T, m + 1)
                    reused(pe, c_lg, m, 1)
                    for t in range(T):
                        last = pe.matmul(ps[7][:, t * E:(t + 1) * E], xp[:, v % 2, t], cols[:, 18:26], start=True, stop=True)
                    last.then_inc(c_lgp, 1)
                m = n - M_Z3T
                if live(n, M_Z3T, B):
                    v = (u - M_Z3T) % 4
                    pe.wait_ge(c_z3, m + 1)
                    reused(pe, c_x3T, m, 1)
                    for t in range(T):
                        last = pe.transpose(ps[1][:, t * P:(t + 1) * P], x0[:, v % 2, t], ident[:])
                    last.then_inc(c_z3t, 1)
                m = n - M_HOM
                if live(n, M_HOM, B):
                    v = (u - M_HOM) % 4
                    pe.wait_ge(at_in[v], (m - v) * 4 + 16)
                    pe.wait_ge(c_f1, m + 1)
                    reused(pe, c_o, m, 1)
                    for t in range(T):
                        for j in range(T):
                            last = pe.matmul(ps[6][:, t * D:(t + 1) * D], AT[:, v, j, t * P:(t + 1) * P], hrel[:, v % 2, j, 0:D], start=(j == 0), stop=(j == T - 1))
                    last.then_inc(c_hom, 1)
                m = n - M_ZT
                if live(n, M_ZT, B):
                    v = (u - M_ZT) % 4
                    pe.wait_ge(c_z, m + 1)
                    reused(pe, c_xT, m, 1)
                    for t in range(T):
                        last = pe.transpose(ps[0][:, t * P:(t + 1) * P], z[:, v % 2, t], ident[:])
                    last.then_inc(c_zt, 1)
                m = n - M_P
                if live(n, M_P, B):
                    v = (u - M_P) % 4
                    pp = PS[:, 2 + 2 * (v % 2):4 + 2 * (v % 2)]
                    pe.wait_ge(c_xT, m + 1)
                    reused(pe, c_pr, m, 2)
                    for t in range(T):
                        pe.matmul(pp[:, t, 0:3 * D], hT[:, v % 2, t * P:(t + 1) * P], Wc[:].rearrange("p a c -> p (a c)"), start=True, stop=False)
                        last = pe.matmul(pp[:, t, 2 * D:3 * D], ones[0:1, :], bt_row[:], start=False, stop=True)
                    last.then_inc(c_p, 1)
            pipeline(pe, B, M_LG, gnn1, peel=16)

            pe.wait_ge(q_M, 1)
            pe.matmul(ps[0][:, 0:NT * E], tri[:], R[4].rearrange("p t e -> p (t e)"), start=True, stop=True)
            pe.matmul(ps[2][:, 0:NT * E], ones[:], R[4].rearrange("p t e -> p (t e)"), start=True, stop=True).then_inc(q_rank, 1)
            def turn(n, u):
                pe.wait_ge(ws_in[u], (n - u) * 20 + 80)
                reused(pe, wp_sb, n, 1)
                for i in range(2):
                    for c in range(HC):
                        h = P if c < HC - 1 else HL
                        pe.transpose(ps[3 + i][:, c * P:c * P + h], w_stage[0:h, u % 2, (i * HC + c) * P:(i * HC + c + 1) * P], ident[0:h, 0:h])
                for c in range(HC):
                    h = P if c < HC - 1 else HL
                    last = pe.transpose(ps[5][0:h, c * D:(c + 1) * D], w2_stage[:, u % 2, c * P:c * P + h], ident[:])
                last.then_inc(wp_ps, 1)
            pipeline(pe, E, 0, turn, peel=4)
            pe.wait_ge(q_done, 1)
            pe.wait_ge(wp_sb, E)

            def ffn1(n, u):
                m = n - N_Y
                e = pe.value_load(etab_i[0:1, bass.ds(m, 1)], min_val=0, max_val=E - 1) if live(n, N_Y, NG) else None
                if live(n, N_Y, NG):
                    v = (u - N_Y) % 4
                    pe.wait_ge(e_hT, m + 1)
                    reused(pe, e_ys, m, 2)
                    for c in range(HC):
                        h = P if c < HC - 1 else HL
                        last = pe.matmul(ps[6 + v % 2][:, 0:D], hhT[0:h, v % 2, c], w2T[0:h, bass.ds(e, 1), c].rearrange("p o d -> p (o d)"), start=(c == 0), stop=(c == HC - 1))
                    last.then_inc(e_y, 1)
                m = n - N_HT
                if live(n, N_HT, NG):
                    v = (u - N_HT) % 4
                    pe.wait_ge(e_hh, m + 1)
                    reused(pe, e_hT, m, 1)
                    for c in range(HC):
                        last = pe.transpose(ps[5][:, c * P:(c + 1) * P], hh[:, v % 2, c * P:(c + 1) * P], ident[:])
                    last.then_inc(e_ht, 1)
                m = n - N_XT
                if live(n, N_XT, NG):
                    v = (u - N_XT) % 4
                    pe.wait_ge(e_in[v], (m - v) * 4 + 16)
                    reused(pe, e_xT, m, 1)
                    pe.transpose(ps[0][:, 0:P], XS[:, v, 0:D], ident[:]).then_inc(e_xt, 1)
                m = n - N_H
                if live(n, N_H, NG):
                    v = (u - N_H) % 4
                    e = pe.value_load(etab_i[0:1, bass.ds(m, 1)], min_val=0, max_val=E - 1)
                    pe.wait_ge(e_xT, m + 1)
                    reused(pe, e_silu, m, 2)
                    reused(pe, e_hh, m, 2)
                    pe.matmul(ps[1 + v % 2][:, 0:H], xsT[:, v % 2], w1T[:, bass.ds(e, 1)].rearrange("p o h -> p (o h)"), start=True, stop=True)
                    pe.matmul(ps[3 + v % 2][:, 0:H], xsT[:, v % 2], w3T[:, bass.ds(e, 1)].rearrange("p o h -> p (o h)"), start=True, stop=True).then_inc(e_h, 1)
            pipeline(pe, NG, N_SC, ffn1)


_INS = ['x', 'adj', 'L0_gnn_W_rel', 'L0_gnn_b_rel', 'L0_gnn_W_root', 'L0_gnn_ln_gamma', 'L0_gnn_ln_beta', 'L0_ffn_Wr',
        'L0_ffn_br', 'L0_ffn_W1', 'L0_ffn_b1', 'L0_ffn_W2', 'L0_ffn_b2', 'L0_ffn_gamma', 'L0_ffn_beta', 'L1_gnn_W_t',
        'L1_gnn_b_t', 'L1_gnn_W_h', 'L1_gnn_theta', 'L1_ffn_router_w', 'L1_ffn_w1', 'L1_ffn_w2', 'L1_ffn_w3']


def kernel(**inputs):
    import numpy as _np
    import concourse.bacc as _bacc
    from concourse import mybir as _mybir
    from concourse.bass_utils import run_bass_kernel_spmd as _run

    nc = _bacc.Bacc("TRN2", target_bir_lowering=False, num_devices=1)
    arrays, args = {}, []
    for name in _INS:
        a = _np.ascontiguousarray(inputs[name])
        arrays[f"in_{name}"] = a
        args.append(nc.dram_tensor(f"in_{name}", a.shape, _mybir.dt.from_np(a.dtype), kind="ExternalInput").ap())
    args.append(nc.dram_tensor("out", inputs['x'].shape, _mybir.dt.float32, kind="ExternalOutput").ap())
    build(nc, *args)
    r = _run(nc, [arrays], core_ids=[0])
    return r.results[0]["out"]
```

```python
import concourse.bass as bass
from concourse import mybir
from contextlib import ExitStack

P = 128
UNROLL = 4
PEEL = 12
LN_EPS = 1e-5
DEG_EPS = 1e-6


def pipeline(eng, count, lag, step, peel=PEEL):
    whole = count // UNROLL
    for n in range(peel):
        step(n, n % UNROLL)
    with eng.Fori(peel // UNROLL, whole) as g:
        for u in range(UNROLL):
            step(g * UNROLL + u, u)
    for n in range(whole * UNROLL, count + lag):
        step(n, n % UNROLL)


def live(n, lag, count):
    return not isinstance(n, int) or 0 <= n - lag < count


def reused(eng, done, m, depth, per=1):
    if not isinstance(m, int) or m >= depth:
        eng.wait_ge(done, (m - depth + 1) * per)


def build(nc, x, adj, W_rel, b_rel, W_root, g_gamma, g_beta, Wr, br, W1, b1, W2, b2, f_gamma, f_beta,
          W_t, b_t, W_h, theta, router_w, w1, w2, w3, out):
    F32 = mybir.dt.float32
    ACT = mybir.ActivationFunctionType
    ALU = mybir.AluOpType
    AX = mybir.AxisListType

    B, S, D = x.shape
    T = S // P
    NT = B * T
    E, _, F = W1.shape
    FC = F // P
    K = 2
    H = w1.shape[1]
    HC = -(-H // P)
    HL = H - (HC - 1) * P
    NG = NT * K + E
    ROW = D + 4
    NOWHERE = 1.0e6
    CAPACITY = float(-(-B * S * 5 // (4 * E)))

    ctx = ExitStack()
    with ctx:
        def sb(name, shape, dt=F32):
            return ctx.enter_context(nc.sbuf_tensor(name, shape, dt))

        def pb(name, shape):
            return ctx.enter_context(nc.psum_tensor(name, shape, F32))

        def sem(name):
            return ctx.enter_context(nc.semaphore(name))

        def dram(name, shape, dt=F32):
            return nc.dram_tensor(name, shape, dt, kind="Internal").ap()

        adjT_dram = dram("adjT_dram", (B, P, T * S))

        X = sb("X", [P, NT, D])
        X0T = sb("X0T", [D, B * S])
        tok_sum = sb("tok_sum", [D, B])
        deg = sb("deg", [P, NT])
        bias1 = sb("bias1", [P, NT])
        rstd1 = sb("rstd1", [P, NT])
        ident = sb("ident", [P, P])
        hold = sb("hold", [1, 1])
        half = sb("half", [P, NT])
        NROW = 2 + 16 + 8
        rows = sb("rows", [NROW, D])
        cols = sb("cols", [D, NROW])
        Wg = sb("Wg", [D, 2, D])
        brel = sb("brel", [P, D])

        ones = sb("ones", [P, P])
        one_S = sb("one_S", [P, P])
        Wr_sb = sb("Wr_sb", [D, E])
        br_b = sb("br_b", [P, E])
        b2_sb = sb("b2_sb", [E, D])
        fgam = sb("fgam", [P, D])
        fbet = sb("fbet", [P, D])
        rank_e = sb("rank_e", [P, E])
        wk = sb("wk", [P, B, K])
        eidx = sb("eidx", [P, B, K], mybir.dt.int32)
        b1s = sb("b1s", [P, B, K, FC])
        b2b = sb("b2b", [P, B, D])
        rv = [sb(f"rv{i}", [P, B]) for i in range(8)]
        r8 = [sb(f"r8_{i}", [P, E]) for i in range(3)]
        oh = sb("oh", [P, B, K, E])
        wd8 = sb("wd8", [E, B])
        b2w = sb("b2w", [B, D])
        b2w_dram = dram("b2w_dram", (B, D))
        Wc = sb("Wc", [D, 3, D])
        bt_row = sb("bt_row", [1, D])
        norm = sb("norm", [P, NT])
        w1T = sb("w1T", [D, E, H])
        w3T = sb("w3T", [D, E, H])
        w2T = sb("w2T", [P, E, HC, D])
        bias3 = sb("bias3", [P, NT])
        rstd3 = sb("rstd3", [P, NT])
        tri = sb("tri", [P, P])
        etab = sb("etab", [P, NG])
        etab_i = sb("etab_i", [1, NG + 8, 2], mybir.dt.int32)
        gidx = sb("gidx", [P, NG])
        tok_id = sb("tok_id", [P, NT])
        pad_row = sb("pad_row", [P, ROW])
        slots_dram = dram("slots_dram", (NG * P, ROW))
        y_dram = dram("y_dram", (K * NT * P, D))
        dispatch_i = sb("dispatch_i", [P, 4, K], mybir.dt.int32)
        scatter_i = sb("scatter_i", [P, 4], mybir.dt.int32)
        isk1 = sb("isk1", [P, 4, 1])
        gate = sb("gate", [P, NG])
        dest = sb("dest", [P, NG])
        padd = sb("padd", [P, 2])
        W1b = sb("W1b", [P, 4, K, F])
        W2b = sb("W2b", [P, 4, K, FC, D])
        gT = sb("gT", [P, 2, K, FC, S])
        xb = sb("xb", [P, 4, T, D])
        yb = sb("yb", [P, 4, T, D])
        xbeta = sb("xbeta", [P, 4, T, D])

        AJ = sb("AJ", [P, 4, T, S])
        AT = sb("AT", [P, 4, T, S])
        mv = sb("mv", [P, 4, T, 2])
        st = sb("st", [P, 2, T, 6])
        nm = sb("nm", [P, 4, T])
        nb = sb("nb", [P, 4, T])
        ab = sb("ab", [P, 4, 2, T])
        nm1 = sb("nm1", [P, 2, T])
        q = sb("q", [P, 4, 2, T])
        x0 = sb("x0", [P, 2, T, D])
        z = sb("z", [P, 2, T, D])
        xx = sb("xx", [P, 4, T, D])
        hT = sb("hT", [D, 4, S])
        hrel = sb("hrel", [P, 2, T, D + 1])
        cv = sb("cv", [P, 2, T, D])
        mv1 = sb("mv1", [P, 2, T, 2])
        st1 = sb("st1", [P, 2, T, 6])
        q1 = sb("q1", [P, 2, T])
        xp = sb("xp", [P, 2, T, D])

        PS = pb("PS", [P, 8, 512])
        ps = [PS[:, i] for i in range(8)]
        ps_at, ps_cv, ps_z, ps_hr, ps_xp = ps[0:2], ps[2:4], ps[4:6], ps[6], ps[7]

        w_stage = gT[:].rearrange("p a k c s -> p a (k c s)")
        w2_stage = xb[:].rearrange("p (a b) t c -> p a (b t c)", a=2)
        gflat = gT[:].rearrange("p a k c s -> p (a k c s)")
        wflat = W1b[:].rearrange("p a k f -> p (a k f)")
        het = gflat[:, 0:1024].rearrange("p (a t c) -> p a t c", a=4, t=T)
        th = gflat[:, 1024:2048].rearrange("p (a t c) -> p a t c", a=4, t=T)
        dd = wflat[:, 0:512].rearrange("p (a t c) -> p a t c", a=2, t=T)
        oo = wflat[:, 512:1024].rearrange("p (a t c) -> p a t c", a=2, t=T)
        mn = wflat[:, 1024:1536].rearrange("p (a t c) -> p a t c", a=2, t=T)
        ee = wflat[:, 1536:2048].rearrange("p (a t c) -> p a t c", a=2, t=T)
        ajflat = AJ[:].rearrange("p a t s -> p (a t s)")
        rt = [ajflat[:, i * B * E:(i + 1) * B * E].rearrange("p (b e) -> p b e", e=E) for i in range(7)]
        b2flat = b2b[:].rearrange("p b c -> p (b c)")
        lgt = b2flat[:, 0:NT * E].rearrange("p (t e) -> p t e", e=E)
        SR = NT * E
        R = [b2flat[:, SR * (i + 1):SR * (i + 2)].rearrange("p (t e) -> p t e", e=E) for i in range(7)]
        x0flat = X0T[:]
        at = [0]

        def carve(*shape):
            n = 1
            for d in shape:
                n *= d
            v = x0flat[:, at[0]:at[0] + n]
            at[0] += n
            if len(shape) == 1:
                return v
            names = "abcd"[:len(shape)]
            return v.rearrange(f"p ({' '.join(names)}) -> p {' '.join(names)}", **dict(zip(names, shape)))

        XR = carve(4, ROW)
        XS = carve(4, ROW)
        xsT = carve(2, P)
        sg = carve(2, H)
        hh = carve(2, HC * P)
        hhT = carve(2, HC, P)
        YS = carve(4, D)
        pay = carve(NT, 4)
        slot_f = carve(NT, K)
        slot_i = carve(NT, K).bitcast(mybir.dt.int32)
        v_ = [carve(NT) for _ in range(8)]
        etmp = carve(NG, E)
        cnt = [carve(E) for _ in range(6)]
        cnt_i = carve(E).bitcast(mybir.dt.int32)
        ya = AJ[:].rearrange("p a t s -> p a (t s)")
        ybb = AT[:].rearrange("p a t s -> p a (t s)")

        def tokens(t, m):
            return t[:, bass.ds(m * T, T), :]

        def tile(t, m):
            return t[:, bass.ds(m, 1), :].rearrange("p o c -> p (o c)")

        s_id = sem("s_id"); s_ones = sem("s_ones"); s_row = sem("s_row"); s_wg = sem("s_wg"); s_colp = sem("s_colp"); s_col = sem("s_col")
        x_in = [sem(f"x_in{i}") for i in range(4)]
        adj_in = [sem(f"adj_in{i}") for i in range(4)]
        at_ps = sem("at_ps"); at_sb = sem("at_sb"); at_out = [sem(f"at_out{i}") for i in range(4)]
        stat = sem("stat"); pow0 = sem("pow0"); q_rdy = sem("q_rdy")
        ab_a = sem("ab_a"); nb1 = sem("nb1"); f_nb = sem("f_nb"); c_nb = sem("c_nb"); c_nb3 = sem("c_nb3"); z_rdy = sem("z_rdy"); xx_rdy = sem("xx_rdy")
        z_ps = sem("z_ps"); hT_rdy = sem("hT_rdy"); hr_ps = sem("hr_ps"); hr_rdy = sem("hr_rdy")
        cv_ps = sem("cv_ps"); cv_bias = sem("cv_bias"); cv_read = sem("cv_read"); x1_rdy = sem("x1_rdy"); stat1 = sem("stat1"); q1_rdy = sem("q1_rdy"); pow1 = sem("pow1")
        xp_rdy = sem("xp_rdy"); xp_ps = sem("xp_ps"); xp_sb = sem("xp_sb")
        s_cst = sem("s_cst"); rlink = sem("rlink"); r_g = sem("r_g"); r_lg = sem("r_lg"); r_sub = sem("r_sub"); r_exp = sem("r_exp")
        r_wd8 = sem("r_wd8"); r_b2 = sem("r_b2"); r_b2w = sem("r_b2w"); r_b2d = sem("r_b2d"); r_b2b = sem("r_b2b"); r_done = sem("r_done"); r_eidx = sem("r_eidx")
        w_in = [sem(f"w_in{i}") for i in range(4)]
        f_h = sem("f_h"); f_g = sem("f_g"); f_y = sem("f_y"); f_xn = sem("f_xn"); f_xb = sem("f_xb"); f_xbeta = sem("f_xbeta")
        f_sum = sem("f_sum"); f_st = sem("f_st"); f_q = sem("f_q"); f_pow = sem("f_pow"); f_n = sem("f_n"); f_gm = sem("f_gm"); x2_rdy = sem("x2_rdy")
        s_wc = sem("s_wc"); c_deg = sem("c_deg"); c_norm = sem("c_norm")
        ws_in = [sem(f"ws_in{i}") for i in range(4)]
        wp_ps = sem("wp_ps"); wp_sb = sem("wp_sb")
        at_in = [sem(f"at_in{i}") for i in range(4)]
        c_st = sem("c_st"); c_q = sem("c_q"); c_pow = sem("c_pow"); c_z = sem("c_z"); c_zt = sem("c_zt"); c_xT = sem("c_xT"); c_p = sem("c_p")
        c_f1 = sem("c_f1"); c_pr = sem("c_pr"); c_hom = sem("c_hom"); c_o = sem("c_o"); c_mn = sem("c_mn"); c_exp = sem("c_exp")
        c_t2 = sem("c_t2"); x3_rdy = sem("x3_rdy"); c_st3 = sem("c_st3"); c_q3 = sem("c_q3"); c_pow3 = sem("c_pow3"); c_z3 = sem("c_z3"); c_z3t = sem("c_z3t"); c_x3T = sem("c_x3T")
        c_lgp = sem("c_lgp"); c_lg = sem("c_lg")
        qlink = sem("qlink"); q_sub = sem("q_sub"); q_exp = sem("q_exp"); q_M = sem("q_M"); q_rank = sem("q_rank"); q_read = sem("q_read"); q_done = sem("q_done")
        pad_out = sem("pad_out"); p_held = sem("p_held"); d_pad = sem("d_pad")
        d_row = sem("d_row"); d_sc = [sem(f"d_sc{i}") for i in range(4)]
        e_in = [sem(f"e_in{i}") for i in range(4)]
        e_xt = sem("e_xt"); e_xT = sem("e_xT"); e_is = sem("e_is"); e_gate = sem("e_gate"); e_dest = sem("e_dest"); e_h = sem("e_h"); e_silu = sem("e_silu"); e_hh = sem("e_hh")
        e_ht = sem("e_ht"); e_hT = sem("e_hT"); e_y = sem("e_y"); e_ys = sem("e_ys"); e_sc = [sem(f"e_sc{i}") for i in range(4)]
        o_in = [sem(f"o_in{i}") for i in range(4)]; o_b = sem("o_b"); o_out = [sem(f"o_out{i}") for i in range(4)]
        block = ctx.enter_context(nc.Block())

        L_Z, L_ZT, L_AT, L_HREL, L_CONV, L_X1, L_XP, L_XPT = 1, 2, 3, 3, 4, 5, 6, 7
        LAG1 = L_XPT
        L_Y, L_SUM, L_N, L_X2 = 1, 2, 3, 4
        LAG3 = L_X2
        M_Z, M_ZT, M_P, M_PR, M_HOM, M_O, M_X3, M_Z3, M_Z3T, M_LG, M_LGC = 1, 2, 3, 4, 5, 6, 7, 8, 9, 10, 11
        LAG4 = M_LGC
        N_XT, N_H, N_MUL, N_HT, N_Y, N_SC = 1, 2, 3, 4, 5, 6

        @block.sync
        def _(sp):
            sp.dma_start(rows[0:1, :], g_gamma.rearrange("(a c) -> a c", a=1)).then_inc(s_row, 16)
            sp.dma_start(rows[1:2, :], g_beta.rearrange("(a c) -> a c", a=1)).then_inc(s_row, 16)
            sp.dma_start(rows[2:18, :], b1.rearrange("e (f c) -> (e f) c", c=D)).then_inc(s_row, 16)
            sp.dma_start(rows[18:26, :], router_w).then_inc(s_row, 16)

            def load(n, u):
                if live(n, 0, B):
                    reused(sp, q_rdy, n, 4, per=3)
                    sp.dma_start(tokens(X, n), x[bass.ds(n, 1)].rearrange("o (t p) c -> p (o t) c", p=P)).then_inc(x_in[u], 16)
                    reused(sp, at_ps, n, 4)
                    sp.dma_start(AJ[:, u], adj[bass.ds(n, 1)].rearrange("o (t p) j -> p (o t) j", p=P)).then_inc(adj_in[u], 16)
                    if isinstance(n, int) and n == 1:
                        sp.dma_start(Wr_sb[:], Wr).then_inc(s_cst, 16)
                        for i, w in enumerate((theta, W_h, W_t)):
                            sp.dma_start(Wc[:, i], w).then_inc(s_wc, 16)
                        sp.dma_start(bt_row[:], b_t.rearrange("(a c) -> a c", a=1)).then_inc(s_wc, 16)
                        sp.dma_start(br_b[:], br.rearrange("(a c) -> a c", a=1).to_broadcast([P, E])).then_inc(s_cst, 16)
                        sp.dma_start(b2_sb[:], b2).then_inc(s_cst, 16)
                        sp.dma_start(fgam[:], f_gamma.rearrange("(a c) -> a c", a=1).to_broadcast([P, D])).then_inc(s_cst, 16)
                        sp.dma_start(fbet[:], f_beta.rearrange("(a c) -> a c", a=1).to_broadcast([P, D])).then_inc(s_cst, 16)
                    if isinstance(n, int) and n == 0:
                        sp.dma_start(Wg[:, 0], W_rel).then_inc(s_wg, 16)
                        sp.dma_start(Wg[:, 1], W_root).then_inc(s_wg, 16)
                        sp.dma_start(brel[:], b_rel.rearrange("(a c) -> a c", a=1).to_broadcast([P, D])).then_inc(s_wg, 16)
            pipeline(sp, B, 0, load)
            sp.wait_ge(r_b2w, 1)
            sp.dma_start(b2w_dram, b2w[:]).then_inc(r_b2d, 16)
            sp.wait_ge(r_b2d, 16)
            sp.dma_start(b2b[:].rearrange("p b c -> p (b c)"), b2w_dram.rearrange("b c -> (b c)").unsqueeze(0).to_broadcast([P, B * D])).then_inc(r_b2b, 16)
            sp.wait_ge(r_eidx, 1)

            def load_experts(n, u):
                if live(n, 0, B):
                    reused(sp, f_y, n, 4)
                    for k in range(K):
                        e = sp.value_load(eidx[0:1, bass.ds(n, 1), k:k + 1].rearrange("p b k -> p (b k)"), min_val=0, max_val=E - 1)
                        sp.dma_start(W1b[:, u, k], W1[bass.ds(e, 1)].rearrange("o d f -> d (o f)")).then_inc(w_in[u], 16)
                        sp.dma_start(W2b[:, u, k], W2[bass.ds(e, 1)].rearrange("o (c p) d -> p (o c) d", p=P)).then_inc(w_in[u], 16)
            pipeline(sp, B, 0, load_experts)
            for u in range(4):
                sp.wait_ge(at_out[u], 16 * (B // 4))

            def load_adjT(n, u):
                reused(sp, c_hom, n, 4)
                sp.dma_start(AT[:, u].rearrange("p t i -> p (t i)"), adjT_dram[bass.ds(n, 1)].rearrange("o p f -> p (o f)")).then_inc(at_in[u], 16)
            pipeline(sp, B, 0, load_adjT, peel=4)

            def load_raw(n, u):
                reused(sp, wp_ps, n, 2)
                if isinstance(n, int) and n < 2:
                    sp.wait_ge(x3_rdy, B)
                one = bass.ds(n, 1)
                for i, w in enumerate((w1, w3)):
                    dst = w_stage[:, u % 2, i * HC * P:(i + 1) * HC * P].rearrange("p (c d) -> p c d", c=HC)
                    sp.dma_start(dst[:, 0:HC - 1], w[one, 0:(HC - 1) * P].rearrange("o (c p) d -> p (o c) d", p=P)).then_inc(ws_in[u], 16)
                    sp.dma_start(dst[0:HL, HC - 1], w[one, (HC - 1) * P:H].rearrange("o p d -> (o p) d")).then_inc(ws_in[u], 16)
                sp.dma_start(w2_stage[:, u % 2, 0:H], w2[one].rearrange("o d h -> (o d) h")).then_inc(ws_in[u], 16)
            pipeline(sp, E, 0, load_raw, peel=4)
            for u in range(4):
                sp.wait_ge(d_sc[u], 16 * K * (NT // 4))

            def load_slots(n, u):
                reused(sp, e_gate, n, 4, per=2)
                reused(sp, e_xt, n, 4)
                sp.dma_start(XS[:, u], slots_dram[bass.ds(n * P, P)]).then_inc(e_in[u], 16)
            pipeline(sp, NG, 0, load_slots, peel=4)

            for u in range(4):
                sp.wait_ge(e_sc[u], 16 * (NG // 4))

            def load_y(n, u):
                if live(n, 0, NT // 4):
                    if not isinstance(n, int) or n >= 4:
                        sp.wait_ge(o_out[u], (n - u) * 4)
                    sp.dma_start(ya[:, u].rearrange("p (t c) -> p t c", c=D), y_dram[bass.ds(n * 4 * P, 4 * P)].rearrange("(t p) c -> p t c", p=P)).then_inc(o_in[u], 16)
                    sp.dma_start(ybb[:, u].rearrange("p (t c) -> p t c", c=D), y_dram[bass.ds(n * 4 * P + NT * P, 4 * P)].rearrange("(t p) c -> p t c", p=P)).then_inc(o_in[u], 16)
            pipeline(sp, NT // 4, 0, load_y, peel=4)

        @block.gpsimd
        def _(gp):
            gp.memset(ident[:], 0.0).then_inc(s_ones, 1)
            gp.memset(half[:], -0.5).then_inc(s_ones, 1)
            gp.memset(hrel[:, :, :, D:D + 1], 1.0).then_inc(s_ones, 1)
            gp.memset(ones[:], 1.0).then_inc(s_ones, 1)
            gp.memset(one_S[:], 1.0 / S).then_inc(s_ones, 1)
            gp.iota(rank_e[:], pattern=[[-1, E]], base=E, channel_multiplier=0, allow_small_or_imprecise_dtypes=True).then_inc(s_ones, 1)
            gp.wait_ge(s_ones, 6)
            gp.memset(pad_row[:], 0.0).then_inc(pad_out, 1)
            gp.wait_ge(pad_out, 1)
            gp.memset(pad_row[:, D + 2:D + 3], -1.0).then_inc(pad_out, 1)
            gp.memset(pad_row[:, D + 3:D + 4], NOWHERE).then_inc(pad_out, 1)
            gp.memset(padd[:], 0.0).then_inc(pad_out, 1)
            gp.iota(gidx[:], pattern=[[1, NG]], base=0, channel_multiplier=0, allow_small_or_imprecise_dtypes=True).then_inc(pad_out, 1)
            gp.iota(tok_id[:], pattern=[[P, NT]], base=0, channel_multiplier=1, allow_small_or_imprecise_dtypes=True).then_inc(pad_out, 1)
            gp.affine_select(out=tri[:], in_=ones[:], compare_op=ALU.is_gt, fill=0.0, base=0,
                             pattern=[[1, P]], channel_multiplier=-1).then_inc(pad_out, 1)
            gp.affine_select(out=ident[:], in_=ident[:], compare_op=ALU.not_equal, fill=1.0, base=0,
                             pattern=[[-1, P]], channel_multiplier=1).then_inc(s_id, 1)

            def step(n, u):
                if live(n, 0, B):
                    gp.wait_ge(q_rdy, (n + 1) * 3)
                    gp.tensor_tensor(q[:, u], q[:, u], half[:, 0:4].rearrange("p (a t) -> p a t", a=2), ALU.pow).then_inc(pow0, 1)
                    reused(gp, xx_rdy, n, 4)
                    gp.wait_ge(pow0, n + 1)
                    gp.tensor_tensor(ab[:, u, 0], q[:, u, 0], ones[:, 0:T], ALU.add)
                    gp.tensor_tensor(ab[:, u, 1], q[:, u, 0], nm[:, u], ALU.mult).then_inc(ab_a, 1)
                m = n - L_X1
                if live(n, L_X1, B):
                    gp.wait_ge(q1_rdy, (m + 1) * 2)
                    gp.tensor_tensor(rstd1[:, bass.ds(m * T, T)], q1[:, (u - L_X1) % 2], half[:, 0:T], ALU.pow).then_inc(pow1, 1)
                    gp.wait_ge(pow1, m + 1)
                    gp.tensor_tensor(bias1[:, bass.ds(m * T, T)], rstd1[:, bass.ds(m * T, T)], nm1[:, (u - L_X1) % 2], ALU.mult).then_inc(nb1, 1)
            pipeline(gp, B, LAG1, step)
            gp.wait_ge(c_deg, 1)
            gp.tensor_tensor(norm[:], norm[:], half[:], ALU.pow).then_inc(c_norm, 1)
            gp.wait_ge(s_cst, 80)
            gp.wait_ge(r_b2b, 16)

            def ffn0(n, u):
                if live(n, 0, B):
                    gp.wait_ge(f_xn, n + 1)
                    gp.tensor_tensor(xb[:, u], xb[:, u], b2b[:, bass.ds(n, 1), :].to_broadcast([P, T, D]), ALU.add).then_inc(f_xb, 1)
                    reused(gp, x2_rdy, n, 4)
                    gp.tensor_tensor(xbeta[:, u], tokens(X, n), fbet[:].unsqueeze(1).to_broadcast([P, T, D]), ALU.add).then_inc(f_xbeta, 1)
                m = n - L_SUM
                if live(n, L_SUM, B):
                    gp.wait_ge(f_q, (m + 1) * 2)
                    v = (u - L_SUM) % 4
                    gp.tensor_tensor(q[:, v, 0], q[:, v, 0], half[:, 0:T], ALU.pow).then_inc(f_pow, 1)
                    gp.wait_ge(f_pow, m + 1)
                    gp.tensor_tensor(nb[:, v], q[:, v, 0], nm[:, v], ALU.mult).then_inc(f_nb, 1)
            pipeline(gp, B, LAG3, ffn0)

            def gnn1(n, u):
                if live(n, 0, B):
                    gp.wait_ge(c_q, (n + 1) * 2)
                    gp.tensor_tensor(q[:, u, 0], q[:, u, 0], half[:, 0:T], ALU.pow).then_inc(c_pow, 1)
                    reused(gp, c_z, n, 4)
                    gp.wait_ge(c_pow, n + 1)
                    gp.tensor_tensor(nb[:, u], q[:, u, 0], nm[:, u], ALU.mult).then_inc(c_nb, 1)
                m = n - M_X3
                if live(n, M_X3, B):
                    gp.wait_ge(c_q3, (m + 1) * 2)
                    gp.tensor_tensor(rstd3[:, bass.ds(m * T, T)], q1[:, (u - M_X3) % 2], half[:, 0:T], ALU.pow).then_inc(c_pow3, 1)
                    gp.wait_ge(c_pow3, m + 1)
                    gp.tensor_tensor(bias3[:, bass.ds(m * T, T)], rstd3[:, bass.ds(m * T, T)], nm1[:, (u - M_X3) % 2], ALU.mult).then_inc(c_nb3, 1)
            pipeline(gp, B, LAG4, gnn1, peel=16)

            def held(done, value, before):
                if not isinstance(before, int) or before > 0:
                    gp.wait_ge(p_held, before)
                gp.wait_ge(done, value)
                gp.tensor_tensor(padd[:, 0:1], padd[:, 1:2], padd[:, 1:2], ALU.add).then_inc(p_held, 1)

            gp.wait_ge(d_pad, 16)

            def dispatch(n, u):
                held(d_row, n + 1, n)
                for k in range(K):
                    gp.indirect_dma_start(slots_dram, bass.IndirectOffsetOnAxis(ap=dispatch_i[:, u, k:k + 1].bitcast(mybir.dt.uint32), axis=0),
                                          XR[:, u], None).then_inc(d_sc[u], 16)
            pipeline(gp, NT, 0, dispatch, peel=4)

            def give(n, u):
                m = n - N_SC
                if live(n, N_SC, NG):
                    v = (u - N_SC) % 4
                    gp.wait_ge(e_dest, m + 1)
                    held(e_ys, m + 1, NT + m)
                    gp.indirect_dma_start(y_dram, bass.IndirectOffsetOnAxis(ap=scatter_i[:, v:v + 1].bitcast(mybir.dt.uint32), axis=0),
                                          YS[:, v], None, bounds_check=K * NT * P - 1, oob_is_err=False).then_inc(e_sc[v], 16)
            pipeline(gp, NG, N_SC, give)

        @block.scalar
        def _(act):
            act.wait_ge(s_colp, 1)
            act.activation(cols[:], ps_z[0][:, 0:NROW], ACT.Copy).then_inc(s_col, 1)
            act.wait_ge(s_col, 1)

            def step(n, u):
                m = n - L_XPT
                if live(n, L_XPT, B):
                    act.wait_ge(xp_ps, m + 1)
                    act.activation(X0T[:, bass.ds(m * S, S)], ps_xp[:, 0:S], ACT.Identity, accum_out=tok_sum[:, bass.ds(m, 1)]).then_inc(xp_sb, 1)
                m = n - L_XP
                if live(n, L_XP, B):
                    v = (u - L_XP) % 4
                    act.wait_ge(nb1, m + 1)
                    reused(act, xp_ps, m, 2)
                    for t in range(T):
                        last = act.activation(xp[:, v % 2, t], tile(X, m * T + t), ACT.Identity, scale=rstd1[:, bass.ds(m * T + t, 1)], bias=bias1[:, bass.ds(m * T + t, 1)])
                    last.then_inc(xp_rdy, 1)
                m = n - L_ZT
                if live(n, L_ZT, B):
                    v = (u - L_ZT) % 4
                    act.wait_ge(z_ps, m + 1)
                    reused(act, cv_ps, m, 4)
                    act.activation(hT[:, v], ps_z[v % 2][:, 0:S], ACT.Identity, scale=cols[:, 0:1], bias=cols[:, 1:2]).then_inc(hT_rdy, 1)
                m = n - L_AT
                if live(n, L_AT, B):
                    v = (u - L_AT) % 4
                    act.wait_ge(at_ps, m + 1)
                    reused(act, cv_ps, m, 4)
                    if not isinstance(m, int) or m >= 4:
                        act.wait_ge(at_out[v], (m - v) * 4)
                    act.activation(AT[:, v], ps_at[v % 2][:].rearrange("p (t i) -> p t i", t=T), ACT.Copy).then_inc(at_sb, 1)
                m = n - L_ZT
                if live(n, L_ZT, B):
                    v = (u - L_ZT) % 4
                    act.wait_ge(ab_a, m + 1)
                    reused(act, x1_rdy, m, 4)
                    for t in range(T):
                        last = act.activation(xx[:, v, t], tile(X, m * T + t), ACT.Identity, scale=ab[:, v, 0, t:t + 1], bias=ab[:, v, 1, t:t + 1])
                    last.then_inc(xx_rdy, 1)
                m = n - L_HREL
                if live(n, L_HREL, B):
                    v = (u - L_HREL) % 4
                    act.wait_ge(hr_ps, m + 1)
                    reused(act, cv_ps, m, 2)
                    act.activation(hrel[:, v % 2, :, 0:D], ps_hr[:, 0:S].rearrange("p (t c) -> p t c", t=T), ACT.Copy).then_inc(hr_rdy, 1)
                m = n - L_AT
                if live(n, L_AT, B):
                    v = (u - L_AT) % 4
                    act.wait_ge(at_sb, m + 1)
                    act.dma_start(adjT_dram[bass.ds(m, 1)].rearrange("o p f -> p (o f)"), AT[:, v].rearrange("p t i -> p (t i)")).then_inc(at_out[v], 16)
            pipeline(act, B, LAG1, step)
            act.wait_ge(pad_out, 4)
            act.dma_start(slots_dram.rearrange("(g p) c -> p g c", p=P), pad_row[:].unsqueeze(1).to_broadcast([P, NG, ROW])).then_inc(d_pad, 16)

            act.wait_ge(r_sub, 1)
            act.activation(rt[2], rt[1], ACT.Exp).then_inc(r_exp, 1)
            act.wait_ge(r_sub, 2)
            act.activation(rt[2], rt[1], ACT.Exp).then_inc(r_exp, 1)
            act.wait_ge(r_sub, 3)
            act.activation(rv[5][:], rv[4][:], ACT.Exp).then_inc(r_exp, 1)
            act.wait_ge(r_b2, 1)
            act.activation(b2w[:], ps[1][0:B, 0:D], ACT.Copy).then_inc(r_b2w, 1)
            act.wait_ge(r_done, 1)

            def ffn0(n, u):
                m = n - L_N
                if live(n, L_N, B):
                    v = (u - L_N) % 4
                    act.wait_ge(f_nb, m + 1)
                    for t in range(T):
                        last = act.activation(yb[:, v, t], yb[:, v, t], ACT.Identity, scale=q[:, v, 0, t:t + 1], bias=nb[:, v, t:t + 1])
                    last.then_inc(f_n, 1)
                if live(n, 0, B):
                    reused(act, f_sum, n, 4, per=2)
                    for t in range(T):
                        last = act.activation(xb[:, u, t], tile(X, n * T + t), ACT.Identity, scale=rstd1[:, bass.ds(n * T + t, 1)], bias=bias1[:, bass.ds(n * T + t, 1)])
                    last.then_inc(f_xn, 1)
                    reused(act, f_y, n, 2)
                    for k in range(K):
                        act.wait_ge(f_h, n * K + k + 1)
                        for c in range(FC):
                            act.activation(gT[:, u % 2, k, c], ps[(u % 2) * K + k][:, c * S:(c + 1) * S], ACT.Gelu,
                                           bias=b1s[:, bass.ds(n, 1), k, c:c + 1].rearrange("p b c -> p (b c)")).then_inc(f_g, 1)
            pipeline(act, B, LAG3, ffn0)

            act.wait_ge(f_y, B)
            act.wait_ge(c_norm, 1)

            def gnn1(n, u):
                m = n - M_X3
                if live(n, M_X3, B):
                    act.wait_ge(c_mn, m + 1)
                    reused(act, x3_rdy, m, 2)
                    act.activation(ee[:, (u - M_X3) % 2], mn[:, (u - M_X3) % 2], ACT.Exp).then_inc(c_exp, 1)
                m = n - M_PR
                if live(n, M_PR, B):
                    v = (u - M_PR) % 4
                    pp = PS[:, 2 + 2 * (v % 2):4 + 2 * (v % 2)]
                    act.wait_ge(c_p, m + 1)
                    reused(act, c_hom, m, 2)
                    reused(act, c_o, m, 4, per=3)
                    for t in range(T):
                        last = act.activation(hrel[:, v % 2, t, 0:D], pp[:, t, 0:D], ACT.Copy, scale=norm[:, bass.ds(m * T + t, 1)])
                    last.then_inc(c_f1, 1)
                    act.activation(het[:, v], pp[:, :, D:2 * D], ACT.Copy)
                    act.activation(th[:, v], pp[:, :, 2 * D:3 * D], ACT.Tanh, scale=0.5).then_inc(c_pr, 1)
                m = n - M_Z3
                if live(n, M_Z3, B):
                    v = (u - M_Z3) % 4
                    act.wait_ge(c_nb3, m + 1)
                    reused(act, c_z3t, m, 2)
                    for t in range(T):
                        last = act.activation(x0[:, v % 2, t], tile(X, m * T + t), ACT.Identity, scale=rstd3[:, bass.ds(m * T + t, 1)], bias=bias3[:, bass.ds(m * T + t, 1)])
                    last.then_inc(c_z3, 1)
                m = n - M_Z
                if live(n, M_Z, B):
                    v = (u - M_Z) % 4
                    act.wait_ge(c_nb, m + 1)
                    reused(act, c_zt, m, 2)
                    for t in range(T):
                        last = act.activation(z[:, v % 2, t], tile(X, m * T + t), ACT.Identity, scale=q[:, v, 0, t:t + 1], bias=nb[:, v, t:t + 1])
                    last.then_inc(c_z, 1)
                m = n - M_Z3T
                if live(n, M_Z3T, B):
                    act.wait_ge(c_z3t, m + 1)
                    reused(act, c_lgp, m, 2)
                    act.activation(xp[:, (u - M_Z3T) % 2].rearrange("p t c -> p (t c)"), ps[1][:, 0:S], ACT.Copy).then_inc(c_x3T, 1)
                m = n - M_ZT
                if live(n, M_ZT, B):
                    act.wait_ge(c_zt, m + 1)
                    reused(act, c_p, m, 2)
                    act.activation(hT[:, (u - M_ZT) % 2], ps[0][:, 0:S], ACT.Copy).then_inc(c_xT, 1)
            pipeline(act, B, LAG4, gnn1, peel=16)

            act.wait_ge(q_sub, 1)
            act.activation(R[1], R[0], ACT.Exp).then_inc(q_exp, 1)

            def turned(n, u):
                act.wait_ge(wp_ps, n + 1)
                e = bass.ds(n, 1)
                act.activation(w1T[:, e], ps[3][:, 0:H].unsqueeze(1), ACT.Copy)
                act.activation(w3T[:, e], ps[4][:, 0:H].unsqueeze(1), ACT.Copy)
                act.activation(w2T[:, e, 0:HC - 1].rearrange("p o c d -> p (o c) d"), ps[5][:, 0:(HC - 1) * D].rearrange("p (c d) -> p c d", d=D), ACT.Copy)
                act.activation(w2T[0:HL, e, HC - 1], ps[5][0:HL, (HC - 1) * D:HC * D].unsqueeze(1), ACT.Copy).then_inc(wp_sb, 1)
            pipeline(act, E, 0, turned, peel=4)

            def ffn1(n, u):
                m = n - N_MUL
                if live(n, N_MUL, NG):
                    v = (u - N_MUL) % 4
                    act.wait_ge(e_h, m + 1)
                    reused(act, e_hh, m, 2)
                    act.activation(sg[:, v % 2], ps[1 + v % 2][:, 0:H], ACT.Silu).then_inc(e_silu, 1)
                m = n - N_Y
                if live(n, N_Y, NG):
                    v = (u - N_Y) % 4
                    act.wait_ge(e_y, m + 1)
                    act.wait_ge(e_gate, (m + 1) * 2)
                    if not isinstance(m, int) or m >= 4:
                        act.wait_ge(e_sc[v], (m - v) * 4)
                    act.activation(YS[:, v], ps[6 + v % 2][:, 0:D], ACT.Copy, scale=gate[:, bass.ds(m, 1)]).then_inc(e_ys, 1)
                m = n - N_HT
                if live(n, N_HT, NG):
                    v = (u - N_HT) % 4
                    act.wait_ge(e_ht, m + 1)
                    reused(act, e_y, m, 2)
                    act.activation(hhT[:, v % 2].rearrange("p c s -> p (c s)"), ps[5][:, 0:HC * P], ACT.Copy).then_inc(e_hT, 1)
            pipeline(act, NG, N_SC, ffn1)

            def store(n, u):
                act.wait_ge(o_b, n * 2 + 2)
                act.dma_start(out[bass.ds(n * 2, 2)].rearrange("b (t p) c -> p (b t) c", p=P), ya[:, u].rearrange("p (t c) -> p t c", c=D)).then_inc(o_out[u], 16)
            pipeline(act, NT // 4, 0, store, peel=4)
            for u in range(4):
                act.wait_ge(o_out[u], 16 * (NT // 16))

        @block.vector
        def _(dve):
            def held(done, value):
                dve.wait_ge(done, value)
                dve.memset(hold[:], 0.0)

            dve.wait_ge(s_ones, 6)
            dve.wait_ge(s_wg, 48)

            def var_of(v):
                return v[:, :, 1:2].rearrange("p t o -> p (t o)")

            def mean_of(v):
                return v[:, :, 0:1].rearrange("p t o -> p (t o)")

            def step(n, u):
                m = n - L_X1
                new, old = live(n, 0, B), live(n, L_X1, B)
                v = (u - L_X1) % 4
                pc = ps_cv[v % 2].rearrange("p (t c) -> p t c", t=T)
                if old:
                    dve.wait_ge(cv_ps, m + 1)
                    dve.tensor_tensor(cv[:, v % 2], pc[:, :, 0:D], brel[:].unsqueeze(1).to_broadcast([P, T, D]), ALU.add).then_inc(cv_bias, 1)
                if new:
                    held(x_in[u], (n - u) * 4 + 16)
                    for t in range(T):
                        dve.bn_stats(st[:, u % 2, t], tile(X, n * T + t)).then_inc(stat, 1)
                if old:
                    dve.wait_ge(cv_bias, m + 1)
                    dve.wait_ge(xx_rdy, m + 1)
                    dve.scalar_tensor_tensor(tokens(X, m), cv[:, v % 2], 0.0, xx[:, v], ALU.max, ALU.add).then_inc(x1_rdy, 1)
                if new:
                    held(stat, n * 2 * T + T)
                    for t in range(T):
                        dve.bn_aggr(mv[:, u, t], st[:, u % 2, t]).then_inc(stat, 1)
                if old:
                    dve.wait_ge(x1_rdy, m + 1)
                    dve.tensor_scalar(deg[:, bass.ds(m * T, T)], pc[:, :, D:D + 1].rearrange("p t o -> p (t o)"), 1.0, None, ALU.mult).then_inc(cv_read, 1)
                    for t in range(T):
                        dve.bn_stats(st1[:, v % 2, t], tile(X, m * T + t)).then_inc(stat1, 1)
                if new:
                    reused(dve, ab_a, n, 4)
                    dve.wait_ge(stat, (n + 1) * 2 * T)
                    dve.tensor_scalar(nm[:, u], mean_of(mv[:, u]), -1.0, None, ALU.mult).then_inc(q_rdy, 1)
                    dve.tensor_scalar(q[:, u, 0], var_of(mv[:, u]), LN_EPS, None, ALU.add).then_inc(q_rdy, 1)
                    dve.tensor_scalar(q[:, u, 1], var_of(mv[:, u]), 1.0 + LN_EPS, LN_EPS * LN_EPS, ALU.mult, ALU.add).then_inc(q_rdy, 1)
                if old:
                    held(stat1, m * 2 * T + T)
                    for t in range(T):
                        dve.bn_aggr(mv1[:, v % 2, t], st1[:, v % 2, t]).then_inc(stat1, 1)
                k = n - L_Z
                if live(n, L_Z, B):
                    w = (u - L_Z) % 4
                    dve.wait_ge(pow0, k + 1)
                    reused(dve, z_ps, k, 2)
                    for t in range(T):
                        last = dve.tensor_scalar(z[:, w % 2, t], tile(X, k * T + t), mv[:, w, t, 0:1], q[:, w, 1, t:t + 1], ALU.subtract, ALU.mult)
                    last.then_inc(z_rdy, 1)
                if old:
                    reused(dve, nb1, m, 2)
                    dve.wait_ge(stat1, (m + 1) * 2 * T)
                    dve.tensor_scalar(nm1[:, v % 2], mean_of(mv1[:, v % 2]), -1.0, None, ALU.mult).then_inc(q1_rdy, 1)
                    dve.tensor_scalar(q1[:, v % 2], var_of(mv1[:, v % 2]), LN_EPS, None, ALU.add).then_inc(q1_rdy, 1)
            pipeline(dve, B, LAG1, step)

            dve.wait_ge(cv_read, B)
            dve.tensor_scalar(norm[:], deg[:], DEG_EPS, None, ALU.add).then_inc(c_deg, 1)

            links = [0]

            def link(ins):
                links[0] += 1
                ins.then_inc(rlink, 1)
                dve.wait_ge(rlink, links[0])

            def over_e(v):
                return v.unsqueeze(2).to_broadcast([P, B, E])

            def over_b(v):
                return v.unsqueeze(1).to_broadcast([P, B, E])

            dve.wait_ge(s_cst, 80)
            dve.wait_ge(xp_sb, B)
            dve.tensor_tensor(rt[0], over_e(tok_sum[:]), over_b(Wr_sb[:]), ALU.mult).then_inc(r_g, 1)
            dve.wait_ge(r_lg, 1)
            lg = ps[0][:, 0:B * E].rearrange("p (b e) -> p b e", e=E)
            link(dve.tensor_tensor(rt[0], lg, over_b(br_b[:]), ALU.add))

            def softmax(src, dst, nth):
                link(dve.tensor_reduce(rv[0][:], src, AX.X, ALU.max))
                dve.tensor_tensor(rt[1], src, over_e(rv[0][:]), ALU.subtract).then_inc(r_sub, 1)
                dve.wait_ge(r_exp, nth)
                link(dve.tensor_reduce(rv[0][:], rt[2], AX.X, ALU.add))
                link(dve.reciprocal(rv[1][:], rv[0][:]))
                link(dve.tensor_tensor(dst, rt[2], over_e(rv[1][:]), ALU.mult))

            softmax(rt[0], rt[3], 1)
            link(dve.tensor_reduce(r8[0][:], rt[3].rearrange("p b e -> p e b"), AX.X, ALU.add))
            link(dve.tensor_scalar(r8[1][:], r8[0][:], float(S), None, ALU.mult))
            link(dve.reciprocal(r8[0][:], r8[1][:]))
            link(dve.tensor_scalar(r8[2][:], r8[0][:], CAPACITY, 1.0, ALU.mult, ALU.min))
            link(dve.tensor_tensor(rt[0], rt[3], over_b(r8[2][:]), ALU.mult))
            softmax(rt[0], rt[3], 2)

            def first_max(w, top, key, hot):
                link(dve.tensor_reduce(top, w, AX.X, ALU.max))
                link(dve.tensor_tensor(key, w, over_e(top), ALU.is_equal))
                link(dve.tensor_tensor(key, key, over_b(rank_e[:]), ALU.mult))
                link(dve.tensor_reduce(rv[7][:], key, AX.X, ALU.max))
                link(dve.tensor_tensor(hot, key, over_e(rv[7][:]), ALU.is_equal))

            for k in range(K):
                first_max(rt[3], rv[2 + k][:], rt[4], oh[:, :, k])
                link(dve.tensor_scalar(rv[6][:], rv[7][:], -1.0, float(E), ALU.mult, ALU.add))
                link(dve.tensor_copy(eidx[:, :, k:k + 1].rearrange("p b k -> p (b k)"), rv[6][:]))
                if k == 0:
                    link(dve.scalar_tensor_tensor(rt[3], oh[:, :, k], -2.0, rt[3], ALU.mult, ALU.add))
            dve.tensor_tensor(rv[4][:], rv[3][:], rv[2][:], ALU.subtract).then_inc(r_sub, 1)
            dve.sem_inc(r_eidx, 1)
            dve.wait_ge(r_exp, 3)
            link(dve.tensor_scalar(rv[6][:], rv[5][:], 1.0, None, ALU.add))
            link(dve.reciprocal(rv[7][:], rv[6][:]))
            w_of = [wk[:, :, k:k + 1].rearrange("p b k -> p (b k)") for k in range(K)]
            link(dve.tensor_copy(w_of[0], rv[7][:]))
            link(dve.tensor_tensor(w_of[1], rv[5][:], rv[7][:], ALU.mult))
            link(dve.tensor_tensor(rt[4], oh[:, :, 0], over_e(w_of[0]), ALU.mult))
            link(dve.tensor_tensor(rt[5], oh[:, :, 1], over_e(w_of[1]), ALU.mult))
            link(dve.tensor_tensor(rt[4], rt[4], rt[5], ALU.add))
            link(dve.tensor_tensor(rt[5][0:E], rt[4][0:E], ident[0:E, 0:E].unsqueeze(1).to_broadcast([E, B, E]), ALU.mult))
            dve.tensor_reduce(wd8[:], rt[5][0:E], AX.X, ALU.add).then_inc(r_wd8, 1)
            b1c = cols[:, 2:18].rearrange("p (e c) -> p c e", c=FC)
            for k in range(K):
                for c in range(FC):
                    link(dve.tensor_tensor(rt[6], oh[:, :, k], over_b(b1c[:, c]), ALU.mult))
                    link(dve.tensor_reduce(b1s[:, :, k, c:c + 1].rearrange("p b c -> p (b c)"), rt[6], AX.X, ALU.add))
            dve.memset(hold[:], 0.0).then_inc(r_done, 1)

            def ffn0(n, u):
                m, k = n - L_SUM, n - L_X2
                new, old = live(n, L_SUM, B), live(n, L_X2, B)
                v, w = (u - L_SUM) % 4, (u - L_X2) % 4
                py = ps[4 + v % 2].rearrange("p (k t c) -> p k t c", k=K, t=T)
                if new:
                    dve.wait_ge(f_xb, m + 1)
                    dve.wait_ge(f_y, m + 1)
                    dve.scalar_tensor_tensor(yb[:, v], py[:, 0], wk[:, bass.ds(m, 1), 0:1].rearrange("p b k -> p (b k)"), xb[:, v], ALU.mult, ALU.add).then_inc(f_sum, 1)
                if old:
                    dve.wait_ge(f_n, k + 1)
                    dve.tensor_tensor(yb[:, w], yb[:, w], fgam[:].unsqueeze(1).to_broadcast([P, T, D]), ALU.mult).then_inc(f_gm, 1)
                if new:
                    dve.wait_ge(f_sum, m * 2 + 1)
                    dve.scalar_tensor_tensor(yb[:, v], py[:, 1], wk[:, bass.ds(m, 1), 1:2].rearrange("p b k -> p (b k)"), yb[:, v], ALU.mult, ALU.add).then_inc(f_sum, 1)
                if old:
                    dve.wait_ge(f_gm, k + 1)
                    dve.wait_ge(f_xbeta, k + 1)
                    dve.tensor_tensor(tokens(X, k), yb[:, w], xbeta[:, w], ALU.add).then_inc(x2_rdy, 1)
                if new:
                    held(f_sum, m * 2 + 2)
                    for t in range(T):
                        dve.bn_stats(st[:, v % 2, t], yb[:, v, t]).then_inc(f_st, 1)
                    held(f_st, m * 2 * T + T)
                    for t in range(T):
                        dve.bn_aggr(mv[:, v, t], st[:, v % 2, t]).then_inc(f_st, 1)
                    dve.wait_ge(f_st, (m + 1) * 2 * T)
                    dve.tensor_scalar(nm[:, v], mean_of(mv[:, v]), -1.0, None, ALU.mult).then_inc(f_q, 1)
                    dve.tensor_scalar(q[:, v, 0], var_of(mv[:, v]), LN_EPS, None, ALU.add).then_inc(f_q, 1)
            pipeline(dve, B, LAG3, ffn0)

            dve.wait_ge(f_y, B)
            dve.wait_ge(f_xb, B)

            def gnn1(n, u):
                m = n - M_LGC
                if live(n, M_LGC, B):
                    dve.wait_ge(c_lgp, m + 1)
                    dve.tensor_scalar(lgt[:, bass.ds(m * T, T)], ps[7][:, 0:T * E].rearrange("p (t e) -> p t e", e=E), 1.0, None, ALU.mult).then_inc(c_lg, 1)
                m, k = n - M_O, n - M_X3
                new, mid, old = live(n, 0, B), live(n, M_O, B), live(n, M_X3, B)
                v, w = (u - M_O) % 4, (u - M_X3) % 4
                if new:
                    for t in range(T):
                        dve.bn_stats(st[:, u % 2, t], tile(X, n * T + t)).then_inc(c_st, 1)
                if mid:
                    dve.wait_ge(c_hom, m + 1)
                    dve.wait_ge(c_pr, m + 1)
                    for t in range(T):
                        last = dve.scalar_tensor_tensor(dd[:, v % 2, t], ps[6][:, t * D:(t + 1) * D], norm[:, bass.ds(m * T + t, 1)], het[:, v, t], ALU.mult, ALU.subtract)
                    last.then_inc(c_o, 1)
                if new:
                    held(c_st, n * 2 * T + T)
                    for t in range(T):
                        dve.bn_aggr(mv[:, u, t], st[:, u % 2, t]).then_inc(c_st, 1)
                if old:
                    dve.wait_ge(c_exp, k + 1)
                    dve.wait_ge(c_t2, k + 1)
                    dve.scalar_tensor_tensor(tokens(X, k), ee[:, w % 2], -1.0, tokens(X, k), ALU.add, ALU.add).then_inc(x3_rdy, 1)
                if mid:
                    dve.wait_ge(c_o, m * 3 + 1)
                    dve.scalar_tensor_tensor(dd[:, v % 2], th[:, v], 1.0, dd[:, v % 2], ALU.add, ALU.mult).then_inc(c_o, 1)
                if new:
                    reused(dve, c_z, n, 4)
                    dve.wait_ge(c_st, (n + 1) * 2 * T)
                    dve.tensor_scalar(nm[:, u], mean_of(mv[:, u]), -1.0, None, ALU.mult).then_inc(c_q, 1)
                    dve.tensor_scalar(q[:, u, 0], var_of(mv[:, u]), LN_EPS, None, ALU.add).then_inc(c_q, 1)
                if mid:
                    dve.wait_ge(c_o, m * 3 + 2)
                    dve.scalar_tensor_tensor(oo[:, v % 2], dd[:, v % 2], 0.5, het[:, v], ALU.mult, ALU.add).then_inc(c_o, 1)
                if old:
                    held(x3_rdy, k + 1)
                    for t in range(T):
                        dve.bn_stats(st1[:, w % 2, t], tile(X, k * T + t)).then_inc(c_st3, 1)
                if mid:
                    dve.wait_ge(c_o, m * 3 + 3)
                    reused(dve, c_exp, m, 2)
                    dve.tensor_scalar(mn[:, v % 2], oo[:, v % 2], 0.0, None, ALU.min).then_inc(c_mn, 1)
                if old:
                    held(c_st3, k * 2 * T + T)
                    for t in range(T):
                        dve.bn_aggr(mv1[:, w % 2, t], st1[:, w % 2, t]).then_inc(c_st3, 1)
                if mid:
                    dve.scalar_tensor_tensor(tokens(X, m), oo[:, v % 2], 0.0, tokens(X, m), ALU.max, ALU.add).then_inc(c_t2, 1)
                if old:
                    reused(dve, c_nb3, k, 2)
                    dve.wait_ge(c_st3, (k + 1) * 2 * T)
                    dve.tensor_scalar(nm1[:, w % 2], mean_of(mv1[:, w % 2]), -1.0, None, ALU.mult).then_inc(c_q3, 1)
                    dve.tensor_scalar(q1[:, w % 2], var_of(mv1[:, w % 2]), LN_EPS, None, ALU.add).then_inc(c_q3, 1)
            pipeline(dve, B, LAG4, gnn1, peel=16)

            qlinks = [0]

            def qlink_(ins):
                qlinks[0] += 1
                ins.then_inc(qlink, 1)
                dve.wait_ge(qlink, qlinks[0])

            def oe(v, n=NT):
                return v.unsqueeze(2).to_broadcast([P, n, E])

            def ot(v, n=NT):
                return v.unsqueeze(1).to_broadcast([P, n, E])

            dve.wait_ge(pad_out, 7)
            dve.wait_ge(c_lg, B)
            qlink_(dve.tensor_reduce(v_[0], lgt, AX.X, ALU.max))
            dve.tensor_tensor(R[0], lgt, oe(v_[0]), ALU.subtract).then_inc(q_sub, 1)
            dve.wait_ge(q_exp, 1)
            qlink_(dve.tensor_reduce(v_[0], R[1], AX.X, ALU.add))
            qlink_(dve.reciprocal(v_[1], v_[0]))
            qlink_(dve.tensor_tensor(R[0], R[1], oe(v_[1]), ALU.mult))
            hot, top = [R[2], R[3]], [v_[2], v_[3]]
            for k in range(K):
                qlink_(dve.tensor_reduce(top[k], R[0], AX.X, ALU.max))
                qlink_(dve.tensor_tensor(R[1], R[0], oe(top[k]), ALU.is_equal))
                qlink_(dve.tensor_tensor(R[1], R[1], ot(rank_e[:]), ALU.mult))
                qlink_(dve.tensor_reduce(v_[4 + k], R[1], AX.X, ALU.max))
                qlink_(dve.tensor_tensor(hot[k], R[1], oe(v_[4 + k]), ALU.is_equal))
                if k == 0:
                    qlink_(dve.scalar_tensor_tensor(R[0], hot[k], -2.0, R[0], ALU.mult, ALU.add))
            dve.tensor_tensor(R[4], hot[0], hot[1], ALU.add).then_inc(q_M, 1)
            qlink_(dve.tensor_tensor(v_[0], top[0], top[1], ALU.add))
            qlink_(dve.tensor_scalar(v_[1], v_[0], 1e-9, None, ALU.add))
            qlink_(dve.reciprocal(v_[0], v_[1]))
            qlink_(dve.tensor_tensor(v_[6], top[0], v_[0], ALU.mult))
            qlink_(dve.tensor_tensor(v_[7], top[1], v_[0], ALU.mult))

            def col(t, c):
                return t[:, :, c:c + 1].rearrange("p t c -> p (t c)")

            dve.tensor_copy(col(pay, 0), v_[7])
            dve.tensor_tensor(col(pay, 1), v_[6], v_[7], ALU.subtract)
            dve.tensor_scalar(col(pay, 2), v_[4], -1.0, float(E), ALU.mult, ALU.add)
            dve.tensor_scalar(col(pay, 3), tok_id[:], float(NT * P), None, ALU.add)
            dve.wait_ge(q_rank, 1)
            tot = ps[2][:, 0:NT * E].rearrange("p (t e) -> p t e", e=E)
            qlink_(dve.tensor_copy(R[5], tot))
            for e in range(E):
                dve.tensor_tensor_scan(col(R[6], e), ones[:, 0:NT], col(R[5], e), 0.0, ALU.mult, ALU.add).then_inc(q_read, 1)
            dve.wait_ge(q_read, E)
            qlink_(dve.tensor_tensor(R[5], R[6], R[5], ALU.subtract))
            last_t = R[6][:, NT - 1:NT].rearrange("p o e -> p (o e)")
            qlink_(dve.tensor_scalar(cnt[0], last_t, float(P - 1), None, ALU.add))
            qlink_(dve.tensor_copy(cnt_i, cnt[0]))
            qlink_(dve.tensor_scalar(cnt_i, cnt_i, P.bit_length() - 1, None, ALU.logical_shift_right))
            qlink_(dve.tensor_copy(cnt[1], cnt_i))
            qlink_(dve.tensor_tensor_scan(cnt[2], ones[:, 0:E], cnt[1], 0.0, ALU.mult, ALU.add))
            qlink_(dve.tensor_tensor(cnt[3], cnt[2], cnt[1], ALU.subtract))
            qlink_(dve.tensor_scalar(cnt[4], cnt[3], float(P), None, ALU.mult))
            qlink_(dve.tensor_tensor(etmp, oe(gidx[:], NG), ot(cnt[2], NG), ALU.is_ge))
            qlink_(dve.tensor_reduce(etab[:], etmp, AX.X, ALU.add))
            qlink_(dve.tensor_scalar(etab[:], etab[:], float(E - 1), None, ALU.min))
            qlink_(dve.memset(etab_i[:], 0))
            for i, lag in enumerate((N_H, N_Y)):
                qlink_(dve.tensor_copy(etab_i[:, lag:lag + NG, i], etab[0:1, :]))
            qlink_(dve.tensor_tensor(R[5], R[5], ot(cnt[4]), ALU.add))
            qlink_(dve.tensor_tensor(R[5], ps[0][:, 0:NT * E].rearrange("p (t e) -> p t e", e=E), R[5], ALU.add))
            for k in range(K):
                qlink_(dve.tensor_tensor(R[6], R[5], hot[k], ALU.mult))
                qlink_(dve.tensor_reduce(v_[k], R[6], AX.X, ALU.add))
                qlink_(dve.tensor_copy(col(slot_i, k), v_[k]))
            dve.memset(hold[:], 0.0).then_inc(q_done, 1)

            def rows_out(n, u):
                if not isinstance(n, int) or n >= 4:
                    dve.wait_ge(d_sc[u], (n - u) * 4 * K)
                one = bass.ds(n, 1)
                dve.tensor_scalar(XR[:, u, 0:D], tile(X, n), rstd3[:, one], bias3[:, one], ALU.mult, ALU.add)
                dve.tensor_scalar(XR[:, u, D:ROW], pay[:, one].rearrange("p o c -> p (o c)"), 1.0, None, ALU.mult)
                dve.tensor_copy(dispatch_i[:, u], slot_i[:, one].rearrange("p o k -> p (o k)")).then_inc(d_row, 1)
            dve.memset(hh[:, :, H:HC * P], 0.0).then_inc(qlink, 1)
            qlinks[0] += 1
            pipeline(dve, NT, 0, rows_out, peel=4)

            def ffn1(n, u):
                m = n - N_MUL
                if live(n, N_MUL, NG):
                    v = (u - N_MUL) % 4
                    dve.wait_ge(e_silu, m + 1)
                    reused(dve, e_ht, m, 2)
                    dve.tensor_tensor(hh[:, v % 2, 0:H], ps[3 + v % 2][:, 0:H], sg[:, v % 2], ALU.mult).then_inc(e_hh, 1)
                m = n - N_XT
                if live(n, N_XT, NG):
                    v = (u - N_XT) % 4
                    dve.wait_ge(e_xt, m + 1)
                    reused(dve, e_h, m, 2)
                    dve.tensor_copy(xsT[:, v % 2], ps[0][:, 0:P]).then_inc(e_xT, 1)
                    dve.tensor_scalar(isk1[:, v], XS[:, v, D + 2:D + 3], etab[:, bass.ds(m, 1)], None, ALU.is_equal).then_inc(e_is, 1)
                m = n - N_XT
                if live(n, N_XT, NG):
                    v = (u - N_XT) % 4
                    dve.wait_ge(e_is, m + 1)
                    dve.scalar_tensor_tensor(gate[:, bass.ds(m, 1)], isk1[:, v], XS[:, v, D + 1:D + 2], XS[:, v, D:D + 1], ALU.mult, ALU.add).then_inc(e_gate, 1)
                    dve.scalar_tensor_tensor(dest[:, bass.ds(m, 1)], isk1[:, v], -float(NT * P), XS[:, v, D + 3:D + 4], ALU.mult, ALU.add).then_inc(e_gate, 1)
                m = n - N_Y
                if live(n, N_Y, NG):
                    v = (u - N_Y) % 4
                    if not isinstance(m, int) or m >= 4:
                        dve.wait_ge(e_sc[v], (m - v) * 4)
                    dve.wait_ge(e_gate, (m + 1) * 2)
                    dve.tensor_scalar(scatter_i[:, v:v + 1], dest[:, bass.ds(m, 1)], 1.0, None, ALU.mult).then_inc(e_dest, 1)
            pipeline(dve, NG, N_SC, ffn1)

            def last_sum(n, u):
                dve.wait_ge(o_in[u], (n - u) * 8 + 32)
                dve.tensor_tensor(ybb[:, u], ybb[:, u], ya[:, u], ALU.add).then_inc(o_b, 1)
                dve.wait_ge(o_b, n * 2 + 1)
                dve.tensor_tensor(ya[:, u], ybb[:, u], X[:, bass.ds(n * 4, 4), :].rearrange("p t c -> p (t c)"), ALU.add).then_inc(o_b, 1)
            pipeline(dve, NT // 4, 0, last_sum, peel=4)

        @block.tensor
        def _(pe):
            pe.wait_ge(s_id, 1)
            pe.wait_ge(s_row, 64)
            pe.transpose(ps_z[0][:, 0:NROW], rows[:], ident[0:NROW, 0:NROW]).then_inc(s_colp, 1)
            pe.wait_ge(s_col, 1)
            pe.wait_ge(s_wg, 48)

            def step(n, u):
                m = n - L_XPT
                if live(n, L_XPT, B):
                    v = (u - L_XPT) % 4
                    pe.wait_ge(xp_rdy, m + 1)
                    reused(pe, xp_sb, m, 1)
                    for t in range(T):
                        last = pe.transpose(ps_xp[:, t * P:(t + 1) * P], xp[:, v % 2, t], ident[:])
                    last.then_inc(xp_ps, 1)
                m = n - L_CONV
                if live(n, L_CONV, B):
                    v = (u - L_CONV) % 4
                    pe.wait_ge(at_sb, m + 1)
                    pe.wait_ge(hr_rdy, m + 1)
                    reused(pe, cv_read, m, 2)
                    for t in range(T):
                        acc = ps_cv[v % 2][:, t * S:t * S + D + 1]
                        for j in range(T):
                            pe.matmul(acc, AT[:, v, j, t * P:(t + 1) * P], hrel[:, v % 2, j], start=(j == 0), stop=False)
                        last = pe.matmul(ps_cv[v % 2][:, t * S:t * S + D], hT[:, v, t * P:(t + 1) * P], Wg[:, 1], start=False, stop=True)
                    last.then_inc(cv_ps, 1)
                m = n - L_ZT
                if live(n, L_ZT, B):
                    v = (u - L_ZT) % 4
                    pe.wait_ge(z_rdy, m + 1)
                    reused(pe, hT_rdy, m, 2)
                    for t in range(T):
                        last = pe.transpose(ps_z[v % 2][:, t * P:(t + 1) * P], z[:, v % 2, t], ident[:])
                    last.then_inc(z_ps, 1)
                m = n - L_AT
                if live(n, L_AT, B):
                    v = (u - L_AT) % 4
                    pe.wait_ge(adj_in[v], (m - v) * 4 + 16)
                    reused(pe, at_sb, m, 2)
                    for i in range(T):
                        for j in range(T):
                            last = pe.transpose(ps_at[v % 2][:, j * S + i * P:j * S + (i + 1) * P], AJ[:, v, i, j * P:(j + 1) * P], ident[:])
                    last.then_inc(at_ps, 1)
                m = n - L_HREL
                if live(n, L_HREL, B):
                    v = (u - L_HREL) % 4
                    pe.wait_ge(hT_rdy, m + 1)
                    reused(pe, hr_rdy, m, 1)
                    for t in range(T):
                        last = pe.matmul(ps_hr[:, t * D:(t + 1) * D], hT[:, v, t * P:(t + 1) * P], Wg[:, 0], start=True, stop=True)
                    last.then_inc(hr_ps, 1)
            pipeline(pe, B, LAG1, step)

            pe.wait_ge(r_g, 1)
            pe.matmul(ps[0][:, 0:B * E], one_S[:], rt[0].rearrange("p b e -> p (b e)"), start=True, stop=True).then_inc(r_lg, 1)
            pe.wait_ge(r_wd8, 1)
            pe.matmul(ps[1][0:B, 0:D], wd8[:], b2_sb[:], start=True, stop=True).then_inc(r_b2, 1)
            pe.wait_ge(r_b2w, 1)
            pe.wait_ge(cv_read, B)

            def ffn0(n, u):
                if live(n, 0, B):
                    pe.wait_ge(w_in[u], (n - u) * 16 + 64)
                    reused(pe, f_g, n, 2, per=K * FC)
                    for k in range(K):
                        for c in range(FC):
                            last = pe.matmul(ps[(u % 2) * K + k][:, c * S:(c + 1) * S], W1b[:, u, k, c * P:(c + 1) * P], X0T[:, bass.ds(n * S, S)], start=True, stop=True)
                        last.then_inc(f_h, 1)
                m = n - L_Y
                if live(n, L_Y, B):
                    v = (u - L_Y) % 4
                    pe.wait_ge(f_g, (m + 1) * K * FC)
                    reused(pe, f_sum, m, 2, per=2)
                    for k in range(K):
                        for t in range(T):
                            at = (k * T + t) * D
                            for c in range(FC):
                                last = pe.matmul(ps[4 + v % 2][:, at:at + D], gT[:, v % 2, k, c, t * P:(t + 1) * P], W2b[:, v, k, c], start=(c == 0), stop=(c == FC - 1))
                    last.then_inc(f_y, 1)
            pipeline(pe, B, LAG3, ffn0)

            pe.wait_ge(s_wc, 64)
            pe.wait_ge(f_sum, B * 2)

            def gnn1(n, u):
                m = n - M_ZT
                if live(n, M_ZT, B):
                    v = (u - M_ZT) % 4
                    pe.wait_ge(c_z, m + 1)
                    reused(pe, c_xT, m, 1)
                    for t in range(T):
                        last = pe.transpose(ps[0][:, t * P:(t + 1) * P], z[:, v % 2, t], ident[:])
                    last.then_inc(c_zt, 1)
                m = n - M_Z3T
                if live(n, M_Z3T, B):
                    v = (u - M_Z3T) % 4
                    pe.wait_ge(c_z3, m + 1)
                    reused(pe, c_x3T, m, 1)
                    for t in range(T):
                        last = pe.transpose(ps[1][:, t * P:(t + 1) * P], x0[:, v % 2, t], ident[:])
                    last.then_inc(c_z3t, 1)
                m = n - M_HOM
                if live(n, M_HOM, B):
                    v = (u - M_HOM) % 4
                    pe.wait_ge(at_in[v], (m - v) * 4 + 16)
                    pe.wait_ge(c_f1, m + 1)
                    reused(pe, c_o, m, 1, per=3)
                    for t in range(T):
                        for j in range(T):
                            last = pe.matmul(ps[6][:, t * D:(t + 1) * D], AT[:, v, j, t * P:(t + 1) * P], hrel[:, v % 2, j, 0:D], start=(j == 0), stop=(j == T - 1))
                    last.then_inc(c_hom, 1)
                m = n - M_LG
                if live(n, M_LG, B):
                    v = (u - M_LG) % 4
                    pe.wait_ge(c_x3T, m + 1)
                    reused(pe, c_lg, m, 1)
                    for t in range(T):
                        last = pe.matmul(ps[7][:, t * E:(t + 1) * E], xp[:, v % 2, t], cols[:, 18:26], start=True, stop=True)
                    last.then_inc(c_lgp, 1)
                m = n - M_P
                if live(n, M_P, B):
                    v = (u - M_P) % 4
                    pp = PS[:, 2 + 2 * (v % 2):4 + 2 * (v % 2)]
                    pe.wait_ge(c_xT, m + 1)
                    reused(pe, c_pr, m, 2)
                    for t in range(T):
                        pe.matmul(pp[:, t, 0:3 * D], hT[:, v % 2, t * P:(t + 1) * P], Wc[:].rearrange("p a c -> p (a c)"), start=True, stop=False)
                        last = pe.matmul(pp[:, t, 2 * D:3 * D], ones[0:1, :], bt_row[:], start=False, stop=True)
                    last.then_inc(c_p, 1)
            pipeline(pe, B, LAG4, gnn1, peel=16)

            pe.wait_ge(q_M, 1)
            pe.matmul(ps[0][:, 0:NT * E], tri[:], R[4].rearrange("p t e -> p (t e)"), start=True, stop=True)
            pe.matmul(ps[2][:, 0:NT * E], ones[:], R[4].rearrange("p t e -> p (t e)"), start=True, stop=True).then_inc(q_rank, 1)
            def turn(n, u):
                pe.wait_ge(ws_in[u], (n - u) * 20 + 80)
                reused(pe, wp_sb, n, 1)
                for i in range(2):
                    for c in range(HC):
                        h = P if c < HC - 1 else HL
                        pe.transpose(ps[3 + i][:, c * P:c * P + h], w_stage[0:h, u % 2, (i * HC + c) * P:(i * HC + c + 1) * P], ident[0:h, 0:h])
                for c in range(HC):
                    h = P if c < HC - 1 else HL
                    last = pe.transpose(ps[5][0:h, c * D:(c + 1) * D], w2_stage[:, u % 2, c * P:c * P + h], ident[:])
                last.then_inc(wp_ps, 1)
            pipeline(pe, E, 0, turn, peel=4)
            pe.wait_ge(q_done, 1)
            pe.wait_ge(wp_sb, E)

            def ffn1(n, u):
                _, (e_of_h, e_of_y) = nc.values_load_multi_w_load_instructions(
                    etab_i[0:1, bass.ds(n, 1), :].rearrange("p s a -> p (s a)"), engines=(mybir.EngineType.PE,), min_val=0, max_val=E - 1)
                m = n - N_Y
                if live(n, N_Y, NG):
                    v = (u - N_Y) % 4
                    pe.wait_ge(e_hT, m + 1)
                    reused(pe, e_ys, m, 2)
                    for c in range(HC):
                        h = P if c < HC - 1 else HL
                        last = pe.matmul(ps[6 + v % 2][:, 0:D], hhT[0:h, v % 2, c], w2T[0:h, bass.ds(e_of_y, 1), c].rearrange("p o d -> p (o d)"), start=(c == 0), stop=(c == HC - 1))
                    last.then_inc(e_y, 1)
                m = n - N_XT
                if live(n, N_XT, NG):
                    v = (u - N_XT) % 4
                    pe.wait_ge(e_in[v], (m - v) * 4 + 16)
                    reused(pe, e_xT, m, 1)
                    pe.transpose(ps[0][:, 0:P], XS[:, v, 0:D], ident[:]).then_inc(e_xt, 1)
                m = n - N_HT
                if live(n, N_HT, NG):
                    v = (u - N_HT) % 4
                    pe.wait_ge(e_hh, m + 1)
                    reused(pe, e_hT, m, 1)
                    for c in range(HC):
                        last = pe.transpose(ps[5][:, c * P:(c + 1) * P], hh[:, v % 2, c * P:(c + 1) * P], ident[:])
                    last.then_inc(e_ht, 1)
                m = n - N_H
                if live(n, N_H, NG):
                    v = (u - N_H) % 4
                    pe.wait_ge(e_xT, m + 1)
                    reused(pe, e_silu, m, 2)
                    reused(pe, e_hh, m, 2)
                    pe.matmul(ps[1 + v % 2][:, 0:H], xsT[:, v % 2], w1T[:, bass.ds(e_of_h, 1)].rearrange("p o h -> p (o h)"), start=True, stop=True)
                    pe.matmul(ps[3 + v % 2][:, 0:H], xsT[:, v % 2], w3T[:, bass.ds(e_of_h, 1)].rearrange("p o h -> p (o h)"), start=True, stop=True).then_inc(e_h, 1)
            pipeline(pe, NG, N_SC, ffn1)


_INS = ['x', 'adj', 'L0_gnn_W_rel', 'L0_gnn_b_rel', 'L0_gnn_W_root', 'L0_gnn_ln_gamma', 'L0_gnn_ln_beta', 'L0_ffn_Wr',
        'L0_ffn_br', 'L0_ffn_W1', 'L0_ffn_b1', 'L0_ffn_W2', 'L0_ffn_b2', 'L0_ffn_gamma', 'L0_ffn_beta', 'L1_gnn_W_t',
        'L1_gnn_b_t', 'L1_gnn_W_h', 'L1_gnn_theta', 'L1_ffn_router_w', 'L1_ffn_w1', 'L1_ffn_w2', 'L1_ffn_w3']


def kernel(**inputs):
    import numpy as _np
    import concourse.bacc as _bacc
    from concourse import mybir as _mybir
    from concourse.bass_utils import run_bass_kernel_spmd as _run

    nc = _bacc.Bacc("TRN2", target_bir_lowering=False, num_devices=1)
    arrays, args = {}, []
    for name in _INS:
        a = _np.ascontiguousarray(inputs[name])
        arrays[f"in_{name}"] = a
        args.append(nc.dram_tensor(f"in_{name}", a.shape, _mybir.dt.from_np(a.dtype), kind="ExternalInput").ap())
    args.append(nc.dram_tensor("out", inputs['x'].shape, _mybir.dt.float32, kind="ExternalOutput").ap())
    build(nc, *args)
    r = _run(nc, [arrays], core_ids=[0])
    return r.results[0]["out"]
```

```python
import concourse.bass as bass
from concourse import mybir
from contextlib import ExitStack

P = 128
UNROLL = 4
PEEL = 12
LN_EPS = 1e-5
DEG_EPS = 1e-6


def pipeline(eng, count, lag, step, peel=PEEL, until=None, later=None, start=0):
    whole = count // UNROLL
    for n in range(start, peel):
        step(n, n % UNROLL)
    for first, end, do in ((peel, whole * UNROLL, step),) if until is None else ((peel, until, step), (until, whole * UNROLL, later)):
        with eng.Fori(first // UNROLL, end // UNROLL) as g:
            for u in range(UNROLL):
                do(g * UNROLL + u, u)
    for n in range(whole * UNROLL, count + lag):
        do(n, n % UNROLL)


def for_more(eng, first, end, step):
    with eng.Fori(first // UNROLL, end // UNROLL) as g:
        for u in range(UNROLL):
            step(g * UNROLL + u, u)


def live(n, lag, count):
    return not isinstance(n, int) or 0 <= n - lag < count


def reused(eng, done, m, depth, per=1):
    if not isinstance(m, int) or m >= depth:
        eng.wait_ge(done, (m - depth + 1) * per)


def build(nc, x, adj, W_rel, b_rel, W_root, g_gamma, g_beta, Wr, br, W1, b1, W2, b2, f_gamma, f_beta,
          W_t, b_t, W_h, theta, router_w, w1, w2, w3, out):
    F32 = mybir.dt.float32
    ACT = mybir.ActivationFunctionType
    ALU = mybir.AluOpType
    AX = mybir.AxisListType

    B, S, D = x.shape
    T = S // P
    NT = B * T
    E, _, F = W1.shape
    FC = F // P
    K = 2
    H = w1.shape[1]
    HC = -(-H // P)
    HL = H - (HC - 1) * P
    BLOCKS = 2
    NTB = NT // BLOCKS
    NGB = NTB * K + E
    NG = BLOCKS * NGB
    ROW = D + 4
    NOWHERE = 1.0e6
    CAPACITY = float(-(-B * S * 5 // (4 * E)))

    ctx = ExitStack()
    with ctx:
        def sb(name, shape, dt=F32):
            return ctx.enter_context(nc.sbuf_tensor(name, shape, dt))

        def pb(name, shape):
            return ctx.enter_context(nc.psum_tensor(name, shape, F32))

        def sem(name):
            return ctx.enter_context(nc.semaphore(name))

        def dram(name, shape, dt=F32):
            return nc.dram_tensor(name, shape, dt, kind="Internal").ap()

        adjT_dram = dram("adjT_dram", (B, P, T * S))

        X = sb("X", [P, NT, D])
        X0T = sb("X0T", [D, B * S])
        tok_sum = sb("tok_sum", [D, B])
        deg = sb("deg", [P, NT])
        bias1 = sb("bias1", [P, NT])
        rstd1 = sb("rstd1", [P, NT])
        ident = sb("ident", [P, P])
        hold = sb("hold", [1, 1])
        half = sb("half", [P, NT])
        NROW = 2 + 16 + 8
        rows = sb("rows", [NROW, D])
        cols = sb("cols", [D, NROW])
        Wg = sb("Wg", [D, 2, D])
        brel = sb("brel", [P, D])

        ones = sb("ones", [P, P])
        one_S = sb("one_S", [P, P])
        Wr_sb = sb("Wr_sb", [D, E])
        br_b = sb("br_b", [P, E])
        b2_sb = sb("b2_sb", [E, D])
        fgam = sb("fgam", [P, D])
        fbet = sb("fbet", [P, D])
        rank_e = sb("rank_e", [P, E])
        wk = sb("wk", [P, B, K])
        eidx = sb("eidx", [P, B, K], mybir.dt.int32)
        b1s = sb("b1s", [P, B, K, FC])
        b2b = sb("b2b", [P, B, D])
        rv = [sb(f"rv{i}", [P, B]) for i in range(8)]
        r8 = [sb(f"r8_{i}", [P, E]) for i in range(3)]
        oh = sb("oh", [P, B, K, E])
        wd8 = sb("wd8", [E, B])
        b2w = sb("b2w", [B, D])
        b2w_dram = dram("b2w_dram", (B, D))
        Wc = sb("Wc", [D, 3, D])
        bt_row = sb("bt_row", [1, D])
        norm = sb("norm", [P, NT])
        w1T = sb("w1T", [D, E, H])
        w3T = sb("w3T", [D, E, H])
        w2T = sb("w2T", [P, E, HC, D])
        bias3 = sb("bias3", [P, NT])
        rstd3 = sb("rstd3", [P, NT])
        tri = sb("tri", [P, P])
        etab = sb("etab", [P, NG])
        etab_i = sb("etab_i", [1, NG + 8], mybir.dt.int32)
        etab_f = sb("etab_f", [1, NG + 8])
        gidx = sb("gidx", [P, NGB])
        tok_id = sb("tok_id", [P, NT])
        pad_row = sb("pad_row", [P, ROW])
        slots_dram = dram("slots_dram", (NG * P, ROW))
        y_dram = dram("y_dram", (K * NT * P, D))
        dispatch_i = sb("dispatch_i", [P, 4, K], mybir.dt.int32)
        scatter_i = sb("scatter_i", [P, 4], mybir.dt.int32)
        isk1 = sb("isk1", [P, 4, 1])
        gate = sb("gate", [P, NG])
        dest = sb("dest", [P, NG])
        padd = sb("padd", [P, 2])
        W1b = sb("W1b", [P, 4, K, F])
        W2b = sb("W2b", [P, 4, K, FC, D])
        gT = sb("gT", [P, 2, K, FC, S])
        xb = sb("xb", [P, 4, T, D])
        yb = sb("yb", [P, 4, T, D])
        xbeta = sb("xbeta", [P, 4, T, D])

        AJ = sb("AJ", [P, 4, T, S])
        AT = sb("AT", [P, 4, T, S])
        mv = sb("mv", [P, 4, T, 2])
        st = sb("st", [P, 2, T, 6])
        nm = sb("nm", [P, 4, T])
        nb = sb("nb", [P, 4, T])
        ab = sb("ab", [P, 4, 2, T])
        nm1 = sb("nm1", [P, 2, T])
        mvc = sb("mvc", [P, 4, T, 2])
        stc = sb("stc", [P, 2, T, 6])
        nmc = sb("nmc", [P, 4, T])
        nbc = sb("nbc", [P, 4, T])
        qc = sb("qc", [P, 4, 2, T])
        q = sb("q", [P, 4, 2, T])
        x0 = sb("x0", [P, 2, T, D])
        z = sb("z", [P, 2, T, D])
        xx = sb("xx", [P, 4, T, D])
        hT = sb("hT", [D, 4, S])
        hrel = sb("hrel", [P, 2, T, D + 1])
        cv = sb("cv", [P, 2, T, D])
        mv1 = sb("mv1", [P, 2, T, 2])
        st1 = sb("st1", [P, 2, T, 6])
        q1 = sb("q1", [P, 2, T])
        xp = sb("xp", [P, 2, T, D])

        PS = pb("PS", [P, 8, 512])
        ps = [PS[:, i] for i in range(8)]
        ps_at, ps_cv, ps_z, ps_hr, ps_xp = ps[0:2], ps[2:4], ps[4:6], ps[6], ps[7]

        gflat = gT[:].rearrange("p a k c s -> p (a k c s)")
        wflat = W1b[:].rearrange("p a k f -> p (a k f)")
        W13 = 2 * HC * P
        big = [gflat, wflat, W2b[:].rearrange("p a k c d -> p (a k c d)")]
        small = [t[:].rearrange("p a t c -> p (a t c)") for t in (xb, yb, xbeta)]
        per_big, per_small = 8 * S // W13, 4 * T * D // H
        w13_raw = [big[e // per_big][:, e % per_big * W13:(e % per_big + 1) * W13] for e in range(min(E, 3 * per_big))]
        w13_raw += [b2b[:].rearrange("p b c -> p (b c)")[:, i * W13:(i + 1) * W13] for i in range(E - len(w13_raw))]
        w2_raw = [small[e // per_small][:, e % per_small * H:(e % per_small + 1) * H] for e in range(E)]
        turned = hT[:].rearrange("p (a b) s -> p a (b s)", a=2)
        het = gflat[:, 0:1024].rearrange("p (a t c) -> p a t c", a=4, t=T)
        th = gflat[:, 1024:2048].rearrange("p (a t c) -> p a t c", a=4, t=T)
        dd = wflat[:, 0:512].rearrange("p (a t c) -> p a t c", a=2, t=T)
        oo = wflat[:, 512:1024].rearrange("p (a t c) -> p a t c", a=2, t=T)
        mn = wflat[:, 1024:1536].rearrange("p (a t c) -> p a t c", a=2, t=T)
        ee = wflat[:, 1536:2048].rearrange("p (a t c) -> p a t c", a=2, t=T)
        ajflat = AJ[:].rearrange("p a t s -> p (a t s)")
        rt = [ajflat[:, i * B * E:(i + 1) * B * E].rearrange("p (b e) -> p b e", e=E) for i in range(7)]
        b2flat = b2b[:].rearrange("p b c -> p (b c)")
        lgt = b2flat[:, 0:NT * E].rearrange("p (t e) -> p t e", e=E)
        SR = NT * E
        R_all = [b2flat[:, SR * (i + 1):SR * (i + 2)].rearrange("p (t e) -> p t e", e=E) for i in range(7)]
        x0flat = X0T[:]
        at = [0]

        def carve(*shape):
            n = 1
            for d in shape:
                n *= d
            v = x0flat[:, at[0]:at[0] + n]
            at[0] += n
            if len(shape) == 1:
                return v
            names = "abcd"[:len(shape)]
            return v.rearrange(f"p ({' '.join(names)}) -> p {' '.join(names)}", **dict(zip(names, shape)))

        XR = carve(4, ROW)
        XS = carve(4, ROW)
        xsT = carve(2, P)
        sg = carve(2, H)
        hh = carve(2, HC * P)
        hhT = carve(2, HC, P)
        YS = carve(4, D)
        pay = carve(NT, 4)
        slot = carve(NT, K)
        v_all = [carve(NT) for _ in range(8)]
        etmp = carve(NGB, E)
        cnt = [carve(E) for _ in range(6)]
        cnt_i = carve(E).bitcast(mybir.dt.int32)
        ya = AJ[:].rearrange("p a t s -> p a (t s)")
        ybb = AT[:].rearrange("p a t s -> p a (t s)")
        z_y1, z_y2, z_sum = ya[:, 0, 0:2 * D], ybb[:, 0, 0:2 * D], ya[:, 1, 0:2 * D]

        def tokens(t, m):
            return t[:, bass.ds(m * T, T), :]

        def tile(t, m):
            return t[:, bass.ds(m, 1), :].rearrange("p o c -> p (o c)")

        s_id = sem("s_id"); s_ones = sem("s_ones"); s_row = sem("s_row"); s_wg = sem("s_wg"); s_colp = sem("s_colp"); s_col = sem("s_col")
        x_in = [sem(f"x_in{i}") for i in range(4)]
        adj_in = [sem(f"adj_in{i}") for i in range(4)]
        at_ps = sem("at_ps"); at_sb = sem("at_sb"); at_out = [sem(f"at_out{i}") for i in range(4)]
        stat = sem("stat"); pow0 = sem("pow0"); q_rdy = sem("q_rdy")
        ab_a = sem("ab_a"); nb1 = sem("nb1"); f_nb = sem("f_nb"); c_nb = sem("c_nb"); c_nb3 = sem("c_nb3"); z_rdy = sem("z_rdy"); xx_rdy = sem("xx_rdy")
        z_ps = sem("z_ps"); hT_rdy = sem("hT_rdy"); hr_ps = sem("hr_ps"); hr_rdy = sem("hr_rdy")
        cv_ps = sem("cv_ps"); cv_bias = sem("cv_bias"); cv_read = sem("cv_read"); x1_rdy = sem("x1_rdy"); stat1 = sem("stat1"); q1_rdy = sem("q1_rdy"); pow1 = sem("pow1")
        xp_rdy = sem("xp_rdy"); xp_ps = sem("xp_ps"); xp_sb = sem("xp_sb")
        s_cst = sem("s_cst"); rlink = sem("rlink"); r_g = sem("r_g"); r_lg = sem("r_lg"); r_sub = sem("r_sub"); r_exp = sem("r_exp")
        r_wd8 = sem("r_wd8"); r_b2 = sem("r_b2"); r_b2w = sem("r_b2w"); r_b2d = sem("r_b2d"); r_b2b = [sem(f"r_b2b{i}") for i in range(2)]; r_done = sem("r_done"); r_eidx = sem("r_eidx")
        w_in = [sem(f"w_in{i}") for i in range(4)]
        f_h = sem("f_h"); f_g = sem("f_g"); f_y = sem("f_y"); f_xn = sem("f_xn"); f_xb = sem("f_xb"); f_xbeta = sem("f_xbeta")
        f_sum = sem("f_sum"); f_st = sem("f_st"); f_q = sem("f_q"); f_pow = sem("f_pow"); f_n = sem("f_n"); f_gm = sem("f_gm"); x2_rdy = sem("x2_rdy")
        s_wc = sem("s_wc"); c_deg = sem("c_deg"); c_norm = sem("c_norm")
        ws_in = sem("ws_in")
        wp_ps = sem("wp_ps"); wp_sb = sem("wp_sb")
        at_in = [sem(f"at_in{i}") for i in range(4)]
        c_st = sem("c_st"); c_q = sem("c_q"); c_pow = sem("c_pow"); c_z = sem("c_z"); c_zt = sem("c_zt"); c_xT = sem("c_xT"); c_p = sem("c_p")
        c_f1 = sem("c_f1"); c_pr = sem("c_pr"); c_hom = sem("c_hom"); c_o = sem("c_o"); c_mn = sem("c_mn"); c_exp = sem("c_exp")
        c_t2 = sem("c_t2"); x3_rdy = sem("x3_rdy"); c_st3 = sem("c_st3"); c_q3 = sem("c_q3"); c_pow3 = sem("c_pow3"); c_z3 = sem("c_z3");
        c_lgp = sem("c_lgp"); c_lg = sem("c_lg")
        qlink = sem("qlink"); q_sub = sem("q_sub"); q_exp = sem("q_exp"); q_M = sem("q_M"); q_rank = sem("q_rank"); q_read = sem("q_read"); q_done = sem("q_done"); q_etab = sem("q_etab")
        pad_out = sem("pad_out"); p_held = sem("p_held"); d_pad = sem("d_pad")
        d_row = sem("d_row"); d_sc = [sem(f"d_sc{i}") for i in range(4)]
        e_in = [sem(f"e_in{i}") for i in range(4)]
        e_xt = sem("e_xt"); e_xT = sem("e_xT"); e_is = sem("e_is"); e_gate = sem("e_gate"); e_dest = sem("e_dest"); e_h = sem("e_h"); e_silu = sem("e_silu"); e_hh = sem("e_hh")
        e_ht = sem("e_ht"); e_hT = sem("e_hT"); e_y = sem("e_y"); e_ys = sem("e_ys"); e_sc = [sem(f"e_sc{i}") for i in range(4)]
        o_in = [sem(f"o_in{i}") for i in range(4)]; o_b = sem("o_b"); o_out = [sem(f"o_out{i}") for i in range(4)]
        z_in = sem("z_in"); z_b = sem("z_b"); z_out = sem("z_out")
        block = ctx.enter_context(nc.Block())

        L_Z, L_ZT, L_HT, L_XX, L_AT, L_HREL, L_CONV, L_X1, L_XP, L_XPT = 1, 2, 3, 3, 4, 4, 5, 6, 7, 8
        LAG1 = L_XPT
        L_ADJ = 3
        L_STORE = L_ADJ + L_AT + 1
        L_Y, L_SUM, L_N, L_X2 = 1, 2, 4, 5
        LAG3 = L_X2
        M_Z, M_ZT, M_P, M_PR, M_HOM, M_O, M_X3, M_Z3, M_Z3T, M_LG, M_LGC = 1, 2, 3, 4, 5, 6, 7, 8, 9, 10, 11
        LAG4 = M_LGC
        ROUTE = B // BLOCKS + M_LGC
        GIVEN = NG - 2 * NTB
        N_XT, N_H, N_MUL, N_HT, N_Y, N_SC = 1, 2, 3, 4, 5, 6

        def tiles_beside(n):
            j = 2 * (n - ROUTE)
            return range(j, j + 2 if n < B + LAG4 - 1 else NTB)

        @block.sync
        def _(sp):
            sp.dma_start(rows[0:1, :], g_gamma.rearrange("(a c) -> a c", a=1)).then_inc(s_row, 16)
            sp.dma_start(rows[1:2, :], g_beta.rearrange("(a c) -> a c", a=1)).then_inc(s_row, 16)
            sp.dma_start(rows[2:18, :], b1.rearrange("e (f c) -> (e f) c", c=D)).then_inc(s_row, 16)
            sp.dma_start(rows[18:26, :], router_w).then_inc(s_row, 16)

            def load_raw(e):
                for i, w in enumerate((w1, w3)):
                    raw = w13_raw[e][:, i * HC * P:(i + 1) * HC * P].rearrange("p (c d) -> p c d", c=HC)
                    sp.dma_start(raw[:, 0:HC - 1], w[e, 0:(HC - 1) * P].rearrange("(c p) d -> p c d", p=P)).then_inc(ws_in, 16)
                    sp.dma_start(raw[0:HL, HC - 1], w[e, (HC - 1) * P:H]).then_inc(ws_in, 16)
                sp.dma_start(w2_raw[e], w2[e]).then_inc(ws_in, 16)

            def load(n, u):
                if live(n, 0, B):
                    reused(sp, q_rdy, n, 4, per=3)
                    sp.dma_start(tokens(X, n), x[bass.ds(n, 1)].rearrange("o (t p) c -> p (o t) c", p=P)).then_inc(x_in[u], 16)
                m = n - L_ADJ
                if live(n, L_ADJ, B):
                    v = (u - L_ADJ) % 4
                    reused(sp, at_ps, m, 4)
                    sp.dma_start(AJ[:, v], adj[bass.ds(m, 1)].rearrange("o (t p) j -> p (o t) j", p=P)).then_inc(adj_in[v], 16)
                if isinstance(n, int) and n in range(4, 4 + 2 * E, 2):
                    load_raw(n // 2 - 2)
                m = n - L_STORE
                if live(n, L_STORE, B):
                    v = (u - L_STORE) % 4
                    sp.wait_ge(at_sb, m + 1)
                    sp.dma_start(adjT_dram[bass.ds(m, 1)].rearrange("o p f -> p (o f)"), AT[:, v].rearrange("p t i -> p (t i)")).then_inc(at_out[v], 16)
                if live(n, 0, B):
                    if isinstance(n, int) and n == 1:
                        sp.dma_start(Wr_sb[:], Wr).then_inc(s_cst, 16)
                        for i, w in enumerate((theta, W_h, W_t)):
                            sp.dma_start(Wc[:, i], w).then_inc(s_wc, 16)
                        sp.dma_start(bt_row[:], b_t.rearrange("(a c) -> a c", a=1)).then_inc(s_wc, 16)
                        sp.dma_start(br_b[:], br.rearrange("(a c) -> a c", a=1).to_broadcast([P, E])).then_inc(s_cst, 16)
                        sp.dma_start(b2_sb[:], b2).then_inc(s_cst, 16)
                        sp.dma_start(fgam[:], f_gamma.rearrange("(a c) -> a c", a=1).to_broadcast([P, D])).then_inc(s_cst, 16)
                        sp.dma_start(fbet[:], f_beta.rearrange("(a c) -> a c", a=1).to_broadcast([P, D])).then_inc(s_cst, 16)
                    if isinstance(n, int) and n == 0:
                        sp.dma_start(Wg[:, 0], W_rel).then_inc(s_wg, 16)
                        sp.dma_start(Wg[:, 1], W_root).then_inc(s_wg, 16)
                        sp.dma_start(brel[:], b_rel.rearrange("(a c) -> a c", a=1).to_broadcast([P, D])).then_inc(s_wg, 16)
            pipeline(sp, B, L_STORE, load, peel=20)
            sp.wait_ge(wp_ps, 3 * per_big)
            sp.wait_ge(r_eidx, 1)

            def load_experts(n, u):
                if live(n, 0, B):
                    reused(sp, f_y, n, 4)
                    for k in range(K):
                        e = sp.value_load(eidx[0:1, bass.ds(n, 1), k:k + 1].rearrange("p b k -> p (b k)"), min_val=0, max_val=E - 1)
                        sp.dma_start(W1b[:, u, k], W1[bass.ds(e, 1)].rearrange("o d f -> d (o f)")).then_inc(w_in[u], 16)
                        sp.dma_start(W2b[:, u, k], W2[bass.ds(e, 1)].rearrange("o (c p) d -> p (o c) d", p=P)).then_inc(w_in[u], 16)
            pipeline(sp, B, 0, load_experts)
            for u in range(4):
                sp.wait_ge(at_out[u], 16 * (B // 4))

            def load_adjT(n, u):
                if isinstance(n, int) and n == 4:
                    sp.wait_ge(pad_out, 4)
                if isinstance(n, int) and n >= 4:
                    part = slots_dram[(n - 4) * (NG // 8) * P:(n - 3) * (NG // 8) * P]
                    sp.dma_start(part.rearrange("(g p) c -> p g c", p=P), pad_row[:].unsqueeze(1).to_broadcast([P, NG // 8, ROW])).then_inc(d_pad, 16)
                reused(sp, c_hom, n, 4)
                sp.dma_start(AT[:, u].rearrange("p t i -> p (t i)"), adjT_dram[bass.ds(n, 1)].rearrange("o p f -> p (o f)")).then_inc(at_in[u], 16)
            pipeline(sp, B, 0, load_adjT)

            for u in range(4):
                sp.wait_ge(d_sc[u], 16 * K * (NTB // 4))

            def load_slots(n, u):
                reused(sp, e_gate, n, 4, per=2)
                reused(sp, e_xt, n, 4)
                sp.dma_start(XS[:, u], slots_dram[bass.ds(n * P, P)]).then_inc(e_in[u], 16)
            pipeline(sp, NGB, 0, load_slots, peel=4)
            for i in range(2):
                sp.wait_ge(d_sc[i], 16 * K * (NTB // 4 + NTB // 2))
            for_more(sp, NGB, GIVEN, load_slots)
            for u in range(4):
                sp.wait_ge(e_sc[u], 16 * (NGB // 4))

            def store_sum(j):
                sp.wait_ge(z_b, j * 2 + 2)
                sp.dma_start(out[bass.ds(j, 1)].rearrange("b (t p) c -> p (b t) c", p=P), z_sum.rearrange("p (t c) -> p t c", c=D)).then_inc(z_out, 16)

            def load_slots_and_y(n, u):
                load_slots(n, u)
                if u == 1:
                    j = (n - 1 - GIVEN) // 4
                    if not isinstance(n, int):
                        store_sum(j - 1)
                    for k, ybuf in enumerate((z_y1, z_y2)):
                        sp.dma_start(ybuf.rearrange("p (t c) -> p t c", c=D), y_dram[bass.ds(j * T * P + k * NT * P, T * P)].rearrange("(t p) c -> p t c", p=P)).then_inc(z_in, 16)
            for u in range(UNROLL):
                load_slots_and_y(GIVEN + u, u)
            for_more(sp, GIVEN + 4, NG, load_slots_and_y)
            store_sum(NTB // 2 - 1)

            for u in range(4):
                sp.wait_ge(e_sc[u], 16 * (NG // 4))
            sp.wait_ge(z_out, 16 * (NTB // 2))

            def load_y(n, u):
                if live(n, 0, NTB // 4):
                    if not isinstance(n, int) or n >= 4:
                        sp.wait_ge(o_out[u], (n - u) * 4)
                    sp.dma_start(ya[:, u].rearrange("p (t c) -> p t c", c=D), y_dram[bass.ds(n * 4 * P + NTB * P, 4 * P)].rearrange("(t p) c -> p t c", p=P)).then_inc(o_in[u], 16)
                    sp.dma_start(ybb[:, u].rearrange("p (t c) -> p t c", c=D), y_dram[bass.ds(n * 4 * P + (NTB + NT) * P, 4 * P)].rearrange("(t p) c -> p t c", p=P)).then_inc(o_in[u], 16)
            pipeline(sp, NTB // 4, 0, load_y, peel=4)

        @block.gpsimd
        def _(gp):
            gp.memset(ident[:], 0.0).then_inc(s_ones, 1)
            gp.memset(half[:], -0.5).then_inc(s_ones, 1)
            gp.memset(hrel[:, :, :, D:D + 1], 1.0).then_inc(s_ones, 1)
            gp.memset(ones[:], 1.0).then_inc(s_ones, 1)
            gp.memset(one_S[:], 1.0 / S).then_inc(s_ones, 1)
            gp.iota(rank_e[:], pattern=[[-1, E]], base=E, channel_multiplier=0, allow_small_or_imprecise_dtypes=True).then_inc(s_ones, 1)
            gp.wait_ge(s_ones, 6)
            gp.memset(pad_row[:], 0.0).then_inc(pad_out, 1)
            gp.wait_ge(pad_out, 1)
            gp.memset(pad_row[:, D + 2:D + 3], -1.0).then_inc(pad_out, 1)
            gp.memset(pad_row[:, D + 3:D + 4], NOWHERE).then_inc(pad_out, 1)
            gp.memset(padd[:], 0.0).then_inc(pad_out, 1)
            gp.iota(gidx[:], pattern=[[1, NGB]], base=0, channel_multiplier=0, allow_small_or_imprecise_dtypes=True).then_inc(pad_out, 1)
            gp.iota(tok_id[:], pattern=[[P, NT]], base=0, channel_multiplier=1, allow_small_or_imprecise_dtypes=True).then_inc(pad_out, 1)
            gp.affine_select(out=tri[:], in_=ones[:], compare_op=ALU.is_gt, fill=0.0, base=0,
                             pattern=[[1, P]], channel_multiplier=-1).then_inc(pad_out, 1)
            gp.affine_select(out=ident[:], in_=ident[:], compare_op=ALU.not_equal, fill=1.0, base=0,
                             pattern=[[-1, P]], channel_multiplier=1).then_inc(s_id, 1)

            def step(n, u):
                if live(n, 0, B):
                    gp.wait_ge(q_rdy, (n + 1) * 3)
                    gp.tensor_tensor(q[:, u], q[:, u], half[:, 0:4].rearrange("p (a t) -> p a t", a=2), ALU.pow).then_inc(pow0, 1)
                    reused(gp, xx_rdy, n, 4)
                    gp.wait_ge(pow0, n + 1)
                    gp.tensor_tensor(ab[:, u, 0], q[:, u, 0], ones[:, 0:T], ALU.add)
                    gp.tensor_tensor(ab[:, u, 1], q[:, u, 0], nm[:, u], ALU.mult).then_inc(ab_a, 1)
                m = n - L_X1
                if live(n, L_X1, B):
                    gp.wait_ge(q1_rdy, (m + 1) * 2)
                    gp.tensor_tensor(rstd1[:, bass.ds(m * T, T)], q1[:, (u - L_X1) % 2], half[:, 0:T], ALU.pow).then_inc(pow1, 1)
                    gp.wait_ge(pow1, m + 1)
                    gp.tensor_tensor(bias1[:, bass.ds(m * T, T)], rstd1[:, bass.ds(m * T, T)], nm1[:, (u - L_X1) % 2], ALU.mult).then_inc(nb1, 1)
            pipeline(gp, B, LAG1, step)
            gp.wait_ge(c_deg, 1)
            gp.tensor_tensor(norm[:], norm[:], half[:], ALU.pow).then_inc(c_norm, 1)
            gp.wait_ge(r_b2w, 1)
            gp.dma_start(b2w_dram, b2w[:]).then_inc(r_b2d, 16)
            gp.wait_ge(r_b2d, 16)
            gp.wait_ge(wp_ps, E)
            for first, end in ((0, 4), (4, B)):
                gp.dma_start(b2b[:, first:end].rearrange("p b c -> p (b c)"), b2w_dram[first:end].rearrange("b c -> (b c)").unsqueeze(0).to_broadcast([P, (end - first) * D])).then_inc(r_b2b[first // 4], 16)
            gp.wait_ge(s_cst, 80)
            gp.wait_ge(r_b2b[0], 16)

            def ffn0(n, u):
                if live(n, 0, B):
                    if isinstance(n, int) and n == 4:
                        gp.wait_ge(r_b2b[1], 16)
                    gp.wait_ge(f_xn, n + 1)
                    gp.tensor_tensor(xb[:, u], xb[:, u], b2b[:, bass.ds(n, 1), :].to_broadcast([P, T, D]), ALU.add).then_inc(f_xb, 1)
                m = n - L_SUM
                if live(n, L_SUM, B):
                    reused(gp, x2_rdy, m, 4)
                    gp.tensor_tensor(xbeta[:, (u - L_SUM) % 4], tokens(X, m), fbet[:].unsqueeze(1).to_broadcast([P, T, D]), ALU.add).then_inc(f_xbeta, 1)
                    gp.wait_ge(f_q, (m + 1) * 2)
                    v = (u - L_SUM) % 4
                    gp.tensor_tensor(q[:, v, 0], q[:, v, 0], half[:, 0:T], ALU.pow).then_inc(f_pow, 1)
                    gp.wait_ge(f_pow, m + 1)
                    gp.tensor_tensor(nb[:, v], q[:, v, 0], nm[:, v], ALU.mult).then_inc(f_nb, 1)
            pipeline(gp, B, 0, ffn0)

            def held(done, value, before):
                if not isinstance(before, int) or before > 0:
                    gp.wait_ge(p_held, before)
                gp.wait_ge(done, value)
                gp.tensor_tensor(padd[:, 0:1], padd[:, 1:2], padd[:, 1:2], ALU.add).then_inc(p_held, 1)

            def dispatch(j, v, before=None):
                if before is None:
                    gp.wait_ge(d_row, j + 1)
                else:
                    held(d_row, j + 1, before)
                for k in range(K):
                    gp.indirect_dma_start(slots_dram, bass.IndirectOffsetOnAxis(ap=dispatch_i[:, v, k:k + 1].bitcast(mybir.dt.uint32), axis=0),
                                          XR[:, v], None).then_inc(d_sc[v], 16)

            def gnn1(n, u):
                if live(n, 0, B):
                    gp.wait_ge(c_q, (n + 1) * 2)
                    gp.tensor_tensor(qc[:, u, 0], qc[:, u, 0], half[:, 0:T], ALU.pow).then_inc(c_pow, 1)
                    reused(gp, c_z, n, 4)
                    gp.wait_ge(c_pow, n + 1)
                    gp.tensor_tensor(nbc[:, u], qc[:, u, 0], nmc[:, u], ALU.mult).then_inc(c_nb, 1)
                m = n - M_X3
                if live(n, M_X3, B):
                    gp.wait_ge(c_q3, (m + 1) * 2)
                    gp.tensor_tensor(rstd3[:, bass.ds(m * T, T)], q1[:, (u - M_X3) % 2], half[:, 0:T], ALU.pow).then_inc(c_pow3, 1)
                    gp.wait_ge(c_pow3, m + 1)
                    gp.tensor_tensor(bias3[:, bass.ds(m * T, T)], rstd3[:, bass.ds(m * T, T)], nm1[:, (u - M_X3) % 2], ALU.mult).then_inc(c_nb3, 1)
            for k in range(LAG3):
                ffn0(B + k, k % UNROLL)
                gnn1(k, k % UNROLL)
            pipeline(gp, ROUTE, 0, gnn1, peel=16, start=LAG3)
            gp.wait_ge(d_pad, 8 * 16)
            for n in range(ROUTE, B + LAG4):
                gnn1(n, n % UNROLL)
                for j in tiles_beside(n):
                    dispatch(j, j % 4)

            def give(n, u, before):
                m = n - N_SC
                if live(n, N_SC, NG):
                    v = (u - N_SC) % 4
                    gp.wait_ge(e_dest, m + 1)
                    held(e_ys, m + 1, before)
                    gp.indirect_dma_start(y_dram, bass.IndirectOffsetOnAxis(ap=scatter_i[:, v:v + 1].bitcast(mybir.dt.uint32), axis=0),
                                          YS[:, v], None, bounds_check=K * NT * P - 1, oob_is_err=False).then_inc(e_sc[v], 16)

            def give_and_dispatch(n, u):
                given = max(n - N_SC, 0) if isinstance(n, int) else n - N_SC
                sent = (n + 1) // 2 if isinstance(n, int) else (n - u) // 2 + (u + 1) // 2
                give(n, u, given + sent)
                if u % 2 == 0:
                    if isinstance(n, int):
                        dispatch(NTB + n // 2, u // 2, max(n - N_SC + 1, 0) + sent)
                    else:
                        dispatch((n - u) // 2 + (NTB + u // 2), u // 2, given + sent + 1)
            pipeline(gp, NG, N_SC, give_and_dispatch, until=2 * NTB, later=lambda n, u: give(n, u, n - N_SC + NTB))

        @block.scalar
        def _(act):
            act.wait_ge(s_colp, 1)
            act.activation(cols[:], ps_z[0][:, 0:NROW], ACT.Copy).then_inc(s_col, 1)
            act.wait_ge(s_col, 1)

            def step(n, u):
                m = n - L_XPT
                if live(n, L_XPT, B):
                    act.wait_ge(xp_ps, m + 1)
                    act.activation(X0T[:, bass.ds(m * S, S)], ps_xp[:, 0:S], ACT.Identity, accum_out=tok_sum[:, bass.ds(m, 1)]).then_inc(xp_sb, 1)
                m = n - L_XP
                if live(n, L_XP, B):
                    v = (u - L_XP) % 4
                    act.wait_ge(nb1, m + 1)
                    reused(act, xp_ps, m, 2)
                    for t in range(T):
                        last = act.activation(xp[:, v % 2, t], tile(X, m * T + t), ACT.Identity, scale=rstd1[:, bass.ds(m * T + t, 1)], bias=bias1[:, bass.ds(m * T + t, 1)])
                    last.then_inc(xp_rdy, 1)
                m = n - L_HT
                if live(n, L_HT, B):
                    v = (u - L_HT) % 4
                    act.wait_ge(z_ps, m + 1)
                    reused(act, cv_ps, m, 4)
                    act.activation(hT[:, v], ps_z[v % 2][:, 0:S], ACT.Identity, scale=cols[:, 0:1], bias=cols[:, 1:2]).then_inc(hT_rdy, 1)
                m = n - L_XX
                if live(n, L_XX, B):
                    v = (u - L_XX) % 4
                    act.wait_ge(ab_a, m + 1)
                    reused(act, x1_rdy, m, 4)
                    for t in range(T):
                        last = act.activation(xx[:, v, t], tile(X, m * T + t), ACT.Identity, scale=ab[:, v, 0, t:t + 1], bias=ab[:, v, 1, t:t + 1])
                    last.then_inc(xx_rdy, 1)
                m = n - L_AT
                if live(n, L_AT, B):
                    v = (u - L_AT) % 4
                    act.wait_ge(at_ps, m + 1)
                    reused(act, cv_ps, m, 4)
                    if not isinstance(m, int) or m >= 4:
                        act.wait_ge(at_out[v], (m - v) * 4)
                    act.activation(AT[:, v], ps_at[v % 2][:].rearrange("p (t i) -> p t i", t=T), ACT.Copy).then_inc(at_sb, 1)
                m = n - L_HREL
                if live(n, L_HREL, B):
                    v = (u - L_HREL) % 4
                    act.wait_ge(hr_ps, m + 1)
                    reused(act, cv_ps, m, 2)
                    act.activation(hrel[:, v % 2, :, 0:D], ps_hr[:, 0:S].rearrange("p (t c) -> p t c", t=T), ACT.Copy).then_inc(hr_rdy, 1)
            pipeline(act, B, LAG1, step)
            act.wait_ge(r_sub, 1)
            act.activation(rt[2], rt[1], ACT.Exp).then_inc(r_exp, 1)
            act.wait_ge(r_sub, 2)
            act.activation(rt[2], rt[1], ACT.Exp).then_inc(r_exp, 1)
            def turned_out(e):
                act.wait_ge(wp_ps, e + 1)
                p1, p3, p2 = ps[2 + e % 2 * 3:5 + e % 2 * 3]
                act.activation(w1T[:, e], p1[:, 0:H], ACT.Copy)
                act.activation(w3T[:, e], p3[:, 0:H], ACT.Copy)
                act.activation(w2T[:, e, 0:HC - 1], p2[:, 0:(HC - 1) * D].rearrange("p (c d) -> p c d", d=D), ACT.Copy)
                act.activation(w2T[0:HL, e, HC - 1], p2[0:HL, (HC - 1) * D:HC * D], ACT.Copy).then_inc(wp_sb, 1)
            for e in range(E // 2 + 1):
                turned_out(e)
            act.wait_ge(r_sub, 3)
            act.activation(rv[5][:], rv[4][:], ACT.Exp).then_inc(r_exp, 1)
            for e in range(E // 2 + 1, E):
                turned_out(e)
            act.wait_ge(r_b2, 1)
            act.activation(b2w[:], ps[1][0:B, 0:D], ACT.Copy).then_inc(r_b2w, 1)
            act.wait_ge(r_done, 1)

            def ffn0(n, u):
                m = n - L_N
                if live(n, L_N, B):
                    v = (u - L_N) % 4
                    act.wait_ge(f_nb, m + 1)
                    for t in range(T):
                        last = act.activation(yb[:, v, t], yb[:, v, t], ACT.Identity, scale=q[:, v, 0, t:t + 1], bias=nb[:, v, t:t + 1])
                    last.then_inc(f_n, 1)
                if live(n, 0, B):
                    reused(act, f_sum, n, 4, per=2)
                    for t in range(T):
                        last = act.activation(xb[:, u, t], tile(X, n * T + t), ACT.Identity, scale=rstd1[:, bass.ds(n * T + t, 1)], bias=bias1[:, bass.ds(n * T + t, 1)])
                    last.then_inc(f_xn, 1)
                    reused(act, f_y, n, 2)
                    for k in range(K):
                        act.wait_ge(f_h, n * K + k + 1)
                        for c in range(FC):
                            act.activation(gT[:, u % 2, k, c], ps[(u % 2) * K + k][:, c * S:(c + 1) * S], ACT.Gelu,
                                           bias=b1s[:, bass.ds(n, 1), k, c:c + 1].rearrange("p b c -> p (b c)")).then_inc(f_g, 1)
            pipeline(act, B, 0, ffn0)

            def rows_out(j, v, turns):
                if not isinstance(turns, int) or turns > 0:
                    act.wait_ge(d_sc[v], turns * (16 * K))
                one = bass.ds(j, 1)
                act.activation(XR[:, v, 0:D], tile(X, j), ACT.Identity, scale=rstd3[:, one], bias=bias3[:, one])
                act.activation(XR[:, v, D:ROW], pay[:, one].rearrange("p o c -> p (o c)"), ACT.Copy)
                act.activation(dispatch_i[:, v], slot[:, one].rearrange("p o k -> p (o k)"), ACT.Copy).then_inc(d_row, 1)

            def route_exp(b):
                of_block = slice(b * NTB, (b + 1) * NTB)
                act.wait_ge(q_sub, b + 1)
                act.activation(R_all[1][:, of_block], R_all[0][:, of_block], ACT.Exp).then_inc(q_exp, 1)

            def gnn1(n, u):
                m = n - M_X3
                if live(n, M_X3, B):
                    act.wait_ge(c_mn, m + 1)
                    reused(act, x3_rdy, m, 2)
                    act.activation(ee[:, (u - M_X3) % 2], mn[:, (u - M_X3) % 2], ACT.Exp).then_inc(c_exp, 1)
                m = n - M_PR
                if live(n, M_PR, B):
                    v = (u - M_PR) % 4
                    pp = PS[:, 2 + 2 * (v % 2):4 + 2 * (v % 2)]
                    act.wait_ge(c_p, m + 1)
                    reused(act, c_hom, m, 2)
                    reused(act, c_o, m, 4, per=3)
                    for t in range(T):
                        last = act.activation(hrel[:, v % 2, t, 0:D], pp[:, t, 0:D], ACT.Copy, scale=norm[:, bass.ds(m * T + t, 1)])
                    last.then_inc(c_f1, 1)
                    act.activation(het[:, v], pp[:, :, D:2 * D], ACT.Copy)
                    act.activation(th[:, v], pp[:, :, 2 * D:3 * D], ACT.Tanh, scale=0.5).then_inc(c_pr, 1)
                m = n - M_Z3
                if live(n, M_Z3, B):
                    v = (u - M_Z3) % 4
                    act.wait_ge(c_nb3, m + 1)
                    if not isinstance(m, int) or m >= 2:
                        act.wait_ge(c_zt, m - 2 + M_Z3T - M_ZT + 1)
                    for t in range(T):
                        last = act.activation(x0[:, v % 2, t], tile(X, m * T + t), ACT.Identity, scale=rstd3[:, bass.ds(m * T + t, 1)], bias=bias3[:, bass.ds(m * T + t, 1)])
                    last.then_inc(c_z3, 1)
                m = n - M_Z
                if live(n, M_Z, B):
                    v = (u - M_Z) % 4
                    act.wait_ge(c_nb, m + 1)
                    reused(act, c_zt, m, 2)
                    for t in range(T):
                        last = act.activation(z[:, v % 2, t], tile(X, m * T + t), ACT.Identity, scale=qc[:, v, 0, t:t + 1], bias=nbc[:, v, t:t + 1])
                    last.then_inc(c_z, 1)
                first, second = live(n, M_ZT, B), live(n, M_Z3T, B)
                if first or second:
                    act.wait_ge(c_zt, n - M_ZT + 1)
                    if first and (not isinstance(n, int) or n > M_P):
                        act.wait_ge(c_p, n - M_P)
                    if second and (not isinstance(n, int) or n > M_LG):
                        act.wait_ge(c_lgp, n - M_LG)
                    part = slice(0 if first else S, 2 * S if second else S)
                    act.activation(turned[:, u % 2, part], ps[0][:, part], ACT.Copy).then_inc(c_xT, 1)

            for k in range(LAG3):
                ffn0(B + k, k % UNROLL)
                if k == 1:
                    act.wait_ge(f_y, B)
                    act.wait_ge(c_norm, 1)
                gnn1(k, k % UNROLL)
            pipeline(act, ROUTE, 0, gnn1, peel=16, start=LAG3)
            route_exp(0)
            act.wait_ge(q_done, 1)
            for n in range(ROUTE, B + LAG4):
                gnn1(n, n % UNROLL)
                if n == B + M_Z3T:
                    route_exp(1)
                for j in tiles_beside(n):
                    rows_out(j, j % 4, j // 4)
            act.wait_ge(q_done, 2)

            def ffn1(n, u):
                m = n - N_MUL
                if live(n, N_MUL, NG):
                    v = (u - N_MUL) % 4
                    act.wait_ge(e_h, m + 1)
                    reused(act, e_hh, m, 2)
                    act.activation(sg[:, v % 2], ps[1 + v % 2][:, 0:H], ACT.Silu).then_inc(e_silu, 1)
                m = n - N_Y
                if live(n, N_Y, NG):
                    v = (u - N_Y) % 4
                    act.wait_ge(e_y, m + 1)
                    act.wait_ge(e_gate, (m + 1) * 2)
                    if not isinstance(m, int) or m >= 4:
                        act.wait_ge(e_sc[v], (m - v) * 4)
                    act.activation(YS[:, v], ps[6 + v % 2][:, 0:D], ACT.Copy, scale=gate[:, bass.ds(m, 1)]).then_inc(e_ys, 1)
                m = n - N_HT
                if live(n, N_HT, NG):
                    v = (u - N_HT) % 4
                    act.wait_ge(e_ht, m + 1)
                    reused(act, e_y, m, 2)
                    act.activation(hhT[:, v % 2].rearrange("p c s -> p (c s)"), ps[5][:, 0:HC * P], ACT.Copy).then_inc(e_hT, 1)

            def ffn1_and_rows(n, u):
                ffn1(n, u)
                if u % 2 == 0:
                    rows_out(NTB + n // 2 if isinstance(n, int) else (n - u) // 2 + (NTB + u // 2), u // 2,
                             NTB // 4 + (n // 4 if isinstance(n, int) else (n - u) // 4))
            pipeline(act, GIVEN, 0, ffn1_and_rows, until=2 * NTB, later=ffn1)

            for_more(act, GIVEN, NG, ffn1)
            for n in range(NG, NG + N_SC):
                ffn1(n, n % UNROLL)

            def store(n, u):
                act.wait_ge(o_b, n * 2 + 2)
                act.dma_start(out[bass.ds(n * 2 + B // BLOCKS, 2)].rearrange("b (t p) c -> p (b t) c", p=P), ya[:, u].rearrange("p (t c) -> p t c", c=D)).then_inc(o_out[u], 16)
            pipeline(act, NTB // 4, 0, store, peel=4)
            for u in range(4):
                act.wait_ge(o_out[u], 16 * (NTB // 16))
            act.wait_ge(z_out, 16 * (NTB // 2))

        @block.vector
        def _(dve):
            def held(done, value):
                dve.wait_ge(done, value)
                dve.memset(hold[:], 0.0)

            dve.wait_ge(s_ones, 6)
            dve.wait_ge(s_wg, 48)

            def var_of(v):
                return v[:, :, 1:2].rearrange("p t o -> p (t o)")

            def mean_of(v):
                return v[:, :, 0:1].rearrange("p t o -> p (t o)")

            def step(n, u):
                m = n - L_X1
                new, old = live(n, 0, B), live(n, L_X1, B)
                v = (u - L_X1) % 4
                pc = ps_cv[v % 2].rearrange("p (t c) -> p t c", t=T)
                if old:
                    dve.wait_ge(cv_ps, m + 1)
                    dve.tensor_tensor(cv[:, v % 2], pc[:, :, 0:D], brel[:].unsqueeze(1).to_broadcast([P, T, D]), ALU.add).then_inc(cv_bias, 1)
                if new:
                    held(x_in[u], (n - u) * 4 + 16)
                    for t in range(T):
                        dve.bn_stats(st[:, u % 2, t], tile(X, n * T + t)).then_inc(stat, 1)
                if old:
                    dve.wait_ge(cv_bias, m + 1)
                    dve.wait_ge(xx_rdy, m + 1)
                    dve.scalar_tensor_tensor(tokens(X, m), cv[:, v % 2], 0.0, xx[:, v], ALU.max, ALU.add).then_inc(x1_rdy, 1)
                if new:
                    held(stat, n * 2 * T + T)
                    for t in range(T):
                        dve.bn_aggr(mv[:, u, t], st[:, u % 2, t]).then_inc(stat, 1)
                if old:
                    dve.wait_ge(x1_rdy, m + 1)
                    dve.tensor_scalar(deg[:, bass.ds(m * T, T)], pc[:, :, D:D + 1].rearrange("p t o -> p (t o)"), 1.0, None, ALU.mult).then_inc(cv_read, 1)
                    for t in range(T):
                        dve.bn_stats(st1[:, v % 2, t], tile(X, m * T + t)).then_inc(stat1, 1)
                if new:
                    reused(dve, ab_a, n, 4)
                    dve.wait_ge(stat, (n + 1) * 2 * T)
                    dve.tensor_scalar(nm[:, u], mean_of(mv[:, u]), -1.0, None, ALU.mult).then_inc(q_rdy, 1)
                    dve.tensor_scalar(q[:, u, 0], var_of(mv[:, u]), LN_EPS, None, ALU.add).then_inc(q_rdy, 1)
                    dve.tensor_scalar(q[:, u, 1], var_of(mv[:, u]), 1.0 + LN_EPS, LN_EPS * LN_EPS, ALU.mult, ALU.add).then_inc(q_rdy, 1)
                if old:
                    held(stat1, m * 2 * T + T)
                    for t in range(T):
                        dve.bn_aggr(mv1[:, v % 2, t], st1[:, v % 2, t]).then_inc(stat1, 1)
                k = n - L_Z
                if live(n, L_Z, B):
                    w = (u - L_Z) % 4
                    dve.wait_ge(pow0, k + 1)
                    reused(dve, z_ps, k, 2)
                    for t in range(T):
                        last = dve.tensor_scalar(z[:, w % 2, t], tile(X, k * T + t), mv[:, w, t, 0:1], q[:, w, 1, t:t + 1], ALU.subtract, ALU.mult)
                    last.then_inc(z_rdy, 1)
                if old:
                    reused(dve, nb1, m, 2)
                    dve.wait_ge(stat1, (m + 1) * 2 * T)
                    dve.tensor_scalar(nm1[:, v % 2], mean_of(mv1[:, v % 2]), -1.0, None, ALU.mult).then_inc(q1_rdy, 1)
                    dve.tensor_scalar(q1[:, v % 2], var_of(mv1[:, v % 2]), LN_EPS, None, ALU.add).then_inc(q1_rdy, 1)
            pipeline(dve, B, LAG1, step)

            dve.wait_ge(cv_read, B)
            dve.tensor_scalar(norm[:], deg[:], DEG_EPS, None, ALU.add).then_inc(c_deg, 1)

            links = [0]

            def link(ins):
                links[0] += 1
                ins.then_inc(rlink, 1)
                dve.wait_ge(rlink, links[0])

            def over_e(v):
                return v.unsqueeze(2).to_broadcast([P, B, E])

            def over_b(v):
                return v.unsqueeze(1).to_broadcast([P, B, E])

            dve.wait_ge(s_cst, 80)
            dve.wait_ge(xp_sb, B)
            dve.tensor_tensor(rt[0], over_e(tok_sum[:]), over_b(Wr_sb[:]), ALU.mult).then_inc(r_g, 1)
            dve.wait_ge(r_lg, 1)
            lg = ps[0][:, 0:B * E].rearrange("p (b e) -> p b e", e=E)
            link(dve.tensor_tensor(rt[0], lg, over_b(br_b[:]), ALU.add))

            def softmax(src, dst, nth):
                link(dve.tensor_reduce(rv[0][:], src, AX.X, ALU.max))
                dve.tensor_tensor(rt[1], src, over_e(rv[0][:]), ALU.subtract).then_inc(r_sub, 1)
                dve.wait_ge(r_exp, nth)
                link(dve.tensor_reduce(rv[0][:], rt[2], AX.X, ALU.add))
                link(dve.reciprocal(rv[1][:], rv[0][:]))
                link(dve.tensor_tensor(dst, rt[2], over_e(rv[1][:]), ALU.mult))

            softmax(rt[0], rt[3], 1)
            link(dve.tensor_reduce(r8[0][:], rt[3].rearrange("p b e -> p e b"), AX.X, ALU.add))
            link(dve.tensor_scalar(r8[1][:], r8[0][:], float(S), None, ALU.mult))
            link(dve.reciprocal(r8[0][:], r8[1][:]))
            link(dve.tensor_scalar(r8[2][:], r8[0][:], CAPACITY, 1.0, ALU.mult, ALU.min))
            link(dve.tensor_tensor(rt[0], rt[3], over_b(r8[2][:]), ALU.mult))
            softmax(rt[0], rt[3], 2)

            def first_max(w, top, key, hot):
                link(dve.tensor_reduce(top, w, AX.X, ALU.max))
                link(dve.tensor_tensor(key, w, over_e(top), ALU.is_equal))
                link(dve.tensor_tensor(key, key, over_b(rank_e[:]), ALU.mult))
                link(dve.tensor_reduce(rv[7][:], key, AX.X, ALU.max))
                link(dve.tensor_tensor(hot, key, over_e(rv[7][:]), ALU.is_equal))

            for k in range(K):
                first_max(rt[3], rv[2 + k][:], rt[4], oh[:, :, k])
                link(dve.tensor_scalar(rv[6][:], rv[7][:], -1.0, float(E), ALU.mult, ALU.add))
                link(dve.tensor_copy(eidx[:, :, k:k + 1].rearrange("p b k -> p (b k)"), rv[6][:]))
                if k == 0:
                    link(dve.scalar_tensor_tensor(rt[3], oh[:, :, k], -2.0, rt[3], ALU.mult, ALU.add))
            dve.tensor_tensor(rv[4][:], rv[3][:], rv[2][:], ALU.subtract).then_inc(r_sub, 1)
            dve.sem_inc(r_eidx, 1)
            dve.wait_ge(r_exp, 3)
            link(dve.tensor_scalar(rv[6][:], rv[5][:], 1.0, None, ALU.add))
            link(dve.reciprocal(rv[7][:], rv[6][:]))
            w_of = [wk[:, :, k:k + 1].rearrange("p b k -> p (b k)") for k in range(K)]
            link(dve.tensor_copy(w_of[0], rv[7][:]))
            link(dve.tensor_tensor(w_of[1], rv[5][:], rv[7][:], ALU.mult))
            link(dve.tensor_tensor(rt[4], oh[:, :, 0], over_e(w_of[0]), ALU.mult))
            link(dve.tensor_tensor(rt[5], oh[:, :, 1], over_e(w_of[1]), ALU.mult))
            link(dve.tensor_tensor(rt[4], rt[4], rt[5], ALU.add))
            link(dve.tensor_tensor(rt[5][0:E], rt[4][0:E], ident[0:E, 0:E].unsqueeze(1).to_broadcast([E, B, E]), ALU.mult))
            dve.tensor_reduce(wd8[:], rt[5][0:E], AX.X, ALU.add).then_inc(r_wd8, 1)
            b1c = cols[:, 2:18].rearrange("p (e c) -> p c e", c=FC)
            for k in range(K):
                for c in range(FC):
                    link(dve.tensor_tensor(rt[6], oh[:, :, k], over_b(b1c[:, c]), ALU.mult))
                    link(dve.tensor_reduce(b1s[:, :, k, c:c + 1].rearrange("p b c -> p (b c)"), rt[6], AX.X, ALU.add))
            dve.memset(hold[:], 0.0).then_inc(r_done, 1)

            def ffn0(n, u):
                m, k = n - L_SUM, n - L_X2
                new, old = live(n, L_SUM, B), live(n, L_X2, B)
                v, w = (u - L_SUM) % 4, (u - L_X2) % 4
                py = ps[4 + v % 2].rearrange("p (k t c) -> p k t c", k=K, t=T)
                if new:
                    dve.wait_ge(f_xb, m + 1)
                    dve.wait_ge(f_y, m + 1)
                    dve.scalar_tensor_tensor(yb[:, v], py[:, 0], wk[:, bass.ds(m, 1), 0:1].rearrange("p b k -> p (b k)"), xb[:, v], ALU.mult, ALU.add).then_inc(f_sum, 1)
                if old:
                    dve.wait_ge(f_n, k + 1)
                    dve.tensor_tensor(yb[:, w], yb[:, w], fgam[:].unsqueeze(1).to_broadcast([P, T, D]), ALU.mult).then_inc(f_gm, 1)
                if new:
                    dve.wait_ge(f_sum, m * 2 + 1)
                    dve.scalar_tensor_tensor(yb[:, v], py[:, 1], wk[:, bass.ds(m, 1), 1:2].rearrange("p b k -> p (b k)"), yb[:, v], ALU.mult, ALU.add).then_inc(f_sum, 1)
                if old:
                    dve.wait_ge(f_gm, k + 1)
                    dve.wait_ge(f_xbeta, k + 1)
                    dve.tensor_tensor(tokens(X, k), yb[:, w], xbeta[:, w], ALU.add).then_inc(x2_rdy, 1)
                if new:
                    held(f_sum, m * 2 + 2)
                    for t in range(T):
                        dve.bn_stats(st[:, v % 2, t], yb[:, v, t]).then_inc(f_st, 1)
                    held(f_st, m * 2 * T + T)
                    for t in range(T):
                        dve.bn_aggr(mv[:, v, t], st[:, v % 2, t]).then_inc(f_st, 1)
                    dve.wait_ge(f_st, (m + 1) * 2 * T)
                    dve.tensor_scalar(nm[:, v], mean_of(mv[:, v]), -1.0, None, ALU.mult).then_inc(f_q, 1)
                    dve.tensor_scalar(q[:, v, 0], var_of(mv[:, v]), LN_EPS, None, ALU.add).then_inc(f_q, 1)
            pipeline(dve, B, 0, ffn0)

            qlinks = [0]

            def qlink_(ins):
                qlinks[0] += 1
                ins.then_inc(qlink, 1)
                dve.wait_ge(qlink, qlinks[0])

            def oe(v, n=NTB):
                return v.unsqueeze(2).to_broadcast([P, n, E])

            def ot(v, n=NTB):
                return v.unsqueeze(1).to_broadcast([P, n, E])

            def route(b):
                def blk(t):
                    return t[:, b * NTB:(b + 1) * NTB]

                R = [blk(r) for r in R_all]
                v_ = [blk(v) for v in v_all]
                dve.wait_ge(c_lg, (b + 1) * B // BLOCKS)
                qlink_(dve.tensor_reduce(v_[0], blk(lgt), AX.X, ALU.max))
                dve.tensor_tensor(R[0], blk(lgt), oe(v_[0]), ALU.subtract).then_inc(q_sub, 1)
                dve.wait_ge(q_exp, b + 1)
                qlink_(dve.tensor_reduce(v_[0], R[1], AX.X, ALU.add))
                qlink_(dve.reciprocal(v_[1], v_[0]))
                qlink_(dve.tensor_tensor(R[0], R[1], oe(v_[1]), ALU.mult))
                hot, top = [R[2], R[3]], [v_[2], v_[3]]
                for k in range(K):
                    qlink_(dve.tensor_reduce(top[k], R[0], AX.X, ALU.max))
                    qlink_(dve.tensor_tensor(R[1], R[0], oe(top[k]), ALU.is_equal))
                    qlink_(dve.tensor_tensor(R[1], R[1], ot(rank_e[:]), ALU.mult))
                    qlink_(dve.tensor_reduce(v_[4 + k], R[1], AX.X, ALU.max))
                    qlink_(dve.tensor_tensor(hot[k], R[1], oe(v_[4 + k]), ALU.is_equal))
                    if k == 0:
                        qlink_(dve.scalar_tensor_tensor(R[0], hot[k], -2.0, R[0], ALU.mult, ALU.add))
                dve.tensor_tensor(R[4], hot[0], hot[1], ALU.add).then_inc(q_M, 1)
                qlink_(dve.tensor_tensor(v_[0], top[0], top[1], ALU.add))
                qlink_(dve.tensor_scalar(v_[1], v_[0], 1e-9, None, ALU.add))
                qlink_(dve.reciprocal(v_[0], v_[1]))
                qlink_(dve.tensor_tensor(v_[6], top[0], v_[0], ALU.mult))
                qlink_(dve.tensor_tensor(v_[7], top[1], v_[0], ALU.mult))

                dve.tensor_copy(col(blk(pay), 0), v_[7])
                dve.tensor_tensor(col(blk(pay), 1), v_[6], v_[7], ALU.subtract)
                dve.tensor_scalar(col(blk(pay), 2), v_[4], -1.0, float(E), ALU.mult, ALU.add)
                dve.tensor_scalar(col(blk(pay), 3), blk(tok_id), float(NT * P), None, ALU.add)
                dve.wait_ge(q_rank, b + 1)
                tot = ps[1][:, NTB * E:2 * NTB * E].rearrange("p (t e) -> p t e", e=E)
                qlink_(dve.tensor_copy(R[5], tot))
                for e in range(E):
                    dve.tensor_tensor_scan(col(R[6], e), ones[:, 0:NTB], col(R[5], e), 0.0, ALU.mult, ALU.add).then_inc(q_read, 1)
                dve.wait_ge(q_read, (b + 1) * E)
                qlink_(dve.tensor_tensor(R[5], R[6], R[5], ALU.subtract))
                last_t = R[6][:, NTB - 1:NTB].rearrange("p o e -> p (o e)")
                qlink_(dve.tensor_scalar(cnt[0], last_t, float(P - 1), None, ALU.add))
                qlink_(dve.tensor_copy(cnt_i, cnt[0]))
                qlink_(dve.tensor_scalar(cnt_i, cnt_i, P.bit_length() - 1, None, ALU.logical_shift_right))
                qlink_(dve.tensor_copy(cnt[1], cnt_i))
                qlink_(dve.tensor_tensor_scan(cnt[2], ones[:, 0:E], cnt[1], 0.0, ALU.mult, ALU.add))
                qlink_(dve.tensor_tensor(cnt[3], cnt[2], cnt[1], ALU.subtract))
                qlink_(dve.tensor_scalar(cnt[4], cnt[3], float(P), float(b * NGB * P), ALU.mult, ALU.add))
                qlink_(dve.tensor_tensor(R[5], R[5], ot(cnt[4]), ALU.add))
                qlink_(dve.tensor_tensor(R[5], ps[1][:, 0:NTB * E].rearrange("p (t e) -> p t e", e=E), R[5], ALU.add))
                for k in range(K):
                    qlink_(dve.tensor_tensor(R[6], R[5], hot[k], ALU.mult))
                    qlink_(dve.tensor_reduce(v_[k], R[6], AX.X, ALU.add))
                    qlink_(dve.tensor_copy(col(blk(slot), k), v_[k]))
                dve.memset(hold[:], 0.0).then_inc(q_done, 1)
                etab_b = etab[:, b * NGB:(b + 1) * NGB]
                qlink_(dve.tensor_tensor(etmp, oe(gidx[:], NGB), ot(cnt[2], NGB), ALU.is_ge))
                qlink_(dve.tensor_reduce(etab_b, etmp, AX.X, ALU.add))
                qlink_(dve.tensor_scalar(etab_b, etab_b, float(E - 1), None, ALU.min))
                steps = slice(b * NGB + N_H, (b + 1) * NGB + N_Y)
                if b == 0:
                    qlink_(dve.memset(etab_f[:], 0.0))
                qlink_(dve.tensor_scalar(etab_f[:, N_Y + b * NGB:N_Y + (b + 1) * NGB], etab_b[0:1], float(E), None, ALU.mult))
                now = etab_f[:, N_H + b * NGB:N_H + (b + 1) * NGB]
                qlink_(dve.tensor_tensor(now, now, etab_b[0:1], ALU.add))
                qlink_(dve.tensor_copy(etab_i[:, steps], etab_f[:, steps]))
                if b == 0:
                    qlink_(dve.memset(etab_i[:, 0:N_H], 0))
                else:
                    qlink_(dve.memset(etab_i[:, NG + N_Y:], 0))
                dve.memset(hold[:], 0.0).then_inc(q_etab, 1)

            def col(t, c):
                return t[:, :, c:c + 1].rearrange("p t c -> p (t c)")

            def gnn1(n, u):
                m = n - M_LGC
                if live(n, M_LGC, B):
                    dve.wait_ge(c_lgp, m + 1)
                    dve.tensor_scalar(lgt[:, bass.ds(m * T, T)], ps[7][:, 0:T * E].rearrange("p (t e) -> p t e", e=E), 1.0, None, ALU.mult).then_inc(c_lg, 1)
                m, k = n - M_O, n - M_X3
                new, mid, old = live(n, 0, B), live(n, M_O, B), live(n, M_X3, B)
                v, w = (u - M_O) % 4, (u - M_X3) % 4
                if new:
                    if isinstance(n, int) and n <= LAG3:
                        dve.wait_ge(x2_rdy, n + 1 if n < LAG3 else B)
                    for t in range(T):
                        dve.bn_stats(stc[:, u % 2, t], tile(X, n * T + t)).then_inc(c_st, 1)
                if mid:
                    dve.wait_ge(c_hom, m + 1)
                    dve.wait_ge(c_pr, m + 1)
                    for t in range(T):
                        last = dve.scalar_tensor_tensor(dd[:, v % 2, t], ps[6][:, t * D:(t + 1) * D], norm[:, bass.ds(m * T + t, 1)], het[:, v, t], ALU.mult, ALU.subtract)
                    last.then_inc(c_o, 1)
                if new:
                    held(c_st, n * 2 * T + T)
                    for t in range(T):
                        dve.bn_aggr(mvc[:, u, t], stc[:, u % 2, t]).then_inc(c_st, 1)
                if old:
                    dve.wait_ge(c_exp, k + 1)
                    dve.wait_ge(c_t2, k + 1)
                    dve.scalar_tensor_tensor(tokens(X, k), ee[:, w % 2], -1.0, tokens(X, k), ALU.add, ALU.add).then_inc(x3_rdy, 1)
                if mid:
                    dve.wait_ge(c_o, m * 3 + 1)
                    dve.scalar_tensor_tensor(dd[:, v % 2], th[:, v], 1.0, dd[:, v % 2], ALU.add, ALU.mult).then_inc(c_o, 1)
                if new:
                    reused(dve, c_z, n, 4)
                    dve.wait_ge(c_st, (n + 1) * 2 * T)
                    dve.tensor_scalar(nmc[:, u], mean_of(mvc[:, u]), -1.0, None, ALU.mult).then_inc(c_q, 1)
                    dve.tensor_scalar(qc[:, u, 0], var_of(mvc[:, u]), LN_EPS, None, ALU.add).then_inc(c_q, 1)
                if mid:
                    dve.wait_ge(c_o, m * 3 + 2)
                    dve.scalar_tensor_tensor(oo[:, v % 2], dd[:, v % 2], 0.5, het[:, v], ALU.mult, ALU.add).then_inc(c_o, 1)
                if old:
                    held(x3_rdy, k + 1)
                    for t in range(T):
                        dve.bn_stats(st1[:, w % 2, t], tile(X, k * T + t)).then_inc(c_st3, 1)
                if mid:
                    dve.wait_ge(c_o, m * 3 + 3)
                    reused(dve, c_exp, m, 2)
                    dve.tensor_scalar(mn[:, v % 2], oo[:, v % 2], 0.0, None, ALU.min).then_inc(c_mn, 1)
                if old:
                    held(c_st3, k * 2 * T + T)
                    for t in range(T):
                        dve.bn_aggr(mv1[:, w % 2, t], st1[:, w % 2, t]).then_inc(c_st3, 1)
                if mid:
                    dve.scalar_tensor_tensor(tokens(X, m), oo[:, v % 2], 0.0, tokens(X, m), ALU.max, ALU.add).then_inc(c_t2, 1)
                if old:
                    reused(dve, c_nb3, k, 2)
                    dve.wait_ge(c_st3, (k + 1) * 2 * T)
                    dve.tensor_scalar(nm1[:, w % 2], mean_of(mv1[:, w % 2]), -1.0, None, ALU.mult).then_inc(c_q3, 1)
                    dve.tensor_scalar(q1[:, w % 2], var_of(mv1[:, w % 2]), LN_EPS, None, ALU.add).then_inc(c_q3, 1)
            for k in range(LAG3):
                ffn0(B + k, k % UNROLL)
                if k == 1:
                    dve.wait_ge(f_y, B)
                    dve.wait_ge(f_xb, B)
                gnn1(k, k % UNROLL)
            pipeline(dve, ROUTE, 0, gnn1, peel=16, start=LAG3)
            dve.wait_ge(pad_out, 7)
            qlink_(dve.memset(hh[:, :, H:HC * P], 0.0))
            route(0)
            for n in range(ROUTE, B + LAG4):
                gnn1(n, n % UNROLL)
            route(1)

            def ffn1(n, u):
                m = n - N_MUL
                if live(n, N_MUL, NG):
                    v = (u - N_MUL) % 4
                    dve.wait_ge(e_silu, m + 1)
                    reused(dve, e_ht, m, 2)
                    dve.tensor_tensor(hh[:, v % 2, 0:H], ps[3 + v % 2][:, 0:H], sg[:, v % 2], ALU.mult).then_inc(e_hh, 1)
                m = n - N_XT
                if live(n, N_XT, NG):
                    v = (u - N_XT) % 4
                    dve.wait_ge(e_xt, m + 1)
                    reused(dve, e_h, m, 2)
                    dve.tensor_copy(xsT[:, v % 2], ps[0][:, 0:P]).then_inc(e_xT, 1)
                    dve.tensor_scalar(isk1[:, v], XS[:, v, D + 2:D + 3], etab[:, bass.ds(m, 1)], None, ALU.is_equal).then_inc(e_is, 1)
                m = n - N_XT
                if live(n, N_XT, NG):
                    v = (u - N_XT) % 4
                    dve.wait_ge(e_is, m + 1)
                    dve.scalar_tensor_tensor(gate[:, bass.ds(m, 1)], isk1[:, v], XS[:, v, D + 1:D + 2], XS[:, v, D:D + 1], ALU.mult, ALU.add).then_inc(e_gate, 1)
                    dve.scalar_tensor_tensor(dest[:, bass.ds(m, 1)], isk1[:, v], -float(NT * P), XS[:, v, D + 3:D + 4], ALU.mult, ALU.add).then_inc(e_gate, 1)
                m = n - N_Y
                if live(n, N_Y, NG):
                    v = (u - N_Y) % 4
                    if not isinstance(m, int) or m >= 4:
                        dve.wait_ge(e_sc[v], (m - v) * 4)
                    dve.wait_ge(e_gate, (m + 1) * 2)
                    dve.tensor_scalar(scatter_i[:, v:v + 1], dest[:, bass.ds(m, 1)], 1.0, None, ALU.mult).then_inc(e_dest, 1)

            pipeline(dve, GIVEN, 0, ffn1)

            def ffn1_and_sum(n, u):
                ffn1(n, u)
                if u == 3:
                    j = (n - 3 - GIVEN) // 4
                    dve.wait_ge(z_in, j * 32 + 32)
                    if not isinstance(n, int):
                        dve.wait_ge(z_out, j * 16)
                    dve.tensor_tensor(z_sum, z_y1, z_y2, ALU.add).then_inc(z_b, 1)
                    dve.wait_ge(z_b, j * 2 + 1)
                    dve.tensor_tensor(z_sum, z_sum, X[:, bass.ds(j * T, T), :].rearrange("p t c -> p (t c)"), ALU.add).then_inc(z_b, 1)
            for u in range(UNROLL):
                ffn1_and_sum(GIVEN + u, u)
            for_more(dve, GIVEN + 4, NG, ffn1_and_sum)
            for n in range(NG, NG + N_SC):
                ffn1(n, n % UNROLL)

            def last_sum(n, u):
                dve.wait_ge(o_in[u], (n - u) * 8 + 32)
                dve.tensor_tensor(ybb[:, u], ybb[:, u], ya[:, u], ALU.add).then_inc(o_b, 1)
                dve.wait_ge(o_b, n * 2 + 1)
                dve.tensor_tensor(ya[:, u], ybb[:, u], X[:, bass.ds(n * 4 + NTB, 4), :].rearrange("p t c -> p (t c)"), ALU.add).then_inc(o_b, 1)
            pipeline(dve, NTB // 4, 0, last_sum, peel=4)

        @block.tensor
        def _(pe):
            pe.wait_ge(s_id, 1)
            pe.wait_ge(s_row, 64)
            pe.transpose(ps_z[0][:, 0:NROW], rows[:], ident[0:NROW, 0:NROW]).then_inc(s_colp, 1)
            pe.wait_ge(s_col, 1)
            pe.wait_ge(s_wg, 48)

            def step(n, u):
                m = n - L_XPT
                if live(n, L_XPT, B):
                    v = (u - L_XPT) % 4
                    pe.wait_ge(xp_rdy, m + 1)
                    reused(pe, xp_sb, m, 1)
                    for t in range(T):
                        last = pe.transpose(ps_xp[:, t * P:(t + 1) * P], xp[:, v % 2, t], ident[:])
                    last.then_inc(xp_ps, 1)
                m = n - L_ZT
                if live(n, L_ZT, B):
                    v = (u - L_ZT) % 4
                    pe.wait_ge(z_rdy, m + 1)
                    reused(pe, hT_rdy, m, 2)
                    for t in range(T):
                        last = pe.transpose(ps_z[v % 2][:, t * P:(t + 1) * P], z[:, v % 2, t], ident[:])
                    last.then_inc(z_ps, 1)
                m = n - L_AT
                if live(n, L_AT, B):
                    v = (u - L_AT) % 4
                    pe.wait_ge(adj_in[v], (m - v) * 4 + 16)
                    reused(pe, at_sb, m, 2)
                    for i in range(T):
                        for j in range(T):
                            last = pe.transpose(ps_at[v % 2][:, j * S + i * P:j * S + (i + 1) * P], AJ[:, v, i, j * P:(j + 1) * P], ident[:])
                    last.then_inc(at_ps, 1)
                m = n - L_HREL
                if live(n, L_HREL, B):
                    v = (u - L_HREL) % 4
                    pe.wait_ge(hT_rdy, m + 1)
                    reused(pe, hr_rdy, m, 1)
                    for t in range(T):
                        last = pe.matmul(ps_hr[:, t * D:(t + 1) * D], hT[:, v, t * P:(t + 1) * P], Wg[:, 0], start=True, stop=True)
                    last.then_inc(hr_ps, 1)
                m = n - L_CONV
                if live(n, L_CONV, B):
                    v = (u - L_CONV) % 4
                    pe.wait_ge(at_sb, m + 1)
                    pe.wait_ge(hr_rdy, m + 1)
                    reused(pe, cv_read, m, 2)
                    for t in range(T):
                        acc = ps_cv[v % 2][:, t * S:t * S + D + 1]
                        for j in range(T):
                            pe.matmul(acc, AT[:, v, j, t * P:(t + 1) * P], hrel[:, v % 2, j], start=(j == 0), stop=False)
                        last = pe.matmul(ps_cv[v % 2][:, t * S:t * S + D], hT[:, v, t * P:(t + 1) * P], Wg[:, 1], start=False, stop=True)
                    last.then_inc(cv_ps, 1)
            pipeline(pe, B, LAG1, step)

            pe.wait_ge(r_g, 1)
            pe.matmul(ps[0][:, 0:B * E], one_S[:], rt[0].rearrange("p b e -> p (b e)"), start=True, stop=True).then_inc(r_lg, 1)

            pe.wait_ge(cv_read, B)
            pe.wait_ge(ws_in, 16 * 5 * E)
            for e in range(E):
                p1, p3, p2 = ps[2 + e % 2 * 3:5 + e % 2 * 3]
                if e >= 2:
                    pe.wait_ge(wp_sb, e - 1)
                for i, pi in enumerate((p1, p3)):
                    for c in range(HC):
                        h = P if c < HC - 1 else HL
                        pe.transpose(pi[:, c * P:c * P + h], w13_raw[e][0:h, (i * HC + c) * P:(i * HC + c + 1) * P], ident[0:h, 0:h])
                for c in range(HC):
                    h = P if c < HC - 1 else HL
                    last = pe.transpose(p2[0:h, c * D:(c + 1) * D], w2_raw[e][:, c * P:c * P + h], ident[:])
                last.then_inc(wp_ps, 1)
            pe.wait_ge(r_wd8, 1)
            pe.matmul(ps[1][0:B, 0:D], wd8[:], b2_sb[:], start=True, stop=True).then_inc(r_b2, 1)
            pe.wait_ge(r_b2w, 1)
            pe.wait_ge(cv_read, B)

            def ffn0(n, u):
                if live(n, 0, B):
                    pe.wait_ge(w_in[u], (n - u) * 16 + 64)
                    reused(pe, f_g, n, 2, per=K * FC)
                    for k in range(K):
                        for c in range(FC):
                            last = pe.matmul(ps[(u % 2) * K + k][:, c * S:(c + 1) * S], W1b[:, u, k, c * P:(c + 1) * P], X0T[:, bass.ds(n * S, S)], start=True, stop=True)
                        last.then_inc(f_h, 1)
                m = n - L_Y
                if live(n, L_Y, B):
                    v = (u - L_Y) % 4
                    pe.wait_ge(f_g, (m + 1) * K * FC)
                    reused(pe, f_sum, m, 2, per=2)
                    for k in range(K):
                        for t in range(T):
                            at = (k * T + t) * D
                            for c in range(FC):
                                last = pe.matmul(ps[4 + v % 2][:, at:at + D], gT[:, v % 2, k, c, t * P:(t + 1) * P], W2b[:, v, k, c], start=(c == 0), stop=(c == FC - 1))
                    last.then_inc(f_y, 1)
            pipeline(pe, B, 0, ffn0)

            def ranks(b):
                chosen = R_all[4][:, b * NTB:(b + 1) * NTB].rearrange("p t e -> p (t e)")
                pe.wait_ge(q_M, b + 1)
                if b > 0:
                    pe.wait_ge(q_done, b)
                pe.matmul(ps[1][:, 0:NTB * E], tri[:], chosen, start=True, stop=True)
                pe.matmul(ps[1][:, NTB * E:2 * NTB * E], ones[:], chosen, start=True, stop=True).then_inc(q_rank, 1)

            def gnn1(n, u):
                first, second = live(n, M_ZT, B), live(n, M_Z3T, B)
                if first or second:
                    if not isinstance(n, int) or n > M_ZT:
                        pe.wait_ge(c_xT, n - M_ZT)
                    if first:
                        pe.wait_ge(c_z, n - M_ZT + 1)
                        for t in range(T):
                            last = pe.transpose(ps[0][:, t * P:(t + 1) * P], z[:, u % 2, t], ident[:])
                    if second:
                        pe.wait_ge(c_z3, n - M_Z3T + 1)
                        for t in range(T):
                            last = pe.transpose(ps[0][:, S + t * P:S + (t + 1) * P], x0[:, (u - M_Z3T) % 2, t], ident[:])
                    last.then_inc(c_zt, 1)
                m = n - M_HOM
                if live(n, M_HOM, B):
                    v = (u - M_HOM) % 4
                    pe.wait_ge(at_in[v], (m - v) * 4 + 16)
                    pe.wait_ge(c_f1, m + 1)
                    reused(pe, c_o, m, 1, per=3)
                    for t in range(T):
                        for j in range(T):
                            last = pe.matmul(ps[6][:, t * D:(t + 1) * D], AT[:, v, j, t * P:(t + 1) * P], hrel[:, v % 2, j, 0:D], start=(j == 0), stop=(j == T - 1))
                    last.then_inc(c_hom, 1)
                m = n - M_LG
                if live(n, M_LG, B):
                    v = (u - M_LG) % 4
                    pe.wait_ge(c_xT, m + M_Z3T - M_ZT + 1)
                    reused(pe, c_lg, m, 1)
                    for t in range(T):
                        last = pe.matmul(ps[7][:, t * E:(t + 1) * E], turned[:, (u - 1) % 2, S + t * P:S + (t + 1) * P], cols[:, 18:26], start=True, stop=True)
                    last.then_inc(c_lgp, 1)
                m = n - M_P
                if live(n, M_P, B):
                    v = (u - M_P) % 4
                    pp = PS[:, 2 + 2 * (v % 2):4 + 2 * (v % 2)]
                    pe.wait_ge(c_xT, m + 1)
                    reused(pe, c_pr, m, 2)
                    for t in range(T):
                        pe.matmul(pp[:, t, 0:3 * D], turned[:, (u - 1) % 2, t * P:(t + 1) * P], Wc[:].rearrange("p a c -> p (a c)"), start=True, stop=False)
                        last = pe.matmul(pp[:, t, 2 * D:3 * D], ones[0:1, :], bt_row[:], start=False, stop=True)
                    last.then_inc(c_p, 1)
            for k in range(LAG3):
                ffn0(B + k, k % UNROLL)
                if k == M_P:
                    pe.wait_ge(s_wc, 64)
                    pe.wait_ge(f_sum, B * 2)
                gnn1(k, k % UNROLL)
            pipeline(pe, ROUTE, 0, gnn1, peel=16, start=LAG3)
            ranks(0)
            for n in range(ROUTE, B + LAG4):
                gnn1(n, n % UNROLL)
            ranks(1)

            pe.wait_ge(q_etab, BLOCKS)
            pe.wait_ge(wp_sb, E)
            pe.wait_ge(wp_sb, E)

            def ffn1(n, u):
                both = pe.value_load(etab_i[0:1, bass.ds(n, 1)], min_val=0, max_val=E * E - 1)
                e_of_h, e_of_y = both % E, both // E
                m = n - N_Y
                if live(n, N_Y, NG):
                    v = (u - N_Y) % 4
                    pe.wait_ge(e_hT, m + 1)
                    reused(pe, e_ys, m, 2)
                    for c in range(HC):
                        h = P if c < HC - 1 else HL
                        last = pe.matmul(ps[6 + v % 2][:, 0:D], hhT[0:h, v % 2, c], w2T[0:h, bass.ds(e_of_y, 1), c].rearrange("p o d -> p (o d)"), start=(c == 0), stop=(c == HC - 1))
                    last.then_inc(e_y, 1)
                m = n - N_XT
                if live(n, N_XT, NG):
                    v = (u - N_XT) % 4
                    pe.wait_ge(e_in[v], (m - v) * 4 + 16)
                    reused(pe, e_xT, m, 1)
                    pe.transpose(ps[0][:, 0:P], XS[:, v, 0:D], ident[:]).then_inc(e_xt, 1)
                m = n - N_HT
                if live(n, N_HT, NG):
                    v = (u - N_HT) % 4
                    pe.wait_ge(e_hh, m + 1)
                    reused(pe, e_hT, m, 1)
                    for c in range(HC):
                        last = pe.transpose(ps[5][:, c * P:(c + 1) * P], hh[:, v % 2, c * P:(c + 1) * P], ident[:])
                    last.then_inc(e_ht, 1)
                m = n - N_H
                if live(n, N_H, NG):
                    v = (u - N_H) % 4
                    pe.wait_ge(e_xT, m + 1)
                    reused(pe, e_silu, m, 2)
                    reused(pe, e_hh, m, 2)
                    pe.matmul(ps[1 + v % 2][:, 0:H], xsT[:, v % 2], w1T[:, bass.ds(e_of_h, 1)].rearrange("p o h -> p (o h)"), start=True, stop=True)
                    pe.matmul(ps[3 + v % 2][:, 0:H], xsT[:, v % 2], w3T[:, bass.ds(e_of_h, 1)].rearrange("p o h -> p (o h)"), start=True, stop=True).then_inc(e_h, 1)
            pipeline(pe, NG, N_SC, ffn1)


_INS = ['x', 'adj', 'L0_gnn_W_rel', 'L0_gnn_b_rel', 'L0_gnn_W_root', 'L0_gnn_ln_gamma', 'L0_gnn_ln_beta', 'L0_ffn_Wr',
        'L0_ffn_br', 'L0_ffn_W1', 'L0_ffn_b1', 'L0_ffn_W2', 'L0_ffn_b2', 'L0_ffn_gamma', 'L0_ffn_beta', 'L1_gnn_W_t',
        'L1_gnn_b_t', 'L1_gnn_W_h', 'L1_gnn_theta', 'L1_ffn_router_w', 'L1_ffn_w1', 'L1_ffn_w2', 'L1_ffn_w3']


def kernel(**inputs):
    import numpy as _np
    import concourse.bacc as _bacc
    from concourse import mybir as _mybir
    from concourse.bass_utils import run_bass_kernel_spmd as _run

    nc = _bacc.Bacc("TRN2", target_bir_lowering=False, num_devices=1)
    arrays, args = {}, []
    for name in _INS:
        a = _np.ascontiguousarray(inputs[name])
        arrays[f"in_{name}"] = a
        args.append(nc.dram_tensor(f"in_{name}", a.shape, _mybir.dt.from_np(a.dtype), kind="ExternalInput").ap())
    args.append(nc.dram_tensor("out", inputs['x'].shape, _mybir.dt.float32, kind="ExternalOutput").ap())
    build(nc, *args)
    r = _run(nc, [arrays], core_ids=[0])
    return r.results[0]["out"]
```
